# Optimizing a Trainium2 kernel written in Bass

```python
import numpy as np
import jax
import jax.numpy as jnp

def _softmax(x, axis=-1):
    return jax.nn.softmax(x, axis=axis)

def _gelu(x):
    return jax.nn.gelu(x, approximate=True)

def _silu(x):
    return jax.nn.silu(x)

def _sigmoid(x):
    return jax.nn.sigmoid(x)

def _layernorm(x, axis=-1, eps=1e-05):
    m = jnp.mean(x, axis=axis, keepdims=True)
    v = jnp.var(x, axis=axis, keepdims=True)
    return (x - m) / jnp.sqrt(v + eps)

def _scatter_add(tgt, idx, src, axis=0):
    return tgt.at[idx].add(src)

def _segment_sum(src, seg, n):
    return jax.ops.segment_sum(src, seg, n)
kernel_name = 'mk_flamingo_gated_d2_seqx_r4_8c1189'

def setup_inputs(seed: int=0):
    np.random.seed(seed)
    _w = jnp.asarray

    def _rec_inputs():
        import jax
        import jax.numpy as jnp
        _rk = jax.random.key(seed)
        x = -0.000125 + 0.9999 * jax.random.normal(jax.random.fold_in(_rk, 1), (16, 128, 256), jnp.float32)
        _lenS = 128 - jax.random.randint(jax.random.fold_in(_rk, 7), (16,), 0, max(1, 128 // 4) + 1, jnp.int32)
        _lenS2 = 128 - jax.random.randint(jax.random.fold_in(_rk, 8), (16,), 0, max(1, 128 // 4) + 1, jnp.int32)
        _ctx_1024P = jax.random.normal(jax.random.fold_in(_rk, 11), (16, 16, 256), jnp.float32)
        _ctx_1024c = jax.random.dirichlet(jax.random.fold_in(_rk, 511), 0.3 * jnp.ones((16,), jnp.float32), (16, 128))
        _ctx_1024t = jnp.einsum('bsk,bkd->bsd', _ctx_1024c, _ctx_1024P)
        _ctx_1024t = _ctx_1024t * jax.lax.rsqrt(jnp.mean(jnp.square(_ctx_1024t)) + 1e-12) * 0.953939
        ctx_1024 = -1.52775e-05 + 0.999936 * (_ctx_1024t + 0.3 * jax.random.normal(jax.random.fold_in(_rk, 611), (16, 128, 256), jnp.float32))
        _g = jax.random.normal(jax.random.fold_in(_rk, 9001), (2, 2), jnp.float32)
        _g = jnp.sign(_g) * jnp.maximum(jnp.abs(_g), 1.0) + (_g == 0) * 1.0
        g_xattn = _g[0]
        g_ffn = _g[1]
        return (x, ctx_1024, g_xattn, g_ffn)
    x, ctx_1024, g_xattn, g_ffn = _rec_inputs()

    def _L0_xattn_setup():
        import jax, jax.numpy as jnp
        import numpy as np
        B, LP, LQ, H = (16, 512, 512, 256)
        key = jax.random.key(seed)
        k1, k2, k3 = jax.random.split(key, 3)
        proj_p = jax.random.normal(k1, (B, LP, H), dtype=jnp.float32)
        proj_q = jax.random.normal(k2, (B, LQ, H), dtype=jnp.float32)
        W = jax.random.normal(k3, (H, H), dtype=jnp.float32) * (1.0 / np.sqrt(H))
        b = jnp.zeros((H,), dtype=jnp.float32)
        return {'proj_p': proj_p, 'proj_q': proj_q, 'W': W, 'b': b}
    _L0_xattn_all = _L0_xattn_setup()
    _L0_xattn_in = {k: v for k, v in _L0_xattn_all.items() if k in ('W', 'b')}
    del _L0_xattn_all

    def _L0_ffn_setup():
        import jax, jax.numpy as jnp
        import numpy as np
        B, T, H = (2, 512, 256)
        I = 1024
        HEADS = 4
        RET = 128
        NUM_EXPERTS = 1024
        NUM_KEYS = 64
        K = 8
        key = jax.random.key(seed)
        ks = jax.random.split(key, 7)
        return {'hidden_states': jax.random.normal(ks[0], (B, T, H), jnp.float32), 'W_up': jax.random.normal(ks[1], (I, H), jnp.float32) * 0.02, 'W_down': jax.random.normal(ks[2], (H, I), jnp.float32) * 0.02, 'W_q': jax.random.normal(ks[3], (HEADS * RET, H), jnp.float32) * 0.02, 'keys': jax.random.normal(ks[4], (HEADS, NUM_KEYS, 2, RET // 2), jnp.float32) * 0.02, 'down_embed': jax.random.normal(ks[5], (NUM_EXPERTS, H), jnp.float32) * 0.02, 'up_embed': jax.random.normal(ks[6], (NUM_EXPERTS, H), jnp.float32) * 0.02}
    _L0_ffn_all = _L0_ffn_setup()
    _L0_ffn_in = {k: v for k, v in _L0_ffn_all.items() if k in ('W_up', 'W_down', 'W_q', 'keys', 'down_embed', 'up_embed')}
    del _L0_ffn_all

    def _L1_xattn_setup():
        import jax, jax.numpy as jnp
        import numpy as np
        DIM = 256
        EPS_DENOM = 1e-06
        EPS_LN = 1e-05

        def _layernorm(x, gamma, beta):
            mu = jnp.mean(x, axis=-1, keepdims=True)
            var = jnp.var(x, axis=-1, keepdims=True)
            return (x - mu) * jax.lax.rsqrt(var + EPS_LN) * gamma + beta
        key = jax.random.key(seed)
        ks = jax.random.split(key, 12)
        B, T, D = (8, 1024, DIM)
        s = 1.0 / np.sqrt(D)
        return {'audio': jax.random.normal(ks[0], (B, T, D), jnp.float32), 'video': jax.random.normal(ks[1], (B, T, D), jnp.float32), 'Wq': jax.random.normal(ks[2], (D, D), jnp.float32) * s, 'bq': jax.random.normal(ks[3], (D,), jnp.float32) * 0.02, 'Wk': jax.random.normal(ks[4], (D, D), jnp.float32) * s, 'bk': jax.random.normal(ks[5], (D,), jnp.float32) * 0.02, 'Wv': jax.random.normal(ks[6], (D, D), jnp.float32) * s, 'bv': jax.random.normal(ks[7], (D,), jnp.float32) * 0.02, 'Wo': jax.random.normal(ks[8], (D, D), jnp.float32) * s, 'bo': jax.random.normal(ks[9], (D,), jnp.float32) * 0.02, 'gamma': jnp.ones((D,), jnp.float32), 'beta': jnp.zeros((D,), jnp.float32)}
    _L1_xattn_all = _L1_xattn_setup()
    _L1_xattn_in = {k: v for k, v in _L1_xattn_all.items() if k in ('Wq', 'bq', 'Wk', 'bk', 'Wv', 'bv', 'Wo', 'bo', 'gamma', 'beta')}
    del _L1_xattn_all

    def _L1_ffn_setup():
        import jax, jax.numpy as jnp
        import numpy as np
        D_MODEL = 256
        MLP_DIM = 1024
        N_EXPERTS = 8
        B, T = (4, 256)
        key = jax.random.key(seed)
        ks = jax.random.split(key, 7)
        scale_in = (1.0 / D_MODEL) ** 0.5
        scale_out = (1.0 / MLP_DIM) ** 0.5
        bound_g = (1.0 / D_MODEL) ** 0.5
        w_gate = jax.random.uniform(ks[0], (D_MODEL, N_EXPERTS), minval=-bound_g, maxval=bound_g, dtype=jnp.float32)
        b_gate = jax.random.uniform(ks[1], (N_EXPERTS,), minval=-bound_g, maxval=bound_g, dtype=jnp.float32)
        W1 = jax.random.uniform(ks[2], (N_EXPERTS, D_MODEL, MLP_DIM), minval=-scale_in, maxval=scale_in, dtype=jnp.float32)
        b1 = jnp.zeros((N_EXPERTS, MLP_DIM), dtype=jnp.float32)
        W2 = jax.random.uniform(ks[3], (N_EXPERTS, MLP_DIM, D_MODEL), minval=-scale_out, maxval=scale_out, dtype=jnp.float32)
        b2 = jnp.zeros((N_EXPERTS, D_MODEL), dtype=jnp.float32)
        x = jax.random.normal(ks[4], (B, T, D_MODEL), dtype=jnp.float32)
        return {'x': x, 'w_gate': w_gate, 'b_gate': b_gate, 'W1': W1, 'b1': b1, 'W2': W2, 'b2': b2}
    _L1_ffn_all = _L1_ffn_setup()
    _L1_ffn_in = {k: v for k, v in _L1_ffn_all.items() if k in ('w_gate', 'b_gate', 'W1', 'b1', 'W2', 'b2')}
    del _L1_ffn_all
    return {'x': x, 'ctx_1024': ctx_1024, 'g_xattn': g_xattn, 'g_ffn': g_ffn, 'L0_xattn_W': _L0_xattn_in['W'], 'L0_xattn_b': _L0_xattn_in['b'], 'L0_ffn_W_up': _L0_ffn_in['W_up'], 'L0_ffn_W_down': _L0_ffn_in['W_down'], 'L0_ffn_W_q': _L0_ffn_in['W_q'], 'L0_ffn_keys': _L0_ffn_in['keys'], 'L0_ffn_down_embed': _L0_ffn_in['down_embed'], 'L0_ffn_up_embed': _L0_ffn_in['up_embed'], 'L1_xattn_Wq': _L1_xattn_in['Wq'], 'L1_xattn_bq': _L1_xattn_in['bq'], 'L1_xattn_Wk': _L1_xattn_in['Wk'], 'L1_xattn_bk': _L1_xattn_in['bk'], 'L1_xattn_Wv': _L1_xattn_in['Wv'], 'L1_xattn_bv': _L1_xattn_in['bv'], 'L1_xattn_Wo': _L1_xattn_in['Wo'], 'L1_xattn_bo': _L1_xattn_in['bo'], 'L1_xattn_gamma': _L1_xattn_in['gamma'], 'L1_xattn_beta': _L1_xattn_in['beta'], 'L1_ffn_w_gate': _L1_ffn_in['w_gate'], 'L1_ffn_b_gate': _L1_ffn_in['b_gate'], 'L1_ffn_W1': _L1_ffn_in['W1'], 'L1_ffn_b1': _L1_ffn_in['b1'], 'L1_ffn_W2': _L1_ffn_in['W2'], 'L1_ffn_b2': _L1_ffn_in['b2']}

def reference(x, ctx_1024, g_xattn, g_ffn, L0_xattn_W, L0_xattn_b, L0_ffn_W_up, L0_ffn_W_down, L0_ffn_W_q, L0_ffn_keys, L0_ffn_down_embed, L0_ffn_up_embed, L1_xattn_Wq, L1_xattn_bq, L1_xattn_Wk, L1_xattn_bk, L1_xattn_Wv, L1_xattn_bv, L1_xattn_Wo, L1_xattn_bo, L1_xattn_gamma, L1_xattn_beta, L1_ffn_w_gate, L1_ffn_b_gate, L1_ffn_W1, L1_ffn_b1, L1_ffn_W2, L1_ffn_b2):
    import jax
    import jax.numpy as jnp

    def _L0_xattn_ref(proj_p, proj_q, W, b):
        import jax, jax.numpy as jnp
        import numpy as np
        B, LP, LQ, H = (16, 512, 512, 256)
        trans_q = jnp.einsum('bqh,oh->bqo', proj_q, W) + b
        att_weights = jnp.einsum('bph,bqh->bpq', proj_p, trans_q)
        att_norm = jax.nn.softmax(att_weights, axis=-1)
        att_vec = jnp.einsum('bpq,bqh->bph', att_norm, proj_q)
        out = jax.nn.relu(jnp.einsum('bph,oh->bpo', att_vec, W) + b)
        return out

    def _L0_ffn_ref(hidden_states, W_up, W_down, W_q, keys, down_embed, up_embed):
        import jax, jax.numpy as jnp
        import numpy as np
        B, T, H = (2, 512, 256)
        I = 1024
        HEADS = 4
        RET = 128
        NUM_EXPERTS = 1024
        NUM_KEYS = 64
        K = 8
        b, t, hd = hidden_states.shape
        h, nk, _, n = keys.shape
        q = jnp.einsum('btd,ed->bte', hidden_states, W_q)
        q = q.reshape(b, t, 2, h, n).transpose(2, 0, 1, 3, 4)
        sim = jnp.einsum('pbthn,hkpn->pbthk', q, keys)
        scores_xy, idx_xy = jax.lax.top_k(sim, K)
        sx, sy = (scores_xy[0], scores_xy[1])
        ix, iy = (idx_xy[0], idx_xy[1])
        all_scores = (sx[..., :, None] + sy[..., None, :]).reshape(b, t, h, K * K)
        all_idx = (ix[..., :, None] * nk + iy[..., None, :]).reshape(b, t, h, K * K)
        scores, pk = jax.lax.top_k(all_scores, K)
        indices = jnp.take_along_axis(all_idx, pk, axis=-1)
        de = down_embed[indices]
        ue = up_embed[indices]
        w = jax.nn.silu(jnp.einsum('btd,bthkd->bthk', hidden_states, de) * jax.nn.softmax(scores, axis=-1))
        experts_states = jnp.einsum('bthk,bthkd->btd', w, ue)
        dense = jnp.einsum('bti,di->btd', jax.nn.silu(jnp.einsum('btd,id->bti', hidden_states, W_up)), W_down)
        return dense + experts_states

    def _L1_xattn_ref(audio, video, Wq, bq, Wk, bk, Wv, bv, Wo, bo, gamma, beta):
        import jax, jax.numpy as jnp
        import numpy as np
        DIM = 256
        EPS_DENOM = 1e-06
        EPS_LN = 1e-05

        def _layernorm(x, gamma, beta):
            mu = jnp.mean(x, axis=-1, keepdims=True)
            var = jnp.var(x, axis=-1, keepdims=True)
            return (x - mu) * jax.lax.rsqrt(var + EPS_LN) * gamma + beta
        Q = audio @ Wq.T + bq
        K = video @ Wk.T + bk
        V = video @ Wv.T + bv
        Q = jax.nn.elu(Q) + 1.0
        K = jax.nn.elu(K) + 1.0
        KV = jnp.einsum('btd,bte->bde', K, V)
        K_sum = K.sum(axis=1)
        attn_num = jnp.einsum('btd,bde->bte', Q, KV)
        attn_denom = Q * K_sum[:, None, :] + EPS_DENOM
        attn_out = attn_num / attn_denom
        attn_out = attn_out @ Wo.T + bo
        return _layernorm(audio + attn_out, gamma, beta)

    def _L1_ffn_ref(x, w_gate, b_gate, W1, b1, W2, b2):
        import jax, jax.numpy as jnp
        import numpy as np
        D_MODEL = 256
        MLP_DIM = 1024
        N_EXPERTS = 8
        B, T = (4, 256)
        b, t, d = x.shape
        x_flat = x.reshape(b * t, d)
        logits = x_flat @ w_gate + b_gate
        probs = jax.nn.softmax(logits, axis=-1)
        route_p = jnp.max(probs, axis=-1)
        route_idx = jnp.argmax(probs, axis=-1)
        h = jnp.einsum('nd,edm->enm', x_flat, W1) + b1[:, None, :]
        h = jax.nn.relu(h)
        y = jnp.einsum('enm,emd->end', h, W2) + b2[:, None, :]
        n = b * t
        out = y[route_idx, jnp.arange(n)] * route_p[:, None]
        return out.reshape(b, t, d)
    x = x + jnp.tanh(g_xattn[0]) * _L0_xattn_ref(_layernorm(x, axis=-1), ctx_1024, L0_xattn_W, L0_xattn_b)
    x = x + jnp.tanh(g_ffn[0]) * _L0_ffn_ref(_layernorm(x, axis=-1), L0_ffn_W_up, L0_ffn_W_down, L0_ffn_W_q, L0_ffn_keys, L0_ffn_down_embed, L0_ffn_up_embed)
    x = x + jnp.tanh(g_xattn[1]) * _L1_xattn_ref(_layernorm(x, axis=-1), ctx_1024, L1_xattn_Wq, L1_xattn_bq, L1_xattn_Wk, L1_xattn_bk, L1_xattn_Wv, L1_xattn_bv, L1_xattn_Wo, L1_xattn_bo, L1_xattn_gamma, L1_xattn_beta)
    x = x + jnp.tanh(g_ffn[1]) * _L1_ffn_ref(_layernorm(x, axis=-1), L1_ffn_w_gate, L1_ffn_b_gate, L1_ffn_W1, L1_ffn_b1, L1_ffn_W2, L1_ffn_b2)
    return x

_drawn_inputs = setup_inputs


def setup_inputs(seed=0):
    import zlib

    import numpy as np

    out = dict(_drawn_inputs(seed))
    spreads = {'g_ffn': (-1.0, 0.6),
     'L0_xattn_b': (0.0, 0.1),
     'L1_xattn_gamma': (1.0, 0.2),
     'L1_xattn_beta': (0.0, 0.1),
     'L1_ffn_b1': (0.0, 0.8),
     'L1_ffn_b2': (0.0, 0.579)}
    factors = {'L0_ffn_W_q': 8.0,
     'L0_ffn_keys': 8.0,
     'L0_ffn_down_embed': 7.885,
     'L0_ffn_up_embed': 8.0,
     'L1_xattn_bq': 5.089,
     'L1_xattn_bk': 5.594,
     'L1_xattn_bo': 8.0,
     'L1_ffn_b_gate': 8.0}
    for name, (base, spread) in spreads.items():
        noise = np.random.default_rng([zlib.crc32(name.encode()), seed]).standard_normal(out[name].shape)
        drawn = base * np.exp(spread * noise) if base else spread * noise
        out[name] = jnp.asarray(drawn.astype(out[name].dtype))
    for name, factor in factors.items():
        out[name] = (out[name] * factor).astype(out[name].dtype)
    return out
```

```python
from contextlib import ExitStack

import concourse.bass as bass
from concourse import mybir

F32 = mybir.dt.float32
I32 = mybir.dt.int32
ALU = mybir.AluOpType
ACT = mybir.ActivationFunctionType
AX = mybir.AxisListType

SCRATCH = 8704
P = 128
BANK = 512
EPS_LN = 1e-5
EPS_DENOM = 1e-6
FAR = 4096.0


def pipeline(eng, tiles, depth, step, peel=0):
    first = max(depth + depth % 2, peel)
    for t in range(first):
        step(t, t % 2, [k for k in range(depth) if k <= t])
    loops = (tiles - first) // 2
    with eng.Fori(0, loops) as i:
        for u in range(2):
            step(2 * i + (first + u), (first + u) % 2, list(range(depth)))
    for t in range(first + 2 * loops, tiles + depth - 1):
        step(t, t % 2, [k for k in range(depth) if t - k < tiles])


def wait(eng, sem, value):
    if isinstance(value, int) and value <= 0:
        return
    eng.wait_ge(sem, value)


def build(nc, x, ctxT, rows, cols, w0, wup, wdn, wq, keys, demb, uemb, wkv, wqc, woc,
          wgate, w1, w2, b1, b2, out):
    T, _, D = x.shape
    KC = D // P
    IC = wdn.shape[1]
    HID = IC * P
    HEADS, NK, TOP = 4, 64, 8
    NX = HID // NK
    PAIRS = TOP * TOP
    GRID = HID + PAIRS
    E = w1.shape[1]

    SLOTS = T + E - 1

    with ExitStack() as ctx:
        sorted_rows = nc.dram_tensor("sorted_rows", (SLOTS * P, D + 2), F32, kind="Internal").ap()

        def sb(name, shape, dt=F32):
            return ctx.enter_context(nc.sbuf_tensor(name, shape, dt))

        def sem(name):
            return ctx.enter_context(nc.semaphore(name))

        banks = [ctx.enter_context(nc.psum_tensor(f"bank{i}", [P, BANK], F32)) for i in (0, 1)]
        table_dots = ctx.enter_context(nc.psum_tensor("table_dots", [P, HID], F32))
        banks += [None, None]
        banks += [ctx.enter_context(nc.psum_tensor(f"bank{i}", [P, BANK], F32)) for i in (4, 5, 6, 7)]
        banks[2] = table_dots[:, 0:BANK]
        banks[3] = table_dots[:, BANK:HID]

        ROW = D + 2
        xs = sb("xs", [P, T, ROW])
        ctxb = sb("ctxb", [P, 2, KC, P])
        NR = rows.shape[1]
        rowb = sb("rowb", [P, NR])
        colb = sb("colb", [P, KC])
        gate = sb("gate", [P, 4])
        ident = sb("ident", [P, P])
        ones = sb("ones", [P, P])
        neg_half = sb("neg_half", [P, 1])
        wkvs = sb("wkvs", [P, KC, 2 * D])
        wqcs = sb("wqcs", [P, KC, D])
        wocs = sb("wocs", [P, KC, D])

        region1 = sb("region1", [P, E * KC * HID])
        region2 = sb("region2", [P, max(E * IC * D, 4 * HEADS * GRID)])

        region3 = sb("region3", [P, SCRATCH])

        def carve(region, at, *shape):
            n = 1
            for s in shape:
                n *= s
            names = " ".join("abcd"[:len(shape)])
            v = region[:, at:at + n]
            if len(shape) > 1:
                v = v.rearrange(f"p ({names}) -> p {names}", **dict(zip("abcd", shape)))
            return v, at + n

        at = 0
        wups, at = carve(region1, at, KC, HID)
        wdns, at = carve(region1, at, IC, D)
        dembs, at = carve(region1, at, KC, HID)
        uembs, at = carve(region1, at, IC, D)
        wqs, at = carve(region1, at, 4, D)
        keyb, at = carve(region1, at, 4, P)
        simw, at = carve(region1, at, KC, BANK)
        at2 = 0
        grid, at2 = carve(region2, at2, 2, HEADS, GRID)
        picked, at2 = carve(region2, at2, 2, HEADS, GRID)

        stats = sb("stats", [P, 2, 6])
        mv = sb("mv", [P, 2, 2])
        ve = sb("ve", [P, 2])
        rstd = sb("rstd", [P, 2])
        xn = sb("xn", [P, 2, D])
        xT = sb("xT", [P, 2, KC, P])

        at3 = 0
        w0s, at3 = carve(region3, at3, KC, D)
        tqs, at3 = carve(region3, at3, 2, KC, P)
        vws, at3 = carve(region3, at3, 2, D)
        prob, at3 = carve(region3, at3, 2, P)
        probT, at3 = carve(region3, at3, 2, P)
        u_buf, at3 = carve(region3, at3, 2, D)
        r_buf, at3 = carve(region3, at3, 2, D)
        nmax = sb("nmax", [P, 2])
        esum = sb("esum", [P, 2])
        rsum = sb("rsum", [P, 2])
        scoresA = banks[3:5]
        outA = banks[6:8]

        simS, at = carve(region1, at, 2, BANK)
        hT, at = carve(region1, at, 2, HID)
        pickT, at = carve(region1, at, HID)
        top_x, at = carve(region1, at, 2, HEADS, TOP)
        top_y, at = carve(region1, at, 2, HEADS, TOP)
        top_c, at = carve(region1, at, 2, HEADS, TOP)
        cand, _ = carve(region3, SCRATCH - 2 * HEADS * PAIRS, 2, HEADS, PAIRS)
        top, at = carve(region1, at, 2, HEADS, TOP)
        nm = sb("nm", [P, 2, HEADS])
        d8, at = carve(region1, at, 2, HEADS * TOP)
        e8, at = carve(region1, at, 2, HEADS * TOP)
        zsum = sb("zsum", [P, 2, HEADS])
        rz = sb("rz", [P, 2, HEADS])
        tail = sb("tail", [P, 2])
        far, at = carve(region1, at, ROW)
        assert at <= E * KC * HID

        at3 = 0
        kvb, at3 = carve(region3, at3, 2, 2 * D)
        kvs, at3 = carve(region3, at3, 2, KC, D)
        q1T, at3 = carve(region3, at3, 2, KC, P)
        aoTs, at3 = carve(region3, at3, 2, KC, P)
        audio, at3 = carve(region3, at3, 2, D)
        qb, at3 = carve(region3, at3, 2, D)
        kexp, at3 = carve(region3, at3, 2, D)
        krel, at3 = carve(region3, at3, 2, D)
        qexp, at3 = carve(region3, at3, 2, D)
        qrel, at3 = carve(region3, at3, 2, D)
        k1, at3 = carve(region3, at3, 2, D)
        q1, at3 = carve(region3, at3, 2, D)
        den, at3 = carve(region3, at3, 2, D)
        ao, at3 = carve(region3, at3, 2, D)
        res, at3 = carve(region3, at3, 2, D)
        assert at3 <= SCRATCH
        at3 = 0
        w1s = region1[:, :].rearrange("p (e k m) -> p e k m", e=E, k=KC)
        w2s = region2[:, 0:E * IC * D].rearrange("p (e m d) -> p e m d", e=E, m=IC)
        logits, at3 = carve(region3, at3, T, E)
        shifted, at3 = carve(region3, at3, T, E)
        onehot, at3 = carve(region3, at3, E, T)
        before, at3 = carve(region3, at3, E, T)
        places, at3 = carve(region3, at3, E, T)
        ranked, at3 = carve(region3, at3, T, E)
        fits, at3 = carve(region3, at3, E, T)
        slot_cmp, at3 = carve(region3, at3, SLOTS, E)
        top_logit, at3 = carve(region3, at3, T)
        exp_sum, at3 = carve(region3, at3, T)
        first_best, at3 = carve(region3, at3, T)
        place_f, at3 = carve(region3, at3, T)
        onehot_sum, at3 = carve(region3, at3, E)
        counts, at3 = carve(region3, at3, E)
        slots_of, at3 = carve(region3, at3, E)
        slot_end, at3 = carve(region3, at3, E)
        row_base, at3 = carve(region3, at3, E)
        slot_e, at3 = carve(region3, at3, SLOTS)
        b1s, at3 = carve(region3, at3, E, IC)
        b2s, at3 = carve(region3, at3, E * D)
        rows_in, at3 = carve(region3, at3, 2, ROW)
        h_pre, at3 = carve(region3, at3, HID)
        hTd, at3 = carve(region3, at3, 2, HID)
        rows_out, at3 = carve(region3, at3, 2, D)
        rows_late, at3 = carve(region3, at3, 2, ROW)
        assert at3 <= SCRATCH
        wgates = sb("wgates", [P, KC, E])
        place = sb("place", [P, T], I32)
        slot_expert = sb("slot_expert", [1, SLOTS], I32)
        token = sb("token", [P, 2], I32)
        below = sb("below", [P, P])
        same_expert = sb("same_expert", [P, E * T])
        down = sb("down", [P, E])
        thr = sb("thr", [P, T])
        slot_no = sb("slot_no", [P, SLOTS])
        ints = sb("ints", [P, T + E + T + SLOTS], I32)

        stats2 = sb("stats2", [P, 2, 6])
        mv2 = sb("mv2", [P, 2, 2])
        ve2 = sb("ve2", [P, 2])
        rstd2 = sb("rstd2", [P, 2])

        col = 0

        def row(n):
            nonlocal col
            col += n
            return rowb[:, col - n:col]

        r_b0, r_bkv, r_bq, r_bo, r_gamma, r_beta = row(D), row(2 * D), row(D), row(D), row(D), row(D)
        r_bgate, r_gates = row(E), row(4)
        assert col == NR

        waits_taken = sem("waits_taken")

        def held(eng, s, value):
            if isinstance(value, int) and value <= 0:
                return
            eng.wait_ge(s, value)
            eng.sem_inc(waits_taken, 1)

        ld_x = [sem(f"ld_x{q}") for q in range(2)]
        ld_ca = [sem(f"ld_ca{q}") for q in range(2)]
        ld_cc = [sem(f"ld_cc{q}") for q in range(2)]
        ld_a = sem("ld_a")
        ld_keys = sem("ld_keys")
        ld_b = sem("ld_b")
        ld_cw = sem("ld_cw")
        keyb_zero = sem("keyb_zero")
        consts = sem("consts")
        ident_zero = sem("ident_zero")
        gates_done = sem("gates_done")
        simw_mm = sem("simw_mm")
        simw_done = sem("simw_done")

        def sems(prefix, names):
            return {n: sem(f"{prefix}_{n}") for n in names.split()}

        a = sems("a", "ve rstd xn xT xTs tq tqs vw vws sc mx ex ri pt pts o u r x")
        b = sems("b", "ve rstd xn xT xTs sim simS mx cand ext t8 nm d8 e8 z rz grid dots "
                      "pick pickx ex zz act sum1 sum2 tail last st sts up act2 y x")
        c = sems("c", "ve rstd xn ab xT xTs kv kvb kex k1 kvm kvms ks q qb qex q1 qT qTs den dene deni "
                      "num ao aoT aoTs oo r ve2 rstd2 n ga be x")
        d = sems("d", "ve rstd xn xT xTs lg lgs sh ex oh same cnt rank pli sei scat iota cvt fill ld_b "
                      "ld_w1 ld_w2")
        routing = sem("routing")
        f = sems("f", "ve rstd xn xT xTs h hs hT hTa y yo tok")
        ln2_bn, ln2_ag = sem("ln2_bn"), sem("ln2_ag")
        ln_bn, ln_ag = sem("ln_bn"), sem("ln_ag")
        ld_row = [sem(f"ld_row{q}") for q in range(2)]
        ld_late = [sem(f"ld_late{q}") for q in range(2)]
        sent = [sem(f"sent{q}") for q in range(2)]

        def ln_stats(dve, src, q, n, v):
            dve.bn_stats(stats[:, q, :], src).then_inc(ln_bn, 1)
            held(dve, ln_bn, n + 1)
            dve.bn_aggr(mv[:, q, :], stats[:, q, :]).then_inc(ln_ag, 1)
            dve.wait_ge(ln_ag, n + 1)
            dve.tensor_scalar(ve[:, q:q + 1], mv[:, q, 1:2], EPS_LN, None, ALU.add).then_inc(v, 1)

        def ln_apply(dve, dst, src, q, s, rs, done):
            dve.wait_ge(rs, s + 1)
            dve.tensor_scalar(dst, src, mv[:, q, 0:1], rstd[:, q:q + 1], ALU.subtract, ALU.mult)\
               .then_inc(done, 1)

        def ln_rstd(pool, q, s, v, rs):
            pool.wait_ge(v, s + 1)
            pool.tensor_tensor(rstd[:, q:q + 1], ve[:, q:q + 1], neg_half[:, :], ALU.pow).then_inc(rs, 1)

        def tile_of(t):
            return bass.ds(t, 1)

        def loads(t, q):
            return 8 * (t - q) + 16

        def x_at(t):
            return xs[:, tile_of(t), 0:D].rearrange("p a d -> p (a d)")

        block = ctx.enter_context(nc.Block())

        @block.sync
        def _(sp):
            sp.dma_start(w0s, w0).then_inc(ld_a, 16)
            sp.dma_start(wgates[:], wgate).then_inc(ld_a, 16)
            sp.dma_start(colb[:], cols).then_inc(ld_a, 16)
            sp.dma_start(rowb[:], rows.partition_broadcast(P).rearrange("p a n -> p (a n)")).then_inc(ld_a, 16)

            def load_a(t, q, live):
                wait(sp, ln_bn, t - 1)
                sp.dma_start(x_at(t), x[tile_of(t)].rearrange("a p d -> (a p) d")).then_inc(ld_x[q], 16)
                wait(sp, a["vw"], t - 1)
                sp.dma_start(ctxb[:, q], ctxT[tile_of(t)].rearrange("a p k n -> (a p) k n")).then_inc(ld_ca[q], 16)
            pipeline(sp, T, 2, lambda t, q, live: load_a(t, q, live) if 0 in live else None)

            def load_c(t, q, live):
                if isinstance(t, int):
                    sp.wait_ge(a["vw"], T)
                wait(sp, c["kv"], t - 1)
                sp.dma_start(ctxb[:, q], ctxT[tile_of(t)].rearrange("a p k n -> (a p) k n")).then_inc(ld_cc[q], 16)
            pipeline(sp, T, 2, lambda t, q, live: load_c(t, q, live) if 0 in live else None)
            sp.wait_ge(d["scat"], 16 * T)

            def load_rows(t, q, live):
                if 0 in live:
                    wait(sp, f["xn"], t - 1)
                    sp.dma_start(rows_in[:, q], sorted_rows[bass.ds(t * P, P), :]).then_inc(ld_row[q], 16)
                if 1 in live:
                    s, r = t - 1, 1 - q
                    wait(sp, f["yo"], s - 1)
                    sp.dma_start(rows_late[:, r], sorted_rows[bass.ds(s * P, P), :]).then_inc(ld_late[r], 16)
            pipeline(sp, SLOTS, 2, load_rows, peel=4)

        @block.gpsimd
        def _(pool):
            pool.memset(keyb, 0.0).then_inc(keyb_zero, 1)
            pool.memset(far, FAR).then_inc(d["cvt"], 1)
            pool.memset(ident[:], 0.0).then_inc(ident_zero, 1)
            pool.memset(ones[:], 1.0).then_inc(consts, 1)
            pool.memset(neg_half[:], -0.5).then_inc(consts, 1)
            pool.wait_ge(ident_zero, 1)
            pool.affine_select(out=ident[:], in_=ident[:], compare_op=ALU.not_equal, fill=1.0, base=0,
                               pattern=[[-1, P]], channel_multiplier=1).then_inc(consts, 1)
            pool.wait_ge(consts, 3)
            pool.affine_select(out=below[:], in_=ones[:], compare_op=ALU.is_gt, fill=0.0, base=0,
                               pattern=[[1, P]], channel_multiplier=-1).then_inc(consts, 1)
            n = 0
            for count, first, step, channel in ((E, E, -1, 0), (T, 0, P, 0), (SLOTS, 0, 1, 0), (T, 0, P, 1)):
                pool.iota(ints[:, n:n + count], pattern=[[step, count]], base=first,
                          channel_multiplier=channel).then_inc(d["iota"], 1)
                n += count
            pool.wait_ge(d["cvt"], 1)
            for n in range(SLOTS):
                pool.dma_start(sorted_rows[n * P:(n + 1) * P, :], far).then_inc(d["fill"], 16)
            pool.wait_ge(consts, 4)

            def step_a(t, q, live):
                if 0 in live:
                    ln_rstd(pool, q, t, a["ve"], a["rstd"])
            pipeline(pool, T, 3, step_a)

            def grids(t, q):
                pool.wait_ge(b["simS"], t + 1)
                wait(pool, b["ex"], HEADS * (t - 1))
                for h in range(HEADS):
                    pool.tensor_tensor(
                        grid[:, q, h, 0:HID].rearrange("p (a b) -> p a b", b=NK),
                        simS[:, q, h * NK:h * NK + NX].unsqueeze(2).to_broadcast([P, NX, NK]),
                        simS[:, q, BANK // 2 + h * NK:BANK // 2 + (h + 1) * NK].unsqueeze(1).to_broadcast([P, NX, NK]),
                        ALU.add).then_inc(b["grid"], 1)

            def sum_heads(s, q):
                for h in (0, 2):
                    pool.wait_ge(b["act"], HEADS * s + h + 2)
                    pool.tensor_tensor(picked[:, q, h], picked[:, q, h], picked[:, q, h + 1], ALU.add)\
                        .then_inc(b["sum1"], 1)
                pool.wait_ge(b["sum1"], 2 * s + 2)
                pool.tensor_tensor(picked[:, q, 0], picked[:, q, 0], picked[:, q, 2], ALU.add)\
                    .then_inc(b["sum2"], 1)

            def step_b(t, q, live):
                if 0 in live:
                    ln_rstd(pool, q, t, b["ve"], b["rstd"])
                if 2 in live:
                    sum_heads(t - 2, q)
                if 0 in live:
                    grids(t, q)
            pipeline(pool, T, 4, step_b)

            def step_c(t, q, live):
                if 0 in live:
                    ln_rstd(pool, q, t, c["ve"], c["rstd"])
                    pool.wait_ge(c["xn"], t + 1)
                    wait(pool, c["r"], t - 1)
                    pool.tensor_tensor(audio[:, q], xn[:, q], r_bo, ALU.add).then_inc(c["ab"], 1)
                if 2 in live:
                    pool.wait_ge(c["ve2"], t - 1)
                    pool.tensor_tensor(rstd2[:, q:q + 1], ve2[:, q:q + 1], neg_half[:, :], ALU.pow)\
                        .then_inc(c["rstd2"], 1)
            pipeline(pool, T, 3, step_c)

            def step_d(t, q, live):
                if 0 in live:
                    ln_rstd(pool, q, t, d["ve"], d["rstd"])
            pipeline(pool, T, 2, step_d)
            pool.wait_ge(d["fill"], 16 * SLOTS)
            pool.wait_ge(d["pli"], 1)
            for t in range(T):
                pool.indirect_dma_start(out=sorted_rows, out_offset=bass.IndirectOffsetOnAxis(ap=place[:, t:t + 1], axis=0),
                                        in_=xs[:, t, :], in_offset=None).then_inc(d["scat"], 16)

            def step_f(t, q, live):
                if 0 in live:
                    ln_rstd(pool, q, t, f["ve"], f["rstd"])
                if 2 in live:
                    held(pool, f["yo"], t - 1)
                    pool.indirect_dma_start(
                        out=out.rearrange("t p d -> (t p) d"),
                        out_offset=bass.IndirectOffsetOnAxis(ap=token[:, q:q + 1], axis=0),
                        in_=rows_out[:, q], in_offset=None, bounds_check=T * P - 1, oob_is_err=False)\
                        .then_inc(sent[q], 16)
            pipeline(pool, SLOTS, 3, step_f)
            pool.wait_ge(sent[0], 16 * ((SLOTS + 1) // 2))
            pool.wait_ge(sent[1], 16 * (SLOTS // 2))

        @block.vector
        def _(dve):
            dve.wait_ge(consts, 4)

            def step_a(t, q, live):
                if 0 in live:
                    dve.wait_ge(ld_x[q], loads(t, q))
                    ln_stats(dve, x_at(t), q, t, a["ve"])
                if 1 in live:
                    s, r = t - 1, 1 - q
                    dve.wait_ge(a["sc"], s + 1)
                    dve.tensor_reduce(nmax[:, r:r + 1], scoresA[r][:, 0:P], AX.X, ALU.max, negate=True)\
                        .then_inc(a["mx"], 1)
                if 0 in live:
                    ln_apply(dve, xn[:, q], x_at(t), q, t, a["rstd"], a["xn"])
                if 2 in live:
                    s = t - 2
                    dve.wait_ge(a["ex"], s + 1)
                    dve.reciprocal(rsum[:, q:q + 1], esum[:, q:q + 1]).then_inc(a["ri"], 1)
                if 0 in live:
                    dve.wait_ge(a["xT"], t + 1)
                    dve.tensor_copy(xT[:, q].rearrange("p k n -> p (k n)"), banks[0][:, 0:D]).then_inc(a["xTs"], 1)
                if 2 in live:
                    dve.wait_ge(a["ri"], s + 1)
                    dve.wait_ge(a["o"], s + 1)
                    dve.scalar_tensor_tensor(out=u_buf[:, q], in0=outA[q][:, 0:D], scalar=rsum[:, q:q + 1],
                                             in1=r_b0, op0=ALU.mult, op1=ALU.add).then_inc(a["u"], 1)
                    dve.wait_ge(a["u"], s + 1)
                    dve.tensor_scalar(r_buf[:, q], u_buf[:, q], 0.0, gate[:, 0:1], ALU.max, ALU.mult)\
                       .then_inc(a["r"], 1)
                    dve.wait_ge(a["r"], s + 1)
                    dve.tensor_tensor(x_at(s), x_at(s), r_buf[:, q], ALU.add).then_inc(a["x"], 1)
            dve.wait_ge(ld_a, 64)
            dve.wait_ge(gates_done, 1)
            dve.wait_ge(d["iota"], 4)
            dve.memset(same_expert[:, :], 1.0).then_inc(d["same"], 1)
            dve.tensor_copy(down[:, :], ints[:, 0:E])
            dve.wait_ge(d["same"], 1)
            dve.memset(same_expert[:, :].rearrange("p (e t) -> p e t", e=E)[:, :, 0], 0.0)
            dve.tensor_copy(thr[:, :], ints[:, E:E + T])
            dve.tensor_copy(slot_no[:, :], ints[:, E + T:E + T + SLOTS])
            dve.tensor_copy(xs[:, :, D + 1], ints[:, E + T + SLOTS:E + 2 * T + SLOTS]).then_inc(d["cvt"], 1)
            pipeline(dve, T, 3, step_a)
            dve.wait_ge(simw_mm, 1)
            dve.tensor_copy(simw[:, 0], banks[6][:]).then_inc(simw_done, 1)
            dve.tensor_copy(simw[:, 1], banks[7][:]).then_inc(simw_done, 1)

            def pick(s, r, h):
                if h == 0:
                    dve.wait_ge(b["dots"], s + 1)
                    wait(dve, b["st"], s - 1)
                dve.wait_ge(b["grid"], HEADS * s + h + 1)
                least = top[:, r, h, TOP - 1:TOP]
                dve.scalar_tensor_tensor(out=picked[:, r, h, 0:HID], in0=grid[:, r, h, 0:HID], scalar=least,
                                         in1=table_dots[:, :], op0=ALU.is_ge, op1=ALU.mult).then_inc(b["pick"], 1)
                dve.scalar_tensor_tensor(out=picked[:, r, h, HID:GRID], in0=grid[:, r, h, HID:GRID], scalar=least,
                                         in1=table_dots[:, HID - 1:HID].to_broadcast([P, PAIRS]),
                                         op0=ALU.is_ge, op1=ALU.mult).then_inc(b["pick"], 1)

            def weigh(s, r, h):
                dve.wait_ge(b["ex"], HEADS * s + h + 1)
                dve.tensor_tensor(picked[:, r, h], picked[:, r, h], grid[:, r, h], ALU.mult).then_inc(b["zz"], 1)

            def step_b(t, q, live):
                F, B1, B2, FIN = (k in live for k in range(4))
                if FIN:
                    s = t - 3
                    dve.wait_ge(b["y"], s + 1)
                    dve.scalar_tensor_tensor(out=x_at(s), in0=banks[6][:, 0:D], scalar=gate[:, 2:3], in1=x_at(s),
                                             op0=ALU.mult, op1=ALU.add).then_inc(b["x"], 1)
                if F:
                    ln_stats(dve, x_at(t), q, t + T, b["ve"])
                if B1:
                    pick(t - 1, 1 - q, 0)
                if F:
                    ln_apply(dve, xn[:, q], x_at(t), q, t, b["rstd"], b["xn"])
                if B1:
                    s, r = t - 1, 1 - q
                    dve.wait_ge(b["e8"], s + 1)
                    dve.tensor_reduce(zsum[:, r], e8[:, r].rearrange("p (h k) -> p h k", k=TOP), AX.X, ALU.add)\
                       .then_inc(b["z"], 1)
                    pick(s, r, 1)
                    dve.wait_ge(b["z"], s + 1)
                    dve.reciprocal(rz[:, r], zsum[:, r]).then_inc(b["rz"], 1)
                if F:
                    dve.wait_ge(b["xT"], t + 1)
                    dve.tensor_copy(xT[:, q].rearrange("p k n -> p (k n)"), banks[0][:, 0:D]).then_inc(b["xTs"], 1)
                if B1:
                    pick(t - 1, 1 - q, 2)
                    pick(t - 1, 1 - q, 3)
                if F:
                    dve.wait_ge(b["sim"], t + 1)
                    wait(dve, b["grid"], HEADS * (t - 1))
                    dve.tensor_copy(simS[:, q], banks[1][:]).then_inc(b["simS"], 1)
                if B2:
                    s = t - 2
                    dve.wait_ge(b["sum2"], s + 1)
                    dve.tensor_reduce(tail[:, q:q + 1], picked[:, q, 0, HID - 1:GRID], AX.X, ALU.add)\
                       .then_inc(b["tail"], 1)
                if B1:
                    weigh(t - 1, 1 - q, 0)
                if B2:
                    dve.wait_ge(b["tail"], s + 1)
                    dve.tensor_copy(picked[:, q, 0, HID - 1:HID], tail[:, q:q + 1]).then_inc(b["last"], 1)
                if F:
                    held(dve, b["simS"], t + 1)
                    for h in range(HEADS):
                        first, second = h * NK, BANK // 2 + h * NK
                        dve.max(top_x[:, q, h], simS[:, q, first:first + NK])
                        dve.max(top_y[:, q, h], simS[:, q, second:second + NK])
                        last = dve.max(top_c[:, q, h], simS[:, q, first + NX:first + NK])
                    last.then_inc(b["mx"], 1)
                if B1:
                    weigh(t - 1, 1 - q, 1)
                if F:
                    dve.wait_ge(b["mx"], t + 1)
                    wait(dve, b["ex"], HEADS * (t - 1))
                    for h in range(HEADS):
                        y = top_y[:, q, h].unsqueeze(1).to_broadcast([P, TOP, TOP])
                        dve.tensor_tensor(cand[:, q, h].rearrange("p (i j) -> p i j", j=TOP),
                                          top_x[:, q, h].unsqueeze(2).to_broadcast([P, TOP, TOP]), y, ALU.add)
                        last = dve.tensor_tensor(grid[:, q, h, HID:GRID].rearrange("p (i j) -> p i j", j=TOP),
                                                 top_c[:, q, h].unsqueeze(2).to_broadcast([P, TOP, TOP]), y, ALU.add)
                    last.then_inc(b["cand"], 1)
                    held(dve, b["cand"], t + 1)
                    for h in range(HEADS):
                        last = dve.max(top[:, q, h], cand[:, q, h])
                    last.then_inc(b["t8"], 1)
                if B1:
                    weigh(t - 1, 1 - q, 2)
                if F:
                    dve.wait_ge(b["t8"], t + 1)
                    dve.tensor_scalar(nm[:, q], top[:, q, :, 0], -1.0, None, ALU.mult).then_inc(b["nm"], 1)
                    wait(dve, b["e8"], t - 1)
                    dve.tensor_tensor(d8[:, q].rearrange("p (h k) -> p h k", k=TOP), top[:, q],
                                      top[:, q, :, 0:1].to_broadcast([P, HEADS, TOP]), ALU.subtract).then_inc(b["d8"], 1)
                if B1:
                    weigh(t - 1, 1 - q, 3)
            pipeline(dve, T, 4, step_b)

            def step_c(t, q, live):
                A0, A1, A2 = (k in live for k in range(3))
                if A0:
                    ln_stats(dve, x_at(t), q, t + 2 * T, c["ve"])
                if A1:
                    s, r = t - 1, 1 - q
                    dve.wait_ge(c["kex"], s + 1)
                    dve.scalar_tensor_tensor(out=k1[:, r], in0=kexp[:, r], scalar=1.0, in1=krel[:, r],
                                             op0=ALU.min, op1=ALU.add).then_inc(c["k1"], 1)
                    dve.wait_ge(c["qex"], s + 1)
                    dve.scalar_tensor_tensor(out=q1[:, r], in0=qexp[:, r], scalar=1.0, in1=qrel[:, r],
                                             op0=ALU.min, op1=ALU.add).then_inc(c["q1"], 1)
                if A2:
                    s = t - 2
                    dve.wait_ge(c["num"], s + 1)
                    dve.tensor_tensor(ao[:, q], banks[6][:, 0:D], den[:, q], ALU.mult).then_inc(c["ao"], 1)
                if A0:
                    ln_apply(dve, xn[:, q], x_at(t), q, t, c["rstd"], c["xn"])
                if A1:
                    s, r = t - 1, 1 - q
                    dve.wait_ge(c["q1"], s + 1)
                    dve.wait_ge(c["ks"], s + 1)
                    dve.tensor_tensor(den[:, r], q1[:, r], banks[3][:, 0:D], ALU.mult).then_inc(c["den"], 1)
                    dve.wait_ge(c["den"], s + 1)
                    dve.tensor_scalar(den[:, r], den[:, r], EPS_DENOM, None, ALU.add).then_inc(c["dene"], 1)
                    dve.wait_ge(c["dene"], s + 1)
                    dve.reciprocal(den[:, r], den[:, r]).then_inc(c["deni"], 1)
                if A0:
                    dve.wait_ge(c["xT"], t + 1)
                    dve.tensor_copy(xT[:, q].rearrange("p k n -> p (k n)"), banks[0][:, 0:D]).then_inc(c["xTs"], 1)
                if A2:
                    s = t - 2
                    dve.wait_ge(c["oo"], s + 1)
                    dve.wait_ge(c["ab"], s + 1)
                    dve.tensor_tensor(res[:, q], banks[7][:, 0:D], audio[:, q], ALU.add).then_inc(c["r"], 1)
                    dve.wait_ge(c["r"], s + 1)
                    dve.bn_stats(stats2[:, q, :], res[:, q]).then_inc(ln2_bn, 1)
                    held(dve, ln2_bn, s + 1)
                    dve.bn_aggr(mv2[:, q, :], stats2[:, q, :]).then_inc(ln2_ag, 1)
                    dve.wait_ge(ln2_ag, s + 1)
                    dve.tensor_scalar(ve2[:, q:q + 1], mv2[:, q, 1:2], EPS_LN, None, ALU.add).then_inc(c["ve2"], 1)
                if A0:
                    dve.wait_ge(c["kv"], t + 1)
                    wait(dve, c["kvm"], t - 1)
                    dve.tensor_tensor(kvb[:, q], banks[1][:], r_bkv, ALU.add).then_inc(c["kvb"], 1)
                    dve.wait_ge(c["q"], t + 1)
                    wait(dve, c["qex"], t - 1)
                    dve.tensor_tensor(qb[:, q], banks[4][:, 0:D], r_bq, ALU.add).then_inc(c["qb"], 1)
                if A2:
                    dve.wait_ge(c["rstd2"], s + 1)
                    dve.tensor_scalar(res[:, q], res[:, q], mv2[:, q, 0:1], rstd2[:, q:q + 1], ALU.subtract, ALU.mult)\
                       .then_inc(c["n"], 1)
                    dve.wait_ge(c["n"], s + 1)
                    dve.tensor_tensor(res[:, q], res[:, q], r_gamma, ALU.mult).then_inc(c["ga"], 1)
                    dve.wait_ge(c["ga"], s + 1)
                    dve.tensor_tensor(res[:, q], res[:, q], r_beta, ALU.add).then_inc(c["be"], 1)
                    dve.wait_ge(c["be"], s + 1)
                    dve.scalar_tensor_tensor(out=x_at(s), in0=res[:, q], scalar=gate[:, 1:2], in1=x_at(s),
                                             op0=ALU.mult, op1=ALU.add).then_inc(c["x"], 1)
            pipeline(dve, T, 3, step_c)

            def step_d(t, q, live):
                if 0 in live:
                    ln_stats(dve, x_at(t), q, t + 3 * T, d["ve"])
                if 1 in live:
                    s, r = t - 1, 1 - q
                    dve.wait_ge(d["xT"], s + 1)
                    dve.tensor_copy(xT[:, r].rearrange("p k n -> p (k n)"), banks[0][:, 0:D]).then_inc(d["xTs"], 1)
                if 0 in live:
                    ln_apply(dve, xn[:, q], x_at(t), q, t, d["rstd"], d["xn"])
                if 1 in live:
                    dve.wait_ge(d["lg"], s + 1)
                    dve.tensor_tensor(logits[:, tile_of(s), :].rearrange("p a e -> p (a e)"), banks[1][:, 0:E],
                                      r_bgate, ALU.add).then_inc(d["lgs"], 1)
            pipeline(dve, T, 2, step_d)

            links = [0]

            def link(ins):
                links[0] += 1
                ins.then_inc(routing, 1)
                dve.wait_ge(routing, links[0])

            dve.wait_ge(d["lgs"], T)
            link(dve.tensor_reduce(top_logit, logits, AX.X, ALU.max))
            best = top_logit.unsqueeze(2).to_broadcast([P, T, E])
            dve.tensor_tensor(shifted, logits, best, ALU.subtract).then_inc(d["sh"], 1)
            link(dve.tensor_tensor(ranked, logits, best, ALU.is_ge))
            link(dve.tensor_tensor(ranked, ranked, down[:, :].unsqueeze(1).to_broadcast([P, T, E]), ALU.mult))
            link(dve.tensor_reduce(first_best, ranked, AX.X, ALU.max))
            link(dve.tensor_tensor(onehot.rearrange("p e t -> p t e"), ranked,
                                   first_best.unsqueeze(2).to_broadcast([P, T, E]), ALU.is_equal))
            flat = lambda v: v.rearrange("p e t -> p (e t)")
            link(dve.tensor_tensor_scan(flat(before), same_expert[:, :], flat(onehot), 0.0, ALU.mult, ALU.add))
            link(dve.tensor_copy(onehot_sum, before[:, :, T - 1]))
            dve.tensor_tensor(before, before, onehot, ALU.subtract).then_inc(d["oh"], 1)
            dve.wait_ge(d["ex"], 1)
            link(dve.tensor_reduce(exp_sum, shifted, AX.X, ALU.add))
            link(dve.reciprocal(exp_sum, exp_sum))
            link(dve.tensor_scalar(xs[:, :, D], exp_sum, gate[:, 3:4], None, ALU.mult))
            dve.wait_ge(d["cnt"], 1)
            link(dve.tensor_copy(counts, banks[5][:, 0:E]))
            link(dve.tensor_tensor(fits, counts.unsqueeze(2).to_broadcast([P, E, T]),
                                   thr[:, :].unsqueeze(1).to_broadcast([P, E, T]), ALU.is_gt))
            link(dve.tensor_reduce(slots_of, fits, AX.X, ALU.add))
            link(dve.tensor_tensor_scan(slot_end, ones[:, 0:E], slots_of, 0.0, ALU.mult, ALU.add))
            link(dve.tensor_tensor(row_base, slot_end, slots_of, ALU.subtract))
            link(dve.tensor_scalar(row_base, row_base, float(P), None, ALU.mult))
            dve.wait_ge(d["rank"], 1)
            link(dve.tensor_tensor(places, banks[4][:, 0:T * E].rearrange("p (e t) -> p e t", e=E),
                                   row_base.unsqueeze(2).to_broadcast([P, E, T]), ALU.add))
            link(dve.tensor_tensor(places, places, onehot, ALU.mult))
            link(dve.tensor_reduce(place_f, places.rearrange("p e t -> p t e"), AX.X, ALU.add))
            dve.tensor_copy(place[:, :], place_f).then_inc(d["pli"], 1)
            link(dve.tensor_tensor(slot_cmp, slot_no[:, :].unsqueeze(2).to_broadcast([P, SLOTS, E]),
                                   slot_end.unsqueeze(1).to_broadcast([P, SLOTS, E]), ALU.is_ge))
            link(dve.tensor_reduce(slot_e, slot_cmp, AX.X, ALU.add))
            dve.tensor_scalar(slot_expert[:, :], slot_e[0:1], float(E - 1), None, ALU.min).then_inc(d["sei"], 1)

            def step_f(t, q, live):
                S0, S1, S2 = (k in live for k in range(3))
                if S0:
                    dve.wait_ge(ld_row[q], loads(t, q))
                    ln_stats(dve, rows_in[:, q, 0:D], q, t + 4 * T, f["ve"])
                if S2:
                    s = t - 2
                    dve.wait_ge(ld_late[q], loads(s, q))
                    wait(dve, sent[q], loads(s, q) - 16)
                    dve.tensor_copy(token[:, q:q + 1], rows_late[:, q, D + 1:D + 2]).then_inc(f["tok"], 1)
                if S0:
                    ln_apply(dve, xn[:, q], rows_in[:, q, 0:D], q, t, f["rstd"], f["xn"])
                    dve.wait_ge(f["xT"], t + 1)
                    dve.tensor_copy(xT[:, q].rearrange("p k n -> p (k n)"), banks[0][:, 0:D]).then_inc(f["xTs"], 1)
                if S2:
                    dve.wait_ge(f["y"], s + 1)
                    dve.scalar_tensor_tensor(out=rows_out[:, q], in0=banks[6][:, 0:D], scalar=rows_late[:, q, D:D + 1],
                                             in1=rows_late[:, q, 0:D], op0=ALU.mult, op1=ALU.add).then_inc(f["yo"], 1)
            pipeline(dve, SLOTS, 3, step_f)

        @block.scalar
        def _(act):
            act.wait_ge(ld_a, 64)
            act.activation(gate[:], r_gates, ACT.Tanh).then_inc(gates_done, 1)
            act.dma_start(wqs, wq).then_inc(ld_keys, 16)
            act.wait_ge(keyb_zero, 1)
            act.dma_start(keyb[0:NK, :, 0:NK], keys[0:NK]).then_inc(ld_keys, 16)
            act.dma_start(keyb[NK:P, :, NK:P], keys[NK:P]).then_inc(ld_keys, 16)
            for dst, src in ((dembs, demb), (wups, wup), (wdns, wdn), (uembs, uemb)):
                act.dma_start(dst, src).then_inc(ld_b, 16)
            for dst, src in ((wkvs, wkv), (wqcs, wqc), (wocs, woc)):
                act.dma_start(dst[:], src).then_inc(ld_cw, 16)

            def step_a(t, q, live):
                if 1 in live:
                    s, r = t - 1, 1 - q
                    act.wait_ge(a["mx"], s + 1)
                    wait(act, a["pt"], s - 1)
                    wait(act, a["ri"], s - 1)
                    act.activation(prob[:, r], scoresA[r][:, 0:P], ACT.Exp, bias=nmax[:, r:r + 1],
                                   accum_out=esum[:, r:r + 1]).then_inc(a["ex"], 1)
                if 0 in live:
                    act.wait_ge(a["tq"], t + 1)
                    wait(act, a["sc"], t - 1)
                    for k in range(KC):
                        last = act.activation(tqs[:, q, k], banks[1][:, k * P:(k + 1) * P], ACT.Identity,
                                              bias=colb[:, k:k + 1])
                    last.then_inc(a["tqs"], 1)
                    act.wait_ge(a["vw"], t + 1)
                    wait(act, a["o"], t - 1)
                    act.activation(vws[:, q], banks[2][:, 0:D], ACT.Copy).then_inc(a["vws"], 1)
                if 1 in live:
                    act.wait_ge(a["pt"], s + 1)
                    wait(act, a["o"], s - 1)
                    act.activation(probT[:, r], banks[5][:, 0:P], ACT.Copy).then_inc(a["pts"], 1)
            pipeline(act, T, 3, step_a)
            def step_b(t, q, live):
                B1, B2 = 1 in live, 2 in live
                if B1:
                    s, r = t - 1, 1 - q
                    act.wait_ge(b["d8"], s + 1)
                    act.activation(e8[:, r], d8[:, r], ACT.Exp).then_inc(b["e8"], 1)
                    for h in range(HEADS):
                        act.wait_ge(b["pick"], 2 * (HEADS * s + h) + 2)
                        act.activation(grid[:, r, h], grid[:, r, h], ACT.Exp, bias=nm[:, r, h:h + 1])\
                           .then_inc(b["ex"], 1)
                if B2:
                    s = t - 2
                    for g in range(2):
                        act.wait_ge(b["st"], 2 * s + g + 1)
                        if g == 0:
                            wait(act, b["y"], s)
                        act.activation(pickT[:, g * BANK:(g + 1) * BANK], banks[7][:] if g else banks[0][:, :],
                                       ACT.Copy).then_inc(b["sts"], 1)
                if B1:
                    s, r = t - 1, 1 - q
                    for g in range(2):
                        act.wait_ge(b["up"], 2 * s + g + 1)
                        if g == 0:
                            wait(act, b["y"], s - 1)
                        act.activation(hT[:, r, g * BANK:(g + 1) * BANK], banks[4 + g][:], ACT.Silu)\
                           .then_inc(b["act2"], 1)
                    for h in range(HEADS):
                        act.wait_ge(b["zz"], HEADS * s + h + 1)
                        if h == 0:
                            act.wait_ge(b["rz"], s + 1)
                        act.activation(picked[:, r, h], picked[:, r, h], ACT.Silu, scale=rz[:, r, h:h + 1])\
                           .then_inc(b["act"], 1)
            pipeline(act, T, 4, step_b)

            act.wait_ge(b["x"], T)
            act.wait_ge(d["fill"], 16 * SLOTS)

            def step_c(t, q, live):
                A0, A1, A2 = (k in live for k in range(3))
                if A2:
                    s = t - 2
                    act.wait_ge(c["aoT"], s + 1)
                    act.activation(aoTs[:, q].rearrange("p k n -> p (k n)"), banks[7][:, D:2 * D], ACT.Copy)\
                       .then_inc(c["aoTs"], 1)
                if A1:
                    s, r = t - 1, 1 - q
                    act.wait_ge(c["kvm"], s + 1)
                    wait(act, c["num"], s - 1)
                    act.activation(kvs[:, r].rearrange("p k n -> p (k n)"), banks[2], ACT.Copy).then_inc(c["kvms"], 1)
                    act.wait_ge(c["qT"], s + 1)
                    act.activation(q1T[:, r].rearrange("p k n -> p (k n)"), banks[5][:, 0:D], ACT.Copy)\
                       .then_inc(c["qTs"], 1)
                if A0:
                    act.wait_ge(c["kvb"], t + 1)
                    wait(act, c["k1"], t - 1)
                    act.activation(kexp[:, q], kvb[:, q, 0:D], ACT.Exp)
                    act.activation(krel[:, q], kvb[:, q, 0:D], ACT.Relu).then_inc(c["kex"], 1)
                    act.wait_ge(c["qb"], t + 1)
                    wait(act, c["q1"], t - 1)
                    act.activation(qexp[:, q], qb[:, q], ACT.Exp)
                    act.activation(qrel[:, q], qb[:, q], ACT.Relu).then_inc(c["qex"], 1)
            for e in range(E):
                act.dma_start(w1s[:, e], w1[:, e]).then_inc(d["ld_w1"], 16)
                act.dma_start(w2s[:, e], w2[:, e]).then_inc(d["ld_w2"], 16)
            pipeline(act, T, 3, step_c)

            act.wait_ge(c["x"], T)
            act.dma_start(b1s, b1).then_inc(d["ld_b"], 16)
            act.dma_start(b2s[0:1], b2).then_inc(d["ld_b"], 16)
            act.wait_ge(d["sh"], 1)
            act.activation(shifted, shifted, ACT.Exp).then_inc(d["ex"], 1)
            act.wait_ge(d["sei"], 1)
            act.wait_ge(d["ld_b"], 32)

            def step_f(t, q, live):
                if 1 in live:
                    s, r = t - 1, 1 - q
                    e = act.value_load(slot_expert[0:1, bass.ds(s, 1)], min_val=0, max_val=E - 1)
                    act.wait_ge(f["h"], s + 1)
                    wait(act, f["hT"], 2 * s)
                    act.activation(h_pre, table_dots[:, :], ACT.Copy).then_inc(f["hs"], 1)
                    for g in range(2):
                        held(act, f["hT"], 2 * s + g + 1)
                        if g == 0:
                            held(act, f["y"], s - 1)
                        for m in range(4 * g, 4 * g + 4):
                            last = act.activation(hTd[:, r, m * P:(m + 1) * P], banks[4 + g][:, (m % 4) * P:(m % 4 + 1) * P],
                                                  ACT.Relu, bias=b1s[:, bass.ds(e, 1), m])
                        last.then_inc(f["hTa"], 1)
            pipeline(act, SLOTS, 3, step_f)

        @block.tensor
        def _(pe):
            pe.wait_ge(consts, 4)
            pe.wait_ge(ld_a, 64)

            def transpose2(dst, src, done):
                for k in range(KC):
                    last = pe.transpose(dst[:, k * P:(k + 1) * P], src[:, k * P:(k + 1) * P], ident[:, :])
                last.then_inc(done, 1)

            def step_a(t, q, live):
                if 1 in live:
                    s, r = t - 1, 1 - q
                    pe.wait_ge(a["xTs"], s + 1)
                    pe.wait_ge(a["tqs"], s + 1)
                    wait(pe, a["ex"], s - 1)
                    for k in range(KC):
                        last = pe.matmul(scoresA[r][:, 0:P], xT[:, r, k], tqs[:, r, k],
                                         start=(k == 0), stop=(k == KC - 1))
                    last.then_inc(a["sc"], 1)
                if 0 in live:
                    pe.wait_ge(a["xn"], t + 1)
                    wait(pe, a["xTs"], t)
                    transpose2(banks[0], xn[:, q], a["xT"])
                    pe.wait_ge(ld_ca[q], loads(t, q))
                    wait(pe, a["tqs"], t)
                    for o in range(KC):
                        for k in range(KC):
                            last = pe.matmul(banks[1][:, o * P:(o + 1) * P], w0s[:, k, o * P:(o + 1) * P], ctxb[:, q, k],
                                             start=(k == 0), stop=(k == KC - 1))
                    last.then_inc(a["tq"], 1)
                    wait(pe, a["vws"], t)
                    for k in range(KC):
                        last = pe.matmul(banks[2][:, 0:D], ctxb[:, q, k], w0s[:, k], start=(k == 0), stop=(k == KC - 1))
                    last.then_inc(a["vw"], 1)
                if 2 in live:
                    s = t - 2
                    pe.wait_ge(a["pts"], s + 1)
                    pe.wait_ge(a["vws"], s + 1)
                    wait(pe, a["u"], s - 1)
                    pe.matmul(outA[q][:, 0:D], probT[:, q], vws[:, q], start=True, stop=True).then_inc(a["o"], 1)
                if 1 in live:
                    s, r = t - 1, 1 - q
                    pe.wait_ge(a["ex"], s + 1)
                    wait(pe, a["pts"], s)
                    pe.transpose(banks[5][:, 0:P], prob[:, r], ident[:, :]).then_inc(a["pt"], 1)
            pipeline(pe, T, 3, step_a)

            pe.wait_ge(ld_keys, 48)
            pe.wait_ge(a["u"], T)
            for k in range(KC):
                for n in range(4):
                    last = pe.matmul(banks[6 + k][:, n * P:(n + 1) * P], wqs[:, n, k * P:(k + 1) * P],
                                     keyb[:, n], start=True, stop=True)
            last.then_inc(simw_mm, 1)

            pe.wait_ge(simw_done, 2)
            pe.wait_ge(ld_b, 64)

            def step_b(t, q, live):
                F, B1, B2 = (k in live for k in range(3))
                if F:
                    pe.wait_ge(b["xn"], t + 1)
                    wait(pe, b["sts"], 2 * (t - 2) - 1)
                    transpose2(banks[0], xn[:, q], b["xT"])
                if B1:
                    s, r = t - 1, 1 - q
                    for g in range(2):
                        wait(pe, b["act2"], 2 * (s - 1) + g + 1)
                        for m in range(4):
                            for k in range(KC):
                                last = pe.matmul(banks[4 + g][:, m * P:(m + 1) * P],
                                                 wups[:, k, (4 * g + m) * P:(4 * g + m + 1) * P],
                                                 xT[:, r, k], start=(k == 0), stop=(k == KC - 1))
                        last.then_inc(b["up"], 1)
                if F:
                    pe.wait_ge(b["xTs"], t + 1)
                    wait(pe, b["simS"], t)
                    for k in range(KC):
                        last = pe.matmul(banks[1][:], xT[:, q, k], simw[:, k], start=(k == 0), stop=(k == KC - 1))
                    last.then_inc(b["sim"], 1)
                    wait(pe, b["pick"], 2 * HEADS * t)
                    for g in range(2):
                        for k in range(KC):
                            last = pe.matmul(banks[2 + g], xT[:, q, k], dembs[:, k, g * BANK:(g + 1) * BANK],
                                             start=(k == 0), stop=(k == KC - 1))
                    last.then_inc(b["dots"], 1)
                if B2:
                    s = t - 2
                    pe.wait_ge(b["last"], s + 1)
                    for g in range(2):
                        if g == 1:
                            wait(pe, b["sts"], 2 * s)
                        for m in range(4):
                            last = pe.transpose((banks[7] if g else banks[0])[:, m * P:(m + 1) * P],
                                                picked[:, q, 0, (4 * g + m) * P:(4 * g + m + 1) * P], ident[:, :])
                        last.then_inc(b["st"], 1)
                    wait(pe, b["x"], s)
                    for m in range(IC):
                        if m % 4 == 0:
                            pe.wait_ge(b["act2"], 2 * s + m // 4 + 1)
                        pe.matmul(banks[6][:, 0:D], hT[:, q, m * P:(m + 1) * P], wdns[:, m], start=(m == 0), stop=False)
                    for m in range(IC):
                        if m % 4 == 0:
                            pe.wait_ge(b["sts"], 2 * s + m // 4 + 1)
                        last = pe.matmul(banks[6][:, 0:D], pickT[:, m * P:(m + 1) * P], uembs[:, m],
                                         start=False, stop=(m == IC - 1))
                    last.then_inc(b["y"], 1)
            pipeline(pe, T, 4, step_b)

            pe.wait_ge(ld_cw, 48)
            pe.wait_ge(b["x"], T)

            def step_c(t, q, live):
                A0, A1, A2 = (k in live for k in range(3))
                if A1:
                    s, r = t - 1, 1 - q
                    pe.wait_ge(c["k1"], s + 1)
                    wait(pe, c["kvms"], s)
                    for k in range(KC):
                        last = pe.matmul(banks[2][:, k * D:(k + 1) * D], k1[:, r, k * P:(k + 1) * P],
                                         kvb[:, r, D:2 * D], start=True, stop=True)
                    last.then_inc(c["kvm"], 1)
                    wait(pe, c["den"], s)
                    pe.matmul(banks[3][:, 0:D], ones[:, :], k1[:, r], start=True, stop=True).then_inc(c["ks"], 1)
                    pe.wait_ge(c["q1"], s + 1)
                    wait(pe, c["qTs"], s)
                    transpose2(banks[5], q1[:, r], c["qT"])
                if A0:
                    pe.wait_ge(c["xn"], t + 1)
                    wait(pe, c["xTs"], t)
                    transpose2(banks[0], xn[:, q], c["xT"])
                    pe.wait_ge(ld_cc[q], loads(t, q))
                    wait(pe, c["kvb"], t)
                    for k in range(KC):
                        last = pe.matmul(banks[1][:], ctxb[:, q, k], wkvs[:, k], start=(k == 0), stop=(k == KC - 1))
                    last.then_inc(c["kv"], 1)
                if A2:
                    s = t - 2
                    pe.wait_ge(c["ao"], s + 1)
                    wait(pe, c["r"], s)
                    transpose2(banks[7][:, D:2 * D], ao[:, q], c["aoT"])
                if A0:
                    pe.wait_ge(c["xTs"], t + 1)
                    wait(pe, c["qb"], t)
                    for k in range(KC):
                        last = pe.matmul(banks[4][:, 0:D], xT[:, q, k], wqcs[:, k], start=(k == 0), stop=(k == KC - 1))
                    last.then_inc(c["q"], 1)
                if A2:
                    pe.wait_ge(c["aoTs"], s + 1)
                    for k in range(KC):
                        last = pe.matmul(banks[7][:, 0:D], aoTs[:, q, k], wocs[:, k], start=(k == 0), stop=(k == KC - 1))
                    last.then_inc(c["oo"], 1)
                if A1:
                    s, r = t - 1, 1 - q
                    pe.wait_ge(c["kvms"], s + 1)
                    pe.wait_ge(c["qTs"], s + 1)
                    wait(pe, c["ao"], s)
                    for k in range(KC):
                        last = pe.matmul(banks[6][:, 0:D], q1T[:, r, k], kvs[:, r, k], start=(k == 0), stop=(k == KC - 1))
                    last.then_inc(c["num"], 1)
            pipeline(pe, T, 3, step_c)

            def step_d(t, q, live):
                if 0 in live:
                    pe.wait_ge(d["xn"], t + 1)
                    wait(pe, d["xTs"], t)
                    transpose2(banks[0], xn[:, q], d["xT"])
                if 1 in live:
                    s, r = t - 1, 1 - q
                    pe.wait_ge(d["xTs"], s + 1)
                    wait(pe, d["lgs"], s)
                    for k in range(KC):
                        last = pe.matmul(banks[1][:, 0:E], xT[:, r, k], wgates[:, k], start=(k == 0), stop=(k == KC - 1))
                    last.then_inc(d["lg"], 1)
            pipeline(pe, T, 2, step_d)
            pe.wait_ge(d["oh"], 1)
            pe.matmul(banks[5][:, 0:E], ones[:, :], onehot_sum, start=True, stop=True).then_inc(d["cnt"], 1)
            pe.matmul(banks[4][:, 0:T * E], below[:, :], onehot.rearrange("p e t -> p (e t)"), start=True, stop=False)
            pe.matmul(banks[4][:, 0:T * E], ones[:, :], before.rearrange("p e t -> p (e t)"), start=False, stop=True)\
              .then_inc(d["rank"], 1)

            pe.wait_ge(d["sei"], 1)
            pe.wait_ge(d["pli"], 1)
            pe.wait_ge(d["ld_w1"], 16 * E)
            pe.wait_ge(d["ld_w2"], 16 * E)
            pe.wait_ge(d["ld_b"], 32)

            def step_f(t, q, live):
                S0, S1, S2 = (k in live for k in range(3))
                if S1:
                    s, r = t - 1, 1 - q
                    e = pe.value_load(slot_expert[0:1, bass.ds(s, 1)], min_val=0, max_val=E - 1)
                    pe.wait_ge(f["xTs"], s + 1)
                    wait(pe, f["hs"], s)
                    for g in range(2):
                        for k in range(KC):
                            last = pe.matmul(banks[2 + g], xT[:, r, k],
                                             w1s[:, bass.ds(e, 1), k, g * BANK:(g + 1) * BANK].rearrange("p a n -> p (a n)"),
                                             start=(k == 0), stop=(k == KC - 1))
                    last.then_inc(f["h"], 1)
                if S0:
                    pe.wait_ge(f["xn"], t + 1)
                    wait(pe, f["xTs"], t)
                    transpose2(banks[0], xn[:, q], f["xT"])
                if S2:
                    s = t - 2
                    e = pe.value_load(slot_expert[0:1, bass.ds(s, 1)], min_val=0, max_val=E - 1)
                    wait(pe, f["yo"], s)
                    pe.matmul(banks[6][:, 0:D], ones[0:1, :], b2s[0:1, bass.ds(e * D, D)], start=True, stop=False)
                    for m in range(IC):
                        if m % 4 == 0:
                            pe.wait_ge(f["hTa"], 2 * s + m // 4 + 1)
                        last = pe.matmul(banks[6][:, 0:D], hTd[:, q, m * P:(m + 1) * P],
                                         w2s[:, bass.ds(e, 1), m].rearrange("p a n -> p (a n)"),
                                         start=False, stop=(m == IC - 1))
                    last.then_inc(f["y"], 1)
                if S1:
                    s = t - 1
                    pe.wait_ge(f["hs"], s + 1)
                    wait(pe, f["hTa"], 2 * s)
                    for g in range(2):
                        for m in range(4):
                            last = pe.transpose(banks[4 + g][:, m * P:(m + 1) * P],
                                                h_pre[:, (4 * g + m) * P:(4 * g + m + 1) * P], ident[:, :])
                        last.then_inc(f["hT"], 1)
            pipeline(pe, SLOTS, 3, step_f)



def kernel(**inputs):
    import numpy as np
    import concourse.bacc as bacc
    from concourse.bass_utils import run_bass_kernel_spmd as run

    v = {k: np.asarray(a) for k, a in inputs.items()}

    def chunks(w):
        return w.reshape(-1, P, w.shape[-1]).transpose(1, 0, 2)

    x, context = v["x"], v["ctx_1024"]
    T, _, D = x.shape
    w1, w2 = v["L1_ffn_W1"], v["L1_ffn_W2"]
    E = w1.shape[0]
    keys = v["L0_ffn_keys"]
    arrays = {
        "x": x,
        "ctxT": context.transpose(0, 2, 1).reshape(T, -1, P, P).transpose(0, 2, 1, 3),
        "rows": np.concatenate([v[n].reshape(-1) for n in (
            "L0_xattn_b", "L1_xattn_bk", "L1_xattn_bv", "L1_xattn_bq", "L1_xattn_bo", "L1_xattn_gamma",
            "L1_xattn_beta", "L1_ffn_b_gate", "g_xattn", "g_ffn")])[None],
        "cols": v["L0_xattn_b"].reshape(-1, P).T,
        "w0": chunks(v["L0_xattn_W"].T),
        "wup": chunks(v["L0_ffn_W_up"].T),
        "wdn": chunks(v["L0_ffn_W_down"].T),
        "wq": chunks(v["L0_ffn_W_q"]),
        "keys": chunks(keys.transpose(2, 0, 3, 1).reshape(-1, keys.shape[1])),
        "demb": chunks(v["L0_ffn_down_embed"].T),
        "uemb": chunks(v["L0_ffn_up_embed"]),
        "wkv": chunks(np.concatenate([v["L1_xattn_Wk"].T, v["L1_xattn_Wv"].T], axis=1)),
        "wqc": chunks(v["L1_xattn_Wq"].T),
        "woc": chunks(v["L1_xattn_Wo"].T),
        "wgate": chunks(v["L1_ffn_w_gate"]),
        "w1": w1.reshape(E, -1, P, w1.shape[2]).transpose(2, 0, 1, 3),
        "w2": w2.reshape(E, -1, P, D).transpose(2, 0, 1, 3),
        "b1": v["L1_ffn_b1"].reshape(E, -1, P).transpose(2, 0, 1),
        "b2": v["L1_ffn_b2"].reshape(1, -1),
    }
    arrays = {f"in_{n}": np.ascontiguousarray(a) for n, a in arrays.items()}
    nc = bacc.Bacc("TRN2", target_bir_lowering=False, num_devices=1)
    args = [nc.dram_tensor(n, a.shape, mybir.dt.from_np(a.dtype), kind="ExternalInput").ap()
            for n, a in arrays.items()]
    out = nc.dram_tensor("out", x.shape, F32, kind="ExternalOutput").ap()
    build(nc, *args, out)
    r = run(nc, [arrays], core_ids=[0])
    return r.results[0]["out"]
```

```python
from contextlib import ExitStack

import concourse.bass as bass
from concourse import mybir

F32 = mybir.dt.float32
I32 = mybir.dt.int32
ALU = mybir.AluOpType
ACT = mybir.ActivationFunctionType
AX = mybir.AxisListType

SCRATCH = 8704
P = 128
BANK = 512
LAG_B, LAG_C = 0, 1
EPS_LN = 1e-5
EPS_DENOM = 1e-6
FAR = 4096.0


def pipeline(eng, tiles, depth, step, peel=0, then=None):
    first = max(depth + depth % 2, peel)
    for t in range(first):
        step(t, t % 2, [k for k in range(depth) if k <= t])
    while True:
        loops = (tiles - first) // 2
        with eng.Fori(0, loops) as i:
            for u in range(2):
                step(2 * i + (first + u), (first + u) % 2, list(range(depth)))
        last = range(first + 2 * loops, tiles + depth - 1)
        drain = [(step, t, [k for k in range(depth) if 0 <= t - k < tiles]) for t in last]
        if then is None:
            for run, t, live in drain:
                run(t, t % 2, live)
            return
        depth, step, lag, then = then
        first = depth + depth % 2
        for n in range(max(len(drain), lag + first)):
            if n < len(drain):
                run, t, live = drain[n]
                run(t, t % 2, live)
            if 0 <= n - lag < first:
                t = n - lag
                step(t, t % 2, [k for k in range(depth) if k <= t])


def at_most(value, most):
    return min(value, most) if isinstance(value, int) else value


def wait(eng, sem, value):
    if isinstance(value, int) and value <= 0:
        return
    eng.wait_ge(sem, value)


def build(nc, x, ctxT, rows, cols, w0, wup, wdn, wq, keys, demb, uemb, wkv, wqc, woc,
          wgate, w1, w2, b1, b2, out):
    T, _, D = x.shape
    KC = D // P
    IC = wdn.shape[1]
    HID = IC * P
    HEADS, NK, TOP = 4, 64, 8
    NX = HID // NK
    PAIRS = TOP * TOP
    GRID = HID + PAIRS
    E = w1.shape[1]

    SLOTS = T + E - 1

    with ExitStack() as ctx:
        sorted_rows = nc.dram_tensor("sorted_rows", (SLOTS * P, D + 2), F32, kind="Internal").ap()

        def sb(name, shape, dt=F32):
            return ctx.enter_context(nc.sbuf_tensor(name, shape, dt))

        def sem(name):
            return ctx.enter_context(nc.semaphore(name))

        banks = [ctx.enter_context(nc.psum_tensor(f"bank{i}", [P, BANK], F32)) for i in (0, 1)]
        table_dots = ctx.enter_context(nc.psum_tensor("table_dots", [P, HID], F32))
        banks += [None, None]
        banks += [ctx.enter_context(nc.psum_tensor(f"bank{i}", [P, BANK], F32)) for i in (4, 5, 6, 7)]
        banks[2] = table_dots[:, 0:BANK]
        banks[3] = table_dots[:, BANK:HID]

        ROW = D + 2
        xs = sb("xs", [P, T, ROW])
        ctxb = sb("ctxb", [P, 2, KC, P])
        NR = rows.shape[1]
        rowb = sb("rowb", [P, NR])
        colb = sb("colb", [P, 2 * KC])
        gate = sb("gate", [P, 4])
        ident = sb("ident", [P, P])
        ones = sb("ones", [P, P])
        neg_half = sb("neg_half", [P, 1])
        wkvs = sb("wkvs", [P, KC, 2 * D])
        wqcs = sb("wqcs", [P, KC, D])
        wocs = sb("wocs", [P, KC, D])

        region1 = sb("region1", [P, E * KC * HID])
        region2 = sb("region2", [P, max(E * IC * D, 4 * HEADS * GRID)])

        region3 = sb("region3", [P, SCRATCH])

        def carve(region, at, *shape):
            n = 1
            for s in shape:
                n *= s
            names = " ".join("abcd"[:len(shape)])
            v = region[:, at:at + n]
            if len(shape) > 1:
                v = v.rearrange(f"p ({names}) -> p {names}", **dict(zip("abcd", shape)))
            return v, at + n

        at = 0
        wups, at = carve(region1, at, KC, HID)
        wdns, at = carve(region1, at, IC, D)
        dembs, at = carve(region1, at, KC, HID)
        uembs, at = carve(region1, at, IC, D)
        wqs, at = carve(region1, at, 4, D)
        keyb, at = carve(region1, at, 4, P)
        simw, at = carve(region1, at, KC, BANK)
        at2 = 0
        grid, at2 = carve(region2, at2, 2, HEADS, GRID)
        picked, at2 = carve(region2, at2, 2, HEADS, GRID)

        stats = sb("stats", [P, 2, 6])
        mv = sb("mv", [P, 2, 2])
        ve = sb("ve", [P, 2])
        rstd = sb("rstd", [P, 2])
        xn = sb("xn", [P, 2, D])
        xT = sb("xT", [P, 2, KC, P])

        at3 = 0
        w0s, at3 = carve(region3, at3, KC, D)
        tqs, at3 = carve(region3, at3, 2, KC, P)
        vws, at3 = carve(region3, at3, 2, D)
        prob, at3 = carve(region3, at3, 2, P)
        probT, at3 = carve(region3, at3, 2, P)
        u_buf, at3 = carve(region3, at3, 2, D)
        r_buf, at3 = carve(region3, at3, 2, D)
        nmax = sb("nmax", [P, 2])
        esum = sb("esum", [P, 2])
        rsum = sb("rsum", [P, 2])
        scoresA = banks[3:5]
        outA = banks[6:8]

        simS, at = carve(region1, at, 2, BANK)
        hT, at = carve(region1, at, 2, HID)
        pickT, at = carve(region1, at, HID)
        top_x, at = carve(region1, at, 2, HEADS, TOP)
        top_y, at = carve(region1, at, 2, HEADS, TOP)
        top_c, at = carve(region1, at, 2, HEADS, TOP)
        cand, _ = carve(region3, SCRATCH - 2 * HEADS * PAIRS, 2, HEADS, PAIRS)
        top, at = carve(region1, at, 2, HEADS, TOP)
        nm = sb("nm", [P, 2, HEADS])
        d8, at = carve(region1, at, 2, HEADS * TOP)
        e8, at = carve(region1, at, 2, HEADS * TOP)
        zsum = sb("zsum", [P, 2, HEADS])
        rz = sb("rz", [P, 2, HEADS])
        tail = sb("tail", [P, 2])
        far, at = carve(region1, at, ROW)
        assert at <= E * KC * HID

        at3 = 0
        audio, at3 = carve(region3, at3, T, D)
        v_c, at3 = carve(region3, at3, 2, D)
        k1, at3 = carve(region3, at3, 2, D)
        kvs, at3 = carve(region3, at3, 2, KC, D)
        q1T, at3 = carve(region3, at3, 2, KC, P)
        den, at3 = carve(region3, at3, 2, KC, P)
        res, at3 = carve(region3, at3, 2, D)
        assert at3 <= SCRATCH
        kexp, at2 = carve(region2, E * IC * D, 2, D)
        qexp, at2 = carve(region2, at2, KC, P)
        xT3, at2 = carve(region2, at2, KC, P)
        assert at2 <= max(E * IC * D, 4 * HEADS * GRID)
        ksum = sb("ksum", [P, 2, KC])
        at3 = 0
        w1s = region1[:, :].rearrange("p (e k m) -> p e k m", e=E, k=KC)
        w2s = region2[:, 0:E * IC * D].rearrange("p (e m d) -> p e m d", e=E, m=IC)
        shifted, at3 = carve(region3, at3, T, E)
        onehot, at3 = carve(region3, at3, E, T)
        before, at3 = carve(region3, at3, E, T)
        places, at3 = carve(region3, at3, E, T)
        ranked, at3 = carve(region3, at3, T, E)
        fits, at3 = carve(region3, at3, E, T)
        slot_cmp, at3 = carve(region3, at3, SLOTS, E)
        top_logit, at3 = carve(region3, at3, T)
        exp_sum, at3 = carve(region3, at3, T)
        first_best, at3 = carve(region3, at3, T)
        place_f, at3 = carve(region3, at3, T)
        onehot_sum, at3 = carve(region3, at3, E)
        counts, at3 = carve(region3, at3, E)
        slots_of, at3 = carve(region3, at3, E)
        slot_end, at3 = carve(region3, at3, E)
        row_base, at3 = carve(region3, at3, E)
        slot_e, at3 = carve(region3, at3, SLOTS)
        b1s, at3 = carve(region3, at3, E, IC)
        b2s, at3 = carve(region3, at3, E, D)
        rows_in, at3 = carve(region3, at3, 2, ROW)
        h_pre, at3 = carve(region3, at3, HID)
        hTd, at3 = carve(region3, at3, 2, HID)
        rows_out, at3 = carve(region3, at3, 2, D)
        rows_late, at3 = carve(region3, at3, 2, ROW)
        below, at3 = carve(region3, at3, P)
        assert at3 <= SCRATCH
        wgates = sb("wgates", [P, KC, E])
        logits = sb("logits", [P, T, E])
        place = sb("place", [P, T], I32)
        slot_expert = sb("slot_expert", [1, SLOTS], I32)
        token = sb("token", [P, 2], I32)
        same_expert = sb("same_expert", [P, E * T])
        down = sb("down", [P, E])
        thr = sb("thr", [P, T])
        slot_no = sb("slot_no", [P, SLOTS])
        ints = sb("ints", [P, T + E + T + SLOTS], I32)

        stats2 = sb("stats2", [P, 2, 6])
        mv2 = sb("mv2", [P, 2, 2])
        ve2 = sb("ve2", [P, 2])
        rstd2 = sb("rstd2", [P, 2])
        stats3 = sb("stats3", [P, 2, 6])
        mv3 = sb("mv3", [P, 2, 2])
        ve3 = sb("ve3", [P, 2])
        rstd3 = sb("rstd3", [P, 2])
        xn3 = sb("xn3", [P, 2, D])

        col = 0

        def row(n):
            nonlocal col
            col += n
            return rowb[:, col - n:col]

        r_b0, r_bk, r_bv, r_bo, r_gamma, r_beta = (row(D) for _ in range(6))
        r_bgate, r_gates = row(E), row(4)
        assert col == NR

        waits_taken = sem("waits_taken")

        def held(eng, s, value):
            if isinstance(value, int) and value <= 0:
                return
            eng.wait_ge(s, value)
            eng.sem_inc(waits_taken, 1)

        ld_x = [sem(f"ld_x{q}") for q in range(2)]
        ld_ca = [sem(f"ld_ca{q}") for q in range(2)]
        ld_cc = [sem(f"ld_cc{q}") for q in range(2)]
        ld_a = sem("ld_a")
        ld_w0 = sem("ld_w0")
        ld_keys = sem("ld_keys")
        ld_b = sem("ld_b")
        ld_cw = sem("ld_cw")
        keyb_zero = sem("keyb_zero")
        consts = sem("consts")
        ident_zero = sem("ident_zero")
        gates_done = sem("gates_done")
        gated = sem("gated")
        simw_mm = sem("simw_mm")
        simw_done = sem("simw_done")

        def sems(prefix, names):
            return {n: sem(f"{prefix}_{n}") for n in names.split()}

        a = sems("a", "ve rstd xn xT xTs tq tqs vw vws sc mx ex ri pt pts o u r x")
        b = sems("b", "ve rstd xn xT xTs sim simS mx cand ext t8 nm d8 e8 z rz grid dots "
                      "pick pickx ex zz act sum1 sum2 tail last st sts up act2 y x")
        c = sems("c", "ve rstd xn ab xT xTs kv vb kex k1 kvm kvms qT qex q1 den deni "
                      "num ao oo r ve2 rstd2 n ga be x")
        d = sems("d", "below ve rstd xn xT xTs lg lgs sh ex oh same cnt rank pli sei scat iota cvt fill ld_b ld_w")
        routing = sem("routing")
        f = sems("f", "ve rstd xn xT xTs h hs hT hTa y yb yo tok")
        ln2_bn, ln2_ag = sem("ln2_bn"), sem("ln2_ag")
        ln3_bn, ln3_ag = sem("ln3_bn"), sem("ln3_ag")
        ln_bn, ln_ag = sem("ln_bn"), sem("ln_ag")
        ld_row = [sem(f"ld_row{q}") for q in range(2)]
        ld_late = [sem(f"ld_late{q}") for q in range(2)]
        sent = [sem(f"sent{q}") for q in range(2)]

        def ln_stats(dve, src, q, n, v):
            dve.bn_stats(stats[:, q, :], src).then_inc(ln_bn, 1)
            held(dve, ln_bn, n + 1)
            dve.bn_aggr(mv[:, q, :], stats[:, q, :]).then_inc(ln_ag, 1)
            dve.wait_ge(ln_ag, n + 1)
            dve.tensor_scalar(ve[:, q:q + 1], mv[:, q, 1:2], EPS_LN, None, ALU.add).then_inc(v, 1)

        def ln_apply(dve, dst, src, q, s, rs, done):
            dve.wait_ge(rs, s + 1)
            dve.tensor_scalar(dst, src, mv[:, q, 0:1], rstd[:, q:q + 1], ALU.subtract, ALU.mult)\
               .then_inc(done, 1)

        def ln_rstd(pool, q, s, v, rs):
            pool.wait_ge(v, s + 1)
            pool.tensor_tensor(rstd[:, q:q + 1], ve[:, q:q + 1], neg_half[:, :], ALU.pow).then_inc(rs, 1)

        def tile_of(t):
            return bass.ds(t, 1)

        def loads(t, q):
            return 8 * (t - q) + 16

        def x_at(t):
            return xs[:, tile_of(t), 0:D].rearrange("p a d -> p (a d)")

        block = ctx.enter_context(nc.Block())

        @block.sync
        def _(sp):
            def load_a(t, q, live):
                wait(sp, ln_bn, t - 1)
                sp.dma_start(x_at(t), x[tile_of(t)].rearrange("a p d -> (a p) d")).then_inc(ld_x[q], 16)
                wait(sp, a["vw"], t - 1)
                sp.dma_start(ctxb[:, q], ctxT[tile_of(t)].rearrange("a p k n -> (a p) k n")).then_inc(ld_ca[q], 16)
                if isinstance(t, int) and t == 0:
                    sp.dma_start(w0s, w0).then_inc(ld_w0, 16)
                    sp.dma_start(colb[:], cols).then_inc(ld_w0, 16)
                if isinstance(t, int) and t == 1:
                    sp.dma_start(rowb[:], rows.partition_broadcast(P).rearrange("p a n -> p (a n)")).then_inc(ld_a, 16)
                    sp.dma_start(wgates[:], wgate).then_inc(ld_a, 16)
            pipeline(sp, T, 2, lambda t, q, live: load_a(t, q, live) if 0 in live else None)

            sp.wait_ge(d["cvt"], 1)
            for n in range(SLOTS):
                sp.dma_start(sorted_rows[n * P:(n + 1) * P, :], far).then_inc(d["fill"], 16)

            def load_c(t, q, live):
                if 0 in live:
                    if isinstance(t, int):
                        sp.wait_ge(a["vw"], T)
                    wait(sp, c["kv"], t - 1)
                    sp.dma_start(ctxb[:, q], ctxT[tile_of(t)].rearrange("a p k n -> (a p) k n")).then_inc(ld_cc[q], 16)
                if 1 in live:
                    if isinstance(t, int):
                        sp.wait_ge(b["x"], T)
                        sp.wait_ge(d["fill"], 16 * SLOTS)
                    for dst, src, n in ((w1s, w1, E * KC // T), (w2s, w2, E * IC // T)):
                        sp.dma_start(dst.rearrange("p e k m -> p (e k) m")[:, bass.ds((t - 1) * n, n)],
                                     src.rearrange("p e k m -> p (e k) m")[:, bass.ds((t - 1) * n, n)])\
                          .then_inc(d["ld_w"], 16)
            assert E * KC % T == 0
            pipeline(sp, T, 2, load_c)

            sp.wait_ge(d["scat"], 16 * T)

            def load_rows(t, q, live):
                if 0 in live:
                    wait(sp, f["xn"], t - 1)
                    sp.dma_start(rows_in[:, q], sorted_rows[bass.ds(t * P, P), :]).then_inc(ld_row[q], 16)
                if 1 in live:
                    s, r = t - 1, 1 - q
                    wait(sp, f["yo"], s - 1)
                    sp.dma_start(rows_late[:, r], sorted_rows[bass.ds(s * P, P), :]).then_inc(ld_late[r], 16)
            pipeline(sp, SLOTS, 2, load_rows, peel=4)

        @block.gpsimd
        def _(pool):
            pool.memset(keyb, 0.0).then_inc(keyb_zero, 1)
            pool.memset(far, FAR).then_inc(d["cvt"], 1)
            pool.memset(ident[:], 0.0).then_inc(ident_zero, 1)
            pool.memset(ones[:], 1.0).then_inc(consts, 1)
            pool.memset(neg_half[:], -0.5).then_inc(consts, 1)
            pool.wait_ge(ident_zero, 1)
            pool.affine_select(out=ident[:], in_=ident[:], compare_op=ALU.not_equal, fill=1.0, base=0,
                               pattern=[[-1, P]], channel_multiplier=1).then_inc(consts, 1)
            n = 0
            for count, first, step, channel in ((E, E, -1, 0), (T, 0, P, 0), (SLOTS, 0, 1, 0), (T, 0, P, 1)):
                pool.iota(ints[:, n:n + count], pattern=[[step, count]], base=first,
                          channel_multiplier=channel).then_inc(d["iota"], 1)
                n += count
            pool.wait_ge(consts, 3)

            def step_a(t, q, live):
                if 0 in live:
                    ln_rstd(pool, q, t, a["ve"], a["rstd"])

            def grids(s, r):
                pool.wait_ge(b["simS"], s + 1)
                wait(pool, b["zz"], HEADS * (s - 1))
                for h in range(HEADS):
                    pool.tensor_tensor(
                        grid[:, r, h, 0:HID].rearrange("p (a b) -> p a b", b=NK),
                        simS[:, r, h * NK:h * NK + NX].unsqueeze(2).to_broadcast([P, NX, NK]),
                        simS[:, r, BANK // 2 + h * NK:BANK // 2 + (h + 1) * NK].unsqueeze(1).to_broadcast([P, NX, NK]),
                        ALU.add).then_inc(b["grid"], 1)

            def sum_heads(s, q):
                for h in (0, 2):
                    pool.wait_ge(b["act"], HEADS * s + h + 2)
                    pool.tensor_tensor(picked[:, q, h], picked[:, q, h], picked[:, q, h + 1], ALU.add)\
                        .then_inc(b["sum1"], 1)
                pool.wait_ge(b["sum1"], 2 * s + 2)
                pool.tensor_tensor(picked[:, q, 0], picked[:, q, 0], picked[:, q, 2], ALU.add)\
                    .then_inc(b["sum2"], 1)

            def step_b(t, q, live):
                if 0 in live:
                    ln_rstd(pool, q, t, b["ve"], b["rstd"])
                if 3 in live:
                    sum_heads(t - 3, 1 - q)
                if 1 in live:
                    grids(t - 1, 1 - q)

            def step_c(t, q, live):
                if 0 in live:
                    ln_rstd(pool, q, t, c["ve"], c["rstd"])
                if 6 in live:
                    pool.wait_ge(d["ve"], t - 5)
                    pool.tensor_tensor(rstd3[:, q:q + 1], ve3[:, q:q + 1], neg_half[:, :], ALU.pow)\
                        .then_inc(d["rstd"], 1)
                if 5 in live:
                    s, r = t - 5, 1 - q
                    if isinstance(t, int):
                        pool.wait_ge(gated, 2)
                    pool.wait_ge(c["n"], s + 1)
                    pool.tensor_tensor(res[:, r], res[:, r], r_gamma, ALU.mult).then_inc(c["ga"], 1)
                    pool.wait_ge(c["ga"], s + 1)
                    pool.tensor_tensor(res[:, r], res[:, r], r_beta, ALU.add).then_inc(c["be"], 1)
                    pool.wait_ge(c["be"], s + 1)
                    pool.tensor_tensor(x_at(s), x_at(s), res[:, r], ALU.add).then_inc(c["x"], 1)
                if 0 in live:
                    pool.wait_ge(c["xn"], t + 1)
                    pool.tensor_tensor(audio[:, tile_of(t)].rearrange("p a d -> p (a d)"), xn[:, q], r_bo, ALU.add)\
                        .then_inc(c["ab"], 1)
                if 4 in live:
                    pool.wait_ge(c["ve2"], t - 3)
                    pool.tensor_tensor(rstd2[:, q:q + 1], ve2[:, q:q + 1], neg_half[:, :], ALU.pow)\
                        .then_inc(c["rstd2"], 1)
            pipeline(pool, T, 5, step_a, then=(5, step_b, LAG_B, (8, step_c, LAG_C, None)))

            pool.wait_ge(d["lgs"], T)
            pool.affine_select(out=below, in_=ones[:], compare_op=ALU.is_gt, fill=0.0, base=0,
                               pattern=[[1, P]], channel_multiplier=-1).then_inc(d["below"], 1)
            pool.wait_ge(d["fill"], 16 * SLOTS)
            pool.wait_ge(d["pli"], 1)
            for t in range(T):
                pool.indirect_dma_start(out=sorted_rows, out_offset=bass.IndirectOffsetOnAxis(ap=place[:, t:t + 1], axis=0),
                                        in_=xs[:, t, :], in_offset=None).then_inc(d["scat"], 16)

            def step_f(t, q, live):
                if 0 in live:
                    ln_rstd(pool, q, t, f["ve"], f["rstd"])
                if 2 in live:
                    held(pool, f["yo"], t - 1)
                    pool.indirect_dma_start(
                        out=out.rearrange("t p d -> (t p) d"),
                        out_offset=bass.IndirectOffsetOnAxis(ap=token[:, q:q + 1], axis=0),
                        in_=rows_out[:, q], in_offset=None, bounds_check=T * P - 1, oob_is_err=False)\
                        .then_inc(sent[q], 16)
            pipeline(pool, SLOTS, 3, step_f)
            pool.wait_ge(sent[0], 16 * ((SLOTS + 1) // 2))
            pool.wait_ge(sent[1], 16 * (SLOTS // 2))

        @block.vector
        def _(dve):
            def step_a(t, q, live):
                if isinstance(t, int) and t == 3:
                    dve.wait_ge(ld_a, 32)
                    dve.wait_ge(gates_done, 1)
                    for r in (r_gamma, r_beta):
                        dve.tensor_scalar(r, r, gate[:, 1:2], None, ALU.mult).then_inc(gated, 1)
                    dve.wait_ge(d["iota"], 4)
                    dve.memset(same_expert[:, :], 1.0).then_inc(d["same"], 1)
                    dve.tensor_copy(down[:, :], ints[:, 0:E])
                    dve.wait_ge(d["same"], 1)
                    dve.memset(same_expert[:, :].rearrange("p (e t) -> p e t", e=E)[:, :, 0], 0.0)
                    dve.tensor_copy(thr[:, :], ints[:, E:E + T])
                    dve.tensor_copy(slot_no[:, :], ints[:, E + T:E + T + SLOTS])
                    dve.tensor_copy(xs[:, :, D + 1], ints[:, E + T + SLOTS:E + 2 * T + SLOTS]).then_inc(d["cvt"], 1)
                if 3 in live:
                    s, r = t - 3, 1 - q
                    dve.wait_ge(a["ex"], s + 1)
                    dve.reciprocal(rsum[:, r:r + 1], esum[:, r:r + 1]).then_inc(a["ri"], 1)
                if 0 in live:
                    dve.wait_ge(ld_x[q], loads(t, q))
                    ln_stats(dve, x_at(t), q, t, a["ve"])
                if 4 in live:
                    s = t - 4
                    dve.wait_ge(a["o"], s + 1)
                    held(dve, a["ri"], s + 1)
                    dve.scalar_tensor_tensor(out=u_buf[:, q], in0=outA[q][:, 0:D], scalar=rsum[:, q:q + 1],
                                             in1=r_b0, op0=ALU.mult, op1=ALU.add).then_inc(a["u"], 1)
                if 0 in live:
                    ln_apply(dve, xn[:, q], x_at(t), q, t, a["rstd"], a["xn"])
                if 4 in live:
                    dve.wait_ge(a["u"], s + 1)
                    dve.tensor_scalar(r_buf[:, q], u_buf[:, q], 0.0, gate[:, 0:1], ALU.max, ALU.mult)\
                       .then_inc(a["r"], 1)
                if 2 in live:
                    dve.wait_ge(a["sc"], t - 1)
                    dve.tensor_reduce(nmax[:, q:q + 1], scoresA[q][:, 0:P], AX.X, ALU.max, negate=True)\
                        .then_inc(a["mx"], 1)
                if 4 in live:
                    dve.wait_ge(a["r"], s + 1)
                    dve.tensor_tensor(x_at(s), x_at(s), r_buf[:, q], ALU.add).then_inc(a["x"], 1)
                if 1 in live:
                    dve.wait_ge(a["xT"], t)
                    dve.tensor_copy(xT[:, 1 - q].rearrange("p k n -> p (k n)"), banks[0][:, 0:D]).then_inc(a["xTs"], 1)
            def pick(s, r, h):
                if h == 0:
                    dve.wait_ge(b["dots"], s + 1)
                    wait(dve, b["st"], 2 * (s - 1))
                dve.wait_ge(b["grid"], HEADS * s + h + 1)
                least = top[:, r, h, TOP - 1:TOP]
                dve.scalar_tensor_tensor(out=picked[:, r, h, 0:HID], in0=grid[:, r, h, 0:HID], scalar=least,
                                         in1=table_dots[:, :], op0=ALU.is_ge, op1=ALU.mult).then_inc(b["pick"], 1)
                dve.scalar_tensor_tensor(out=picked[:, r, h, HID:GRID], in0=grid[:, r, h, HID:GRID], scalar=least,
                                         in1=table_dots[:, HID - 1:HID].to_broadcast([P, PAIRS]),
                                         op0=ALU.is_ge, op1=ALU.mult).then_inc(b["pick"], 1)

            def weigh(s, r, h):
                dve.wait_ge(b["ex"], HEADS * s + h + 1)
                dve.tensor_tensor(picked[:, r, h], picked[:, r, h], grid[:, r, h], ALU.mult).then_inc(b["zz"], 1)

            def step_b(t, q, live):
                f, p, s, r = t - 1, t - 2, t - 3, 1 - q
                L, F, B1, B2, FIN = (k in live for k in range(5))
                if FIN:
                    dve.wait_ge(b["y"], t - 3)
                    dve.scalar_tensor_tensor(out=x_at(t - 4), in0=banks[6][:, 0:D], scalar=gate[:, 2:3],
                                             in1=x_at(t - 4), op0=ALU.mult, op1=ALU.add).then_inc(b["x"], 1)
                if L:
                    dve.wait_ge(a["x"], t + 1)
                    ln_stats(dve, x_at(t), q, t + T, b["ve"])
                if B1:
                    pick(p, q, 0)
                if L:
                    if isinstance(t, int) and t < 2:
                        dve.wait_ge(a["xT"], T)
                    wait(dve, b["xT"], t - 1)
                    ln_apply(dve, xn[:, q], x_at(t), q, t, b["rstd"], b["xn"])
                if B1:
                    dve.wait_ge(b["e8"], p + 1)
                    dve.tensor_reduce(zsum[:, q], e8[:, q].rearrange("p (h k) -> p h k", k=TOP), AX.X, ALU.add)\
                       .then_inc(b["z"], 1)
                    pick(p, q, 1)
                    dve.wait_ge(b["z"], p + 1)
                    dve.reciprocal(rz[:, q], zsum[:, q]).then_inc(b["rz"], 1)
                    pick(p, q, 2)
                    pick(p, q, 3)
                    weigh(p, q, 0)
                if B2:
                    dve.wait_ge(b["sum2"], s + 1)
                    dve.tensor_reduce(tail[:, r:r + 1], picked[:, r, 0, HID - 1:GRID], AX.X, ALU.add)\
                       .then_inc(b["tail"], 1)
                if B1:
                    weigh(p, q, 1)
                if B2:
                    dve.wait_ge(b["tail"], s + 1)
                    dve.tensor_copy(picked[:, r, 0, HID - 1:HID], tail[:, r:r + 1]).then_inc(b["last"], 1)
                if F:
                    held(dve, b["simS"], f + 1)
                    for h in range(HEADS):
                        first, second = h * NK, BANK // 2 + h * NK
                        dve.max(top_x[:, r, h], simS[:, r, first:first + NK])
                        dve.max(top_y[:, r, h], simS[:, r, second:second + NK])
                        last = dve.max(top_c[:, r, h], simS[:, r, first + NX:first + NK])
                    last.then_inc(b["mx"], 1)
                if B1:
                    weigh(p, q, 2)
                if F:
                    dve.wait_ge(b["mx"], f + 1)
                    wait(dve, b["ex"], HEADS * (f - 1))
                    y = top_y[:, r].unsqueeze(2).to_broadcast([P, HEADS, TOP, TOP])
                    dve.tensor_tensor(cand[:, r].rearrange("p h (i j) -> p h i j", j=TOP),
                                      top_x[:, r].unsqueeze(3).to_broadcast([P, HEADS, TOP, TOP]), y, ALU.add)\
                       .then_inc(b["cand"], 1)
                    dve.tensor_tensor(grid[:, r, :, HID:GRID].rearrange("p h (i j) -> p h i j", j=TOP),
                                      top_c[:, r].unsqueeze(3).to_broadcast([P, HEADS, TOP, TOP]), y, ALU.add)\
                       .then_inc(b["cand"], 1)
                    held(dve, b["cand"], 2 * f + 2)
                    for h in range(HEADS):
                        last = dve.max(top[:, r, h], cand[:, r, h])
                    last.then_inc(b["t8"], 1)
                if B1:
                    weigh(p, q, 3)
                if F:
                    dve.wait_ge(b["t8"], f + 1)
                    dve.tensor_scalar(nm[:, r], top[:, r, :, 0], -1.0, None, ALU.mult).then_inc(b["nm"], 1)
                    wait(dve, b["e8"], f - 1)
                    dve.tensor_tensor(d8[:, r].rearrange("p (h k) -> p h k", k=TOP), top[:, r],
                                      top[:, r, :, 0:1].to_broadcast([P, HEADS, TOP]), ALU.subtract).then_inc(b["d8"], 1)

            def step_c(t, q, live):
                if 2 in live:
                    s = t - 2
                    dve.wait_ge(c["kex"], s + 1)
                    dve.scalar_tensor_tensor(out=k1[:, q], in0=kexp[:, q], scalar=1.0, in1=k1[:, q],
                                             op0=ALU.min, op1=ALU.add).then_inc(c["k1"], 1)
                if 3 in live:
                    s, r = t - 3, 1 - q
                    dve.wait_ge(c["qex"], s + 1)
                    dve.scalar_tensor_tensor(out=q1T[:, r], in0=qexp, scalar=1.0, in1=q1T[:, r],
                                             op0=ALU.min, op1=ALU.add).then_inc(c["q1"], 1)
                    dve.wait_ge(c["q1"], s + 1)
                    dve.wait_ge(c["kvms"], s + 1)
                    wait(dve, c["oo"], s - 1)
                    for k in range(KC):
                        dve.tensor_scalar(den[:, r, k], q1T[:, r, k], ksum[:, r, k:k + 1], EPS_DENOM,
                                          ALU.mult, ALU.add).then_inc(c["den"], 1)
                if 6 in live:
                    dve.wait_ge(c["x"], t - 5)
                    dve.bn_stats(stats3[:, q, :], x_at(t - 6)).then_inc(ln3_bn, 1)
                if 0 in live:
                    dve.wait_ge(b["x"], t + 1)
                    ln_stats(dve, x_at(t), q, t + 2 * T, c["ve"])
                if 6 in live:
                    held(dve, ln3_bn, t - 5)
                    dve.bn_aggr(mv3[:, q, :], stats3[:, q, :]).then_inc(ln3_ag, 1)
                    dve.wait_ge(ln3_ag, t - 5)
                    dve.tensor_scalar(ve3[:, q:q + 1], mv3[:, q, 1:2], EPS_LN, None, ALU.add).then_inc(d["ve"], 1)
                if 3 in live:
                    dve.wait_ge(c["den"], 2 * s + 2)
                    dve.reciprocal(den[:, r], den[:, r]).then_inc(c["deni"], 1)
                if 5 in live:
                    s, r = t - 5, 1 - q
                    dve.wait_ge(c["rstd2"], s + 1)
                    dve.tensor_scalar(res[:, r], res[:, r], mv2[:, r, 0:1], rstd2[:, r:r + 1], ALU.subtract, ALU.mult)\
                       .then_inc(c["n"], 1)
                if 4 in live:
                    s = t - 4
                    dve.wait_ge(c["oo"], s + 1)
                    dve.wait_ge(c["ab"], s + 1)
                    wait(dve, c["x"], s - 1)
                    dve.tensor_tensor(res[:, q], banks[7][:, 0:D], audio[:, tile_of(s)].rearrange("p a d -> p (a d)"),
                                      ALU.add).then_inc(c["r"], 1)
                if 0 in live:
                    if isinstance(t, int) and t < 2:
                        dve.wait_ge(b["xT"], T)
                    wait(dve, c["xT"], t - 1)
                    wait(dve, c["ab"], t - 1)
                    ln_apply(dve, xn[:, q], x_at(t), q, t, c["rstd"], c["xn"])
                if 4 in live:
                    dve.wait_ge(c["r"], s + 1)
                    dve.bn_stats(stats2[:, q, :], res[:, q]).then_inc(ln2_bn, 1)
                if 1 in live:
                    s, r = t - 1, 1 - q
                    dve.wait_ge(c["kv"], s + 1)
                    wait(dve, c["kvm"], 2 * (s - 1))
                    dve.tensor_tensor(v_c[:, r], banks[5][:, 0:D], r_bv, ALU.add).then_inc(c["vb"], 1)
                if 4 in live:
                    s = t - 4
                    held(dve, ln2_bn, s + 1)
                    dve.bn_aggr(mv2[:, q, :], stats2[:, q, :]).then_inc(ln2_ag, 1)
                    dve.wait_ge(ln2_ag, s + 1)
                    dve.tensor_scalar(ve2[:, q:q + 1], mv2[:, q, 1:2], EPS_LN, None, ALU.add).then_inc(c["ve2"], 1)
                if 6 in live:
                    dve.wait_ge(d["rstd"], t - 5)
                    wait(dve, d["xT"], t - 7)
                    dve.tensor_scalar(xn3[:, q], x_at(t - 6), mv3[:, q, 0:1], rstd3[:, q:q + 1],
                                      ALU.subtract, ALU.mult).then_inc(d["xn"], 1)
                if 3 in live:
                    s, r = t - 3, 1 - q
                    dve.wait_ge(c["deni"], s + 1)
                    dve.wait_ge(c["num"], s + 1)
                    dve.tensor_tensor(den[:, r].rearrange("p k n -> p (k n)"), banks[6][:, 0:D],
                                      den[:, r].rearrange("p k n -> p (k n)"), ALU.mult).then_inc(c["ao"], 1)
                if 7 in live:
                    s = t - 7
                    dve.wait_ge(d["lg"], s + 1)
                    dve.tensor_tensor(logits[:, tile_of(s), :].rearrange("p a e -> p (a e)"), banks[7][:, D:D + E],
                                      r_bgate, ALU.add).then_inc(d["lgs"], 1)
            pipeline(dve, T, 5, step_a, then=(5, step_b, LAG_B, (8, step_c, LAG_C, None)))

            links = [0]

            def link(ins):
                links[0] += 1
                ins.then_inc(routing, 1)
                dve.wait_ge(routing, links[0])

            dve.wait_ge(d["lgs"], T)
            link(dve.tensor_reduce(top_logit, logits[:, :, :], AX.X, ALU.max))
            best = top_logit.unsqueeze(2).to_broadcast([P, T, E])
            dve.tensor_tensor(shifted, logits[:, :, :], best, ALU.subtract).then_inc(d["sh"], 1)
            link(dve.tensor_tensor(ranked, logits[:, :, :], best, ALU.is_ge))
            link(dve.tensor_tensor(ranked, ranked, down[:, :].unsqueeze(1).to_broadcast([P, T, E]), ALU.mult))
            link(dve.tensor_reduce(first_best, ranked, AX.X, ALU.max))
            link(dve.tensor_tensor(onehot.rearrange("p e t -> p t e"), ranked,
                                   first_best.unsqueeze(2).to_broadcast([P, T, E]), ALU.is_equal))
            flat = lambda v: v.rearrange("p e t -> p (e t)")
            link(dve.tensor_tensor_scan(flat(before), same_expert[:, :], flat(onehot), 0.0, ALU.mult, ALU.add))
            link(dve.tensor_copy(onehot_sum, before[:, :, T - 1]))
            dve.tensor_tensor(before, before, onehot, ALU.subtract).then_inc(d["oh"], 1)
            dve.wait_ge(d["ex"], 1)
            link(dve.tensor_reduce(exp_sum, shifted, AX.X, ALU.add))
            link(dve.reciprocal(exp_sum, exp_sum))
            link(dve.tensor_scalar(xs[:, :, D], exp_sum, gate[:, 3:4], None, ALU.mult))
            dve.wait_ge(d["cnt"], 1)
            link(dve.tensor_copy(counts, banks[5][:, 0:E]))
            link(dve.tensor_tensor(fits, counts.unsqueeze(2).to_broadcast([P, E, T]),
                                   thr[:, :].unsqueeze(1).to_broadcast([P, E, T]), ALU.is_gt))
            link(dve.tensor_reduce(slots_of, fits, AX.X, ALU.add))
            link(dve.tensor_tensor_scan(slot_end, ones[:, 0:E], slots_of, 0.0, ALU.mult, ALU.add))
            link(dve.tensor_tensor(row_base, slot_end, slots_of, ALU.subtract))
            link(dve.tensor_scalar(row_base, row_base, float(P), None, ALU.mult))
            dve.wait_ge(d["rank"], 1)
            link(dve.tensor_tensor(places, banks[4][:, 0:T * E].rearrange("p (e t) -> p e t", e=E),
                                   row_base.unsqueeze(2).to_broadcast([P, E, T]), ALU.add))
            link(dve.tensor_tensor(places, places, onehot, ALU.mult))
            link(dve.tensor_reduce(place_f, places.rearrange("p e t -> p t e"), AX.X, ALU.add))
            dve.tensor_copy(place[:, :], place_f).then_inc(d["pli"], 1)
            link(dve.tensor_tensor(slot_cmp, slot_no[:, :].unsqueeze(2).to_broadcast([P, SLOTS, E]),
                                   slot_end.unsqueeze(1).to_broadcast([P, SLOTS, E]), ALU.is_ge))
            link(dve.tensor_reduce(slot_e, slot_cmp, AX.X, ALU.add))
            dve.tensor_scalar(slot_expert[:, :], slot_e[0:1], float(E - 1), None, ALU.min).then_inc(d["sei"], 1)

            def step_f(t, q, live):
                S0, S1, S2 = (k in live for k in range(3))
                if S0:
                    dve.wait_ge(ld_row[q], loads(t, q))
                    ln_stats(dve, rows_in[:, q, 0:D], q, t + 3 * T, f["ve"])
                if S2:
                    s = t - 2
                    dve.wait_ge(ld_late[q], loads(s, q))
                    wait(dve, sent[q], loads(s, q) - 16)
                    dve.tensor_copy(token[:, q:q + 1], rows_late[:, q, D + 1:D + 2]).then_inc(f["tok"], 1)
                if S0:
                    ln_apply(dve, xn[:, q], rows_in[:, q, 0:D], q, t, f["rstd"], f["xn"])
                    dve.wait_ge(f["xT"], t + 1)
                    dve.tensor_copy(xT[:, q].rearrange("p k n -> p (k n)"), banks[0][:, 0:D]).then_inc(f["xTs"], 1)
                if S2:
                    e = dve.value_load(slot_expert[0:1, bass.ds(s, 1)], min_val=0, max_val=E - 1)
                    dve.wait_ge(f["y"], s + 1)
                    dve.tensor_tensor(rows_out[:, q], banks[6][:, 0:D], b2s[:, bass.ds(e, 1)].rearrange("p a d -> p (a d)"),
                                      ALU.add).then_inc(f["yb"], 1)
                    dve.wait_ge(f["yb"], s + 1)
                    dve.scalar_tensor_tensor(out=rows_out[:, q], in0=rows_out[:, q], scalar=rows_late[:, q, D:D + 1],
                                             in1=rows_late[:, q, 0:D], op0=ALU.mult, op1=ALU.add).then_inc(f["yo"], 1)
            dve.wait_ge(d["sei"], 1)
            dve.wait_ge(d["ld_b"], 32)
            pipeline(dve, SLOTS, 3, step_f)

        @block.scalar
        def _(act):
            act.dma_start(wqs, wq).then_inc(ld_keys, 16)
            act.wait_ge(keyb_zero, 1)
            act.dma_start(keyb[0:NK, :, 0:NK], keys[0:NK]).then_inc(ld_keys, 16)
            act.dma_start(keyb[NK:P, :, NK:P], keys[NK:P]).then_inc(ld_keys, 16)
            act.wait_ge(ld_w0, 32)

            def step_a(t, q, live):
                if isinstance(t, int) and t == 2:
                    act.wait_ge(ld_a, 32)
                    act.activation(gate[:], r_gates, ACT.Tanh).then_inc(gates_done, 1)
                if isinstance(t, int) and t == 3:
                    act.wait_ge(simw_mm, 1)
                    act.activation(simw[:, 0], banks[6][:], ACT.Copy).then_inc(simw_done, 1)
                    act.activation(simw[:, 1], banks[7][:], ACT.Copy).then_inc(simw_done, 1)
                if isinstance(t, int) and 2 <= t < 6:
                    dst, src = ((dembs, demb), (wups, wup), (wdns, wdn), (uembs, uemb))[t - 2]
                    act.dma_start(dst, src).then_inc(ld_b, 16)
                if 2 in live:
                    s = t - 2
                    act.wait_ge(a["vw"], s + 1)
                    wait(act, a["o"], s - 1)
                    act.activation(vws[:, q], banks[2][:, 0:D], ACT.Copy).then_inc(a["vws"], 1)
                if 3 in live:
                    s, r = t - 3, 1 - q
                    act.wait_ge(a["pt"], s + 1)
                    wait(act, a["o"], s - 1)
                    act.activation(probT[:, r], banks[5][:, 0:P], ACT.Copy).then_inc(a["pts"], 1)
                if 2 in live:
                    s = t - 2
                    act.wait_ge(a["mx"], s + 1)
                    wait(act, a["pt"], s - 1)
                    wait(act, a["ri"], s - 1)
                    act.activation(prob[:, q], scoresA[q][:, 0:P], ACT.Exp, bias=nmax[:, q:q + 1],
                                   accum_out=esum[:, q:q + 1]).then_inc(a["ex"], 1)
                if 1 in live:
                    s, r = t - 1, 1 - q
                    act.wait_ge(a["tq"], s + 1)
                    wait(act, a["sc"], s - 1)
                    for k in range(KC):
                        last = act.activation(tqs[:, r, k], banks[1][:, k * P:(k + 1) * P], ACT.Identity,
                                              bias=colb[:, k:k + 1])
                    last.then_inc(a["tqs"], 1)

            def silu(p, q, h):
                act.wait_ge(b["zz"], HEADS * p + h + 1)
                act.activation(picked[:, q, h], picked[:, q, h], ACT.Silu, scale=rz[:, q, h:h + 1])\
                   .then_inc(b["act"], 1)

            def step_b(t, q, live):
                f, p, s, r = t - 1, t - 2, t - 3, 1 - q
                F, B1, B2 = (k in live for k in (1, 2, 3))
                if isinstance(t, int) and t == 0:
                    for dst, src in ((wkvs, wkv), (wqcs, wqc), (wocs, woc)):
                        act.dma_start(dst[:], src).then_inc(ld_cw, 16)
                if F:
                    if isinstance(t, int) and t <= 2:
                        act.wait_ge(a["sc"], T)
                    act.wait_ge(b["xT"], f + 1)
                    wait(act, b["up"], 2 * (f - 1))
                    act.activation(xT[:, r].rearrange("p k n -> p (k n)"), banks[0][:, 0:D], ACT.Copy)\
                       .then_inc(b["xTs"], 1)
                if B1:
                    act.wait_ge(b["d8"], p + 1)
                    act.activation(e8[:, q], d8[:, q], ACT.Exp).then_inc(b["e8"], 1)
                    act.wait_ge(b["pick"], 2 * HEADS * p + 2)
                    act.activation(grid[:, q, 0], grid[:, q, 0], ACT.Exp, bias=nm[:, q, 0:1]).then_inc(b["ex"], 1)
                if F:
                    act.wait_ge(b["sim"], f + 1)
                    wait(act, b["grid"], HEADS * (f - 1))
                    wait(act, b["mx"], f - 1)
                    act.activation(simS[:, r], banks[1][:], ACT.Copy).then_inc(b["simS"], 1)
                if B1:
                    for h in range(1, HEADS):
                        act.wait_ge(b["pick"], 2 * (HEADS * p + h) + 2)
                        act.activation(grid[:, q, h], grid[:, q, h], ACT.Exp, bias=nm[:, q, h:h + 1])\
                           .then_inc(b["ex"], 1)
                    for g in range(2):
                        act.wait_ge(b["up"], 2 * p + g + 1)
                        if g == 0:
                            wait(act, b["y"], p - 1)
                        act.activation(hT[:, q, g * BANK:(g + 1) * BANK], banks[4 + g][:], ACT.Silu)\
                           .then_inc(b["act2"], 1)
                    act.wait_ge(b["rz"], p + 1)
                    silu(p, q, 0)
                if B2:
                    for g in range(2):
                        act.wait_ge(b["st"], 2 * s + g + 1)
                        if g == 0:
                            wait(act, b["y"], s)
                        act.activation(pickT[:, g * BANK:(g + 1) * BANK], banks[7][:] if g else banks[0][:, :],
                                       ACT.Copy).then_inc(b["sts"], 1)
                if B1:
                    for h in range(1, HEADS):
                        silu(p, q, h)

            def step_c(t, q, live):
                if 1 in live:
                    s, r = t - 1, 1 - q
                    if isinstance(t, int) and t <= 2:
                        act.wait_ge(b["up"], 2 * T)
                    act.wait_ge(c["xT"], s + 1)
                    wait(act, c["qT"], s - 1)
                    act.activation(xT[:, r].rearrange("p k n -> p (k n)"), banks[0][:, 0:D], ACT.Copy)\
                       .then_inc(c["xTs"], 1)
                if 7 in live:
                    s = t - 7
                    act.wait_ge(d["xT"], s + 1)
                    wait(act, d["lg"], s)
                    act.activation(xT3.rearrange("p k n -> p (k n)"), banks[0][:, D:2 * D], ACT.Copy)\
                       .then_inc(d["xTs"], 1)
                if 2 in live:
                    s = t - 2
                    act.wait_ge(c["qT"], s + 1)
                    wait(act, c["q1"], s)
                    wait(act, c["den"], 2 * (s - 1))
                    wait(act, c["num"], s - 1)
                    for k in range(KC):
                        act.activation(qexp[:, k], banks[4][:, k * P:(k + 1) * P], ACT.Exp,
                                       bias=colb[:, KC + k:KC + k + 1])
                        last = act.activation(q1T[:, q, k], banks[4][:, k * P:(k + 1) * P], ACT.Relu,
                                              bias=colb[:, KC + k:KC + k + 1])
                    last.then_inc(c["qex"], 1)
                if 1 in live:
                    s, r = t - 1, 1 - q
                    if isinstance(t, int) and t <= 2:
                        act.wait_ge(b["sum1"], 2 * T)
                    act.wait_ge(c["kv"], s + 1)
                    wait(act, c["kvm"], 2 * (s - 1))
                    act.activation(kexp[:, r], banks[1][:, 0:D], ACT.Exp)
                    act.activation(k1[:, r], banks[1][:, 0:D], ACT.Relu).then_inc(c["kex"], 1)
                if 2 in live:
                    s = t - 2
                    act.wait_ge(c["kvm"], 2 * s + 2)
                    wait(act, c["num"], s - 1)
                    wait(act, c["den"], 2 * (s - 1))
                    act.activation(kvs[:, q].rearrange("p k n -> p (k n)"), banks[2], ACT.Copy)
                    act.activation(ksum[:, q], banks[3][:, 0:KC], ACT.Copy).then_inc(c["kvms"], 1)
            pipeline(act, T, 5, step_a, then=(5, step_b, LAG_B, (8, step_c, LAG_C, None)))

            act.wait_ge(d["lgs"], T)
            act.dma_start(b1s, b1).then_inc(d["ld_b"], 16)
            act.dma_start(b2s.rearrange("p e d -> p (e d)"), b2.partition_broadcast(P).rearrange("p a n -> p (a n)"))\
               .then_inc(d["ld_b"], 16)
            act.wait_ge(d["sh"], 1)
            act.activation(shifted, shifted, ACT.Exp).then_inc(d["ex"], 1)
            act.wait_ge(d["sei"], 1)
            act.wait_ge(d["ld_b"], 32)

            def step_f(t, q, live):
                if 1 in live:
                    s, r = t - 1, 1 - q
                    e = act.value_load(slot_expert[0:1, bass.ds(s, 1)], min_val=0, max_val=E - 1)
                    act.wait_ge(f["h"], s + 1)
                    wait(act, f["hT"], 2 * s)
                    act.activation(h_pre, table_dots[:, :], ACT.Copy).then_inc(f["hs"], 1)
                    for g in range(2):
                        held(act, f["hT"], 2 * s + g + 1)
                        if g == 0:
                            held(act, f["y"], s - 1)
                        for m in range(4 * g, 4 * g + 4):
                            last = act.activation(hTd[:, r, m * P:(m + 1) * P], banks[4 + g][:, (m % 4) * P:(m % 4 + 1) * P],
                                                  ACT.Relu, bias=b1s[:, bass.ds(e, 1), m])
                        last.then_inc(f["hTa"], 1)
            pipeline(act, SLOTS, 3, step_f)

        @block.tensor
        def _(pe):
            pe.wait_ge(consts, 3)
            pe.wait_ge(ld_w0, 32)

            def transpose2(dst, src, done):
                for k in range(KC):
                    last = pe.transpose(dst[:, k * P:(k + 1) * P], src[:, k * P:(k + 1) * P], ident[:, :])
                last.then_inc(done, 1)

            def step_a(t, q, live):
                if isinstance(t, int) and t == 3:
                    pe.wait_ge(ld_keys, 48)
                    for k in range(KC):
                        for n in range(4):
                            last = pe.matmul(banks[6 + k][:, n * P:(n + 1) * P], wqs[:, n, k * P:(k + 1) * P],
                                             keyb[:, n], start=True, stop=True)
                    last.then_inc(simw_mm, 1)
                if 2 in live:
                    s = t - 2
                    wait(pe, a["vws"], s)
                    for k in range(KC):
                        last = pe.matmul(banks[2][:, 0:D], ctxb[:, q, k], w0s[:, k], start=(k == 0), stop=(k == KC - 1))
                    last.then_inc(a["vw"], 1)
                if 4 in live:
                    s = t - 4
                    pe.wait_ge(a["pts"], s + 1)
                    pe.wait_ge(a["vws"], s + 1)
                    if isinstance(t, int) and s < 2:
                        pe.wait_ge(simw_done, 2)
                    wait(pe, a["u"], s - 1)
                    pe.matmul(outA[q][:, 0:D], probT[:, q], vws[:, q], start=True, stop=True).then_inc(a["o"], 1)
                if 3 in live:
                    s, r = t - 3, 1 - q
                    pe.wait_ge(a["ex"], s + 1)
                    wait(pe, a["pts"], s)
                    pe.transpose(banks[5][:, 0:P], prob[:, r], ident[:, :]).then_inc(a["pt"], 1)
                if 2 in live:
                    s = t - 2
                    pe.wait_ge(a["xTs"], s + 1)
                    pe.wait_ge(a["tqs"], s + 1)
                    wait(pe, a["ex"], s - 1)
                    for k in range(KC):
                        last = pe.matmul(scoresA[q][:, 0:P], xT[:, q, k], tqs[:, q, k],
                                         start=(k == 0), stop=(k == KC - 1))
                    last.then_inc(a["sc"], 1)
                if 1 in live:
                    s, r = t - 1, 1 - q
                    pe.wait_ge(a["xn"], s + 1)
                    wait(pe, a["xTs"], s)
                    transpose2(banks[0], xn[:, r], a["xT"])
                if 1 in live:
                    s, r = t - 1, 1 - q
                    pe.wait_ge(ld_ca[r], loads(s, r))
                    wait(pe, a["tqs"], s)
                    for o in range(KC):
                        for k in range(KC):
                            last = pe.matmul(banks[1][:, o * P:(o + 1) * P], w0s[:, k, o * P:(o + 1) * P], ctxb[:, r, k],
                                             start=(k == 0), stop=(k == KC - 1))
                    last.then_inc(a["tq"], 1)

            def step_b(t, q, live):
                f, p, s, r = t - 1, t - 2, t - 3, 1 - q
                F, B1, B2 = (k in live for k in (1, 2, 3))
                if isinstance(t, int) and t == 1:
                    pe.wait_ge(ld_b, 64)
                    for bank in ("xTs", "tqs", "vws", "ex"):
                        pe.wait_ge(a[bank], T)
                if isinstance(t, int) and t == 2:
                    pe.wait_ge(a["pts"], T)
                if isinstance(t, int) and t == 3:
                    pe.wait_ge(a["u"], T)
                if F:
                    pe.wait_ge(b["xn"], f + 1)
                    wait(pe, b["sts"], 2 * (t - 4) + 1)
                    transpose2(banks[0], xn[:, r], b["xT"])
                if B2:
                    wait(pe, b["x"], s)
                    for m in range(IC):
                        if m % 4 == 0:
                            pe.wait_ge(b["act2"], 2 * s + m // 4 + 1)
                        pe.matmul(banks[6][:, 0:D], hT[:, r, m * P:(m + 1) * P], wdns[:, m], start=(m == 0), stop=False)
                if F:
                    pe.wait_ge(b["xTs"], f + 1)
                    wait(pe, b["simS"], f)
                    for k in range(KC):
                        last = pe.matmul(banks[1][:], xT[:, r, k], simw[:, k], start=(k == 0), stop=(k == KC - 1))
                    last.then_inc(b["sim"], 1)
                if B1:
                    for g in range(2):
                        wait(pe, b["act2"], 2 * (p - 1) + g + 1)
                        for m in range(4):
                            for k in range(KC):
                                last = pe.matmul(banks[4 + g][:, m * P:(m + 1) * P],
                                                 wups[:, k, (4 * g + m) * P:(4 * g + m + 1) * P],
                                                 xT[:, q, k], start=(k == 0), stop=(k == KC - 1))
                        last.then_inc(b["up"], 1)
                if F:
                    wait(pe, b["pick"], 2 * HEADS * f)
                    for g in range(2):
                        for k in range(KC):
                            last = pe.matmul(banks[2 + g], xT[:, r, k], dembs[:, k, g * BANK:(g + 1) * BANK],
                                             start=(k == 0), stop=(k == KC - 1))
                    last.then_inc(b["dots"], 1)
                if B2:
                    pe.wait_ge(b["last"], s + 1)
                    for g in range(2):
                        if g == 1:
                            wait(pe, b["sts"], 2 * s)
                        for m in range(4):
                            last = pe.transpose((banks[7] if g else banks[0])[:, m * P:(m + 1) * P],
                                                picked[:, r, 0, (4 * g + m) * P:(4 * g + m + 1) * P], ident[:, :])
                        last.then_inc(b["st"], 1)
                    for m in range(IC):
                        if m % 4 == 0:
                            pe.wait_ge(b["sts"], 2 * s + m // 4 + 1)
                        last = pe.matmul(banks[6][:, 0:D], pickT[:, m * P:(m + 1) * P], uembs[:, m],
                                         start=False, stop=(m == IC - 1))
                    last.then_inc(b["y"], 1)

            def step_c(t, q, live):
                if isinstance(t, int) and t == 1:
                    pe.wait_ge(ld_cw, 48)
                    pe.wait_ge(b["sts"], 2 * T)
                    pe.wait_ge(b["simS"], T)
                    pe.wait_ge(b["pick"], 2 * HEADS * T)
                    pe.wait_ge(b["act2"], 2 * T)
                if isinstance(t, int) and t == 3:
                    pe.wait_ge(b["x"], T)
                wait(pe, c["xTs"], at_most(t - 1, T))
                if 7 in live:
                    s, r = t - 7, 1 - q
                    wait(pe, d["xTs"], s)
                    pe.wait_ge(d["xn"], s + 1)
                    transpose2(banks[0][:, D:2 * D], xn3[:, r], d["xT"])
                if 1 in live:
                    s, r = t - 1, 1 - q
                    wait(pe, d["xTs"], t - 7)
                    pe.wait_ge(c["xn"], s + 1)
                    transpose2(banks[0], xn[:, r], c["xT"])
                if 2 in live:
                    s = t - 2
                    pe.wait_ge(c["xTs"], s + 1)
                    wait(pe, c["qex"], s)
                    for o in range(KC):
                        for k in range(KC):
                            last = pe.matmul(banks[4][:, o * P:(o + 1) * P], wqcs[:, k, o * P:(o + 1) * P], xT[:, q, k],
                                             start=(k == 0), stop=(k == KC - 1))
                    last.then_inc(c["qT"], 1)
                if 4 in live:
                    s = t - 4
                    pe.wait_ge(c["ao"], s + 1)
                    wait(pe, c["r"], s)
                    wait(pe, d["lgs"], t - 7)
                    for k in range(KC):
                        last = pe.matmul(banks[7][:, 0:D], den[:, q, k], wocs[:, k], start=(k == 0), stop=(k == KC - 1))
                    last.then_inc(c["oo"], 1)
                if 1 in live:
                    s, r = t - 1, 1 - q
                    pe.wait_ge(ld_cc[r], loads(s, r))
                    wait(pe, c["kex"], s)
                    wait(pe, c["vb"], s)
                    pe.matmul(banks[1][:, 0:D], ones[0:1, :], r_bk[0:1], start=True, stop=False)
                    for k in range(KC):
                        pe.matmul(banks[1][:, 0:D], ctxb[:, r, k], wkvs[:, k, 0:D], start=False, stop=(k == KC - 1))
                    for k in range(KC):
                        last = pe.matmul(banks[5][:, 0:D], ctxb[:, r, k], wkvs[:, k, D:2 * D],
                                         start=(k == 0), stop=(k == KC - 1))
                    last.then_inc(c["kv"], 1)
                if 2 in live:
                    s = t - 2
                    pe.wait_ge(c["k1"], s + 1)
                    pe.wait_ge(c["vb"], s + 1)
                    wait(pe, c["kvms"], s)
                    for k in range(KC):
                        last = pe.matmul(banks[2][:, k * D:(k + 1) * D], k1[:, q, k * P:(k + 1) * P],
                                         v_c[:, q], start=True, stop=True)
                    last.then_inc(c["kvm"], 1)
                    for k in range(KC):
                        last = pe.matmul(banks[3][:, k:k + 1], k1[:, q, k * P:(k + 1) * P], ones[:, 0:1],
                                         start=True, stop=True)
                    last.then_inc(c["kvm"], 1)
                if 3 in live:
                    s, r = t - 3, 1 - q
                    pe.wait_ge(c["kvms"], s + 1)
                    pe.wait_ge(c["q1"], s + 1)
                    wait(pe, c["ao"], s)
                    for o in range(KC):
                        for k in range(KC):
                            last = pe.matmul(banks[6][:, o * P:(o + 1) * P], kvs[:, r, k, o * P:(o + 1) * P], q1T[:, r, k],
                                             start=(k == 0), stop=(k == KC - 1))
                    last.then_inc(c["num"], 1)
                if 7 in live:
                    s = t - 7
                    pe.wait_ge(d["xTs"], s + 1)
                    wait(pe, d["lgs"], s)
                    wait(pe, c["r"], at_most(t - 3, T))
                    for k in range(KC):
                        last = pe.matmul(banks[7][:, D:D + E], xT3[:, k], wgates[:, k], start=(k == 0), stop=(k == KC - 1))
                    last.then_inc(d["lg"], 1)
            pipeline(pe, T, 5, step_a, then=(5, step_b, LAG_B, (8, step_c, LAG_C, None)))

            pe.wait_ge(d["oh"], 1)
            pe.matmul(banks[5][:, 0:E], ones[:, :], onehot_sum, start=True, stop=True).then_inc(d["cnt"], 1)
            pe.wait_ge(d["below"], 1)
            pe.matmul(banks[4][:, 0:T * E], below, onehot.rearrange("p e t -> p (e t)"), start=True, stop=False)
            pe.matmul(banks[4][:, 0:T * E], ones[:, :], before.rearrange("p e t -> p (e t)"), start=False, stop=True)\
              .then_inc(d["rank"], 1)

            pe.wait_ge(d["sei"], 1)
            pe.wait_ge(d["pli"], 1)
            pe.wait_ge(d["ld_w"], 2 * 16 * T)
            pe.wait_ge(d["ld_b"], 32)

            def step_f(t, q, live):
                S0, S1, S2 = (k in live for k in range(3))
                if S1:
                    s, r = t - 1, 1 - q
                    e = pe.value_load(slot_expert[0:1, bass.ds(s, 1)], min_val=0, max_val=E - 1)
                    pe.wait_ge(f["xTs"], s + 1)
                    wait(pe, f["hs"], s)
                    for g in range(2):
                        for k in range(KC):
                            last = pe.matmul(banks[2 + g], xT[:, r, k],
                                             w1s[:, bass.ds(e, 1), k, g * BANK:(g + 1) * BANK].rearrange("p a n -> p (a n)"),
                                             start=(k == 0), stop=(k == KC - 1))
                    last.then_inc(f["h"], 1)
                if S0:
                    pe.wait_ge(f["xn"], t + 1)
                    wait(pe, f["xTs"], t)
                    transpose2(banks[0], xn[:, q], f["xT"])
                if S2:
                    s = t - 2
                    e = pe.value_load(slot_expert[0:1, bass.ds(s, 1)], min_val=0, max_val=E - 1)
                    wait(pe, f["yb"], s)
                    for m in range(IC):
                        if m % 4 == 0:
                            pe.wait_ge(f["hTa"], 2 * s + m // 4 + 1)
                        last = pe.matmul(banks[6][:, 0:D], hTd[:, q, m * P:(m + 1) * P],
                                         w2s[:, bass.ds(e, 1), m].rearrange("p a n -> p (a n)"),
                                         start=(m == 0), stop=(m == IC - 1))
                    last.then_inc(f["y"], 1)
                if S1:
                    s = t - 1
                    pe.wait_ge(f["hs"], s + 1)
                    wait(pe, f["hTa"], 2 * s)
                    for g in range(2):
                        for m in range(4):
                            last = pe.transpose(banks[4 + g][:, m * P:(m + 1) * P],
                                                h_pre[:, (4 * g + m) * P:(4 * g + m + 1) * P], ident[:, :])
                        last.then_inc(f["hT"], 1)
            pipeline(pe, SLOTS, 3, step_f)



def kernel(**inputs):
    import numpy as np
    import concourse.bacc as bacc
    from concourse.bass_utils import run_bass_kernel_spmd as run

    v = {k: np.asarray(a) for k, a in inputs.items()}

    def chunks(w):
        return w.reshape(-1, P, w.shape[-1]).transpose(1, 0, 2)

    x, context = v["x"], v["ctx_1024"]
    T, _, D = x.shape
    w1, w2 = v["L1_ffn_W1"], v["L1_ffn_W2"]
    E = w1.shape[0]
    keys = v["L0_ffn_keys"]
    arrays = {
        "x": x,
        "ctxT": context.transpose(0, 2, 1).reshape(T, -1, P, P).transpose(0, 2, 1, 3),
        "rows": np.concatenate([v[n].reshape(-1) for n in (
            "L0_xattn_b", "L1_xattn_bk", "L1_xattn_bv", "L1_xattn_bo", "L1_xattn_gamma",
            "L1_xattn_beta", "L1_ffn_b_gate", "g_xattn", "g_ffn")])[None],
        "cols": np.concatenate([v["L0_xattn_b"], v["L1_xattn_bq"]]).reshape(-1, P).T,
        "w0": chunks(v["L0_xattn_W"].T),
        "wup": chunks(v["L0_ffn_W_up"].T),
        "wdn": chunks(v["L0_ffn_W_down"].T),
        "wq": chunks(v["L0_ffn_W_q"]),
        "keys": chunks(keys.transpose(2, 0, 3, 1).reshape(-1, keys.shape[1])),
        "demb": chunks(v["L0_ffn_down_embed"].T),
        "uemb": chunks(v["L0_ffn_up_embed"]),
        "wkv": chunks(np.concatenate([v["L1_xattn_Wk"].T, v["L1_xattn_Wv"].T], axis=1)),
        "wqc": chunks(v["L1_xattn_Wq"].T),
        "woc": chunks(v["L1_xattn_Wo"].T),
        "wgate": chunks(v["L1_ffn_w_gate"]),
        "w1": w1.reshape(E, -1, P, w1.shape[2]).transpose(2, 0, 1, 3),
        "w2": w2.reshape(E, -1, P, D).transpose(2, 0, 1, 3),
        "b1": v["L1_ffn_b1"].reshape(E, -1, P).transpose(2, 0, 1),
        "b2": v["L1_ffn_b2"].reshape(1, -1),
    }
    arrays = {f"in_{n}": np.ascontiguousarray(a) for n, a in arrays.items()}
    nc = bacc.Bacc("TRN2", target_bir_lowering=False, num_devices=1)
    args = [nc.dram_tensor(n, a.shape, mybir.dt.from_np(a.dtype), kind="ExternalInput").ap()
            for n, a in arrays.items()]
    out = nc.dram_tensor("out", x.shape, F32, kind="ExternalOutput").ap()
    build(nc, *args, out)
    r = run(nc, [arrays], core_ids=[0])
    return r.results[0]["out"]
```

```python
from contextlib import ExitStack

import concourse.bass as bass
from concourse import mybir

F32 = mybir.dt.float32
I32 = mybir.dt.int32
ALU = mybir.AluOpType
ACT = mybir.ActivationFunctionType
AX = mybir.AxisListType

SCRATCH = 8704
P = 128
BANK = 512
LAG_B, LAG_C = 0, 1
EPS_LN = 1e-5
EPS_DENOM = 1e-6
FAR = 4096.0


def pipeline(eng, tiles, depth, step, then=None):
    first = depth + depth % 2
    for t in range(first):
        step(t, t % 2, [k for k in range(depth) if k <= t])
    while True:
        loops = (tiles - first) // 2
        with eng.Fori(0, loops) as i:
            for u in range(2):
                step(2 * i + (first + u), (first + u) % 2, list(range(depth)))
        last = range(first + 2 * loops, tiles + depth - 1)
        drain = [(step, t, [k for k in range(depth) if 0 <= t - k < tiles]) for t in last]
        if then is None:
            for run, t, live in drain:
                run(t, t % 2, live)
            return
        depth, step, lag, then = then
        first = depth + depth % 2
        for n in range(max(len(drain), lag + first)):
            if n < len(drain):
                run, t, live = drain[n]
                run(t, t % 2, live)
            if 0 <= n - lag < first:
                t = n - lag
                step(t, t % 2, [k for k in range(depth) if k <= t])


def at_most(value, most):
    return min(value, most) if isinstance(value, int) else value


def wait(eng, sem, value):
    if isinstance(value, int) and value <= 0:
        return
    eng.wait_ge(sem, value)


def build(nc, x, ctxT, rows, cols, w0, wup, wdn, wq, keys, demb, uemb, wkv, wqc, woc,
          wgate, w1, w2, b1, b2, out):
    T, _, D = x.shape
    KC = D // P
    IC = wdn.shape[1]
    HID = IC * P
    HEADS, NK, TOP = 4, 64, 8
    NX = HID // NK
    PAIRS = TOP * TOP
    GRID = HID + PAIRS
    E = w1.shape[1]

    SLOTS = T + E - 1

    with ExitStack() as ctx:
        tokens = nc.dram_tensor("tokens", (T * P, D), F32, kind="Internal").ap()

        def sb(name, shape, dt=F32):
            return ctx.enter_context(nc.sbuf_tensor(name, shape, dt))

        def sem(name):
            return ctx.enter_context(nc.semaphore(name))

        banks = [ctx.enter_context(nc.psum_tensor(f"bank{i}", [P, BANK], F32)) for i in (0, 1)]
        table_dots = ctx.enter_context(nc.psum_tensor("table_dots", [P, HID], F32))
        banks += [None, None]
        banks += [ctx.enter_context(nc.psum_tensor(f"bank{i}", [P, BANK], F32)) for i in (4, 5, 6, 7)]
        banks[2] = table_dots[:, 0:BANK]
        banks[3] = table_dots[:, BANK:HID]

        xs = sb("xs", [P, T, D])
        ctxb = sb("ctxb", [P, 2, KC, P])
        NR = rows.shape[1]
        rowb = sb("rowb", [P, NR])
        colb = sb("colb", [P, 2 * KC])
        gate = sb("gate", [P, 4])
        ident = sb("ident", [P, P])
        ones = sb("ones", [P, P])
        neg_half = sb("neg_half", [P, 1])
        minus_one = sb("minus_one", [P, 1])
        region1 = sb("region1", [P, E * KC * HID])
        region2 = sb("region2", [P, max(E * IC * D, 4 * HEADS * GRID)])

        region3 = sb("region3", [P, SCRATCH])
        region4 = sb("region4", [P, KC * HID])

        def carve(region, at, *shape):
            n = 1
            for s in shape:
                n *= s
            names = " ".join("abcd"[:len(shape)])
            v = region[:, at:at + n]
            if len(shape) > 1:
                v = v.rearrange(f"p ({names}) -> p {names}", **dict(zip("abcd", shape)))
            return v, at + n

        at = 0
        wups, at = carve(region1, at, KC, HID)
        wdns, at = carve(region1, at, IC, D)
        dembs, at = carve(region1, at, KC, HID)
        uembs, at = carve(region1, at, IC, D)
        wqs, at = carve(region1, at, 4, D)
        keyb, at = carve(region1, at, 4, P)
        simw, at = carve(region1, at, KC, BANK)
        at4 = 0
        wkvs, at4 = carve(region4, at4, KC, 2 * D)
        wqcs, at4 = carve(region4, at4, KC, D)
        wocs, at4 = carve(region4, at4, KC, D)
        at2 = 0
        grid, at2 = carve(region2, at2, 2, HEADS, GRID)
        picked, at2 = carve(region2, at2, 2, HEADS, GRID)

        stats = sb("stats", [P, 2, 6])
        mv = sb("mv", [P, 2, 2])
        ve = sb("ve", [P, 2])
        rstd = sb("rstd", [P, 2])
        xn = sb("xn", [P, 2, D])
        xT = sb("xT", [P, 2, KC, P])

        at3 = 0
        w0s, at3 = carve(region3, at3, KC, D)
        tqs, at3 = carve(region3, at3, 2, KC, P)
        vws, at3 = carve(region3, at3, 2, D)
        prob, at3 = carve(region3, at3, 2, P)
        probT, at3 = carve(region3, at3, 2, P)
        u_buf, at3 = carve(region3, at3, 2, D)
        r_buf, at3 = carve(region3, at3, 2, D)
        nmax = sb("nmax", [P, 2])
        esum = sb("esum", [P, 2])
        rsum = sb("rsum", [P, 2])
        scoresA = banks[3:5]
        outA = banks[6:8]

        simS, at = carve(region1, at, 2, BANK)
        hT, at = carve(region1, at, 2, HID)
        pickT, at = carve(region1, at, HID)
        top_x, at = carve(region1, at, 2, HEADS, TOP)
        top_y, at = carve(region1, at, 2, HEADS, TOP)
        top_c, at = carve(region1, at, 2, HEADS, TOP)
        cand, _ = carve(region3, SCRATCH - 2 * HEADS * PAIRS, 2, HEADS, PAIRS)
        top, at = carve(region1, at, 2, HEADS, TOP)
        nm = sb("nm", [P, 2, HEADS])
        d8, at = carve(region1, at, 2, HEADS * TOP)
        e8, at = carve(region1, at, 2, HEADS * TOP)
        zsum = sb("zsum", [P, 2, HEADS])
        rz = sb("rz", [P, 2, HEADS])
        tail = sb("tail", [P, 2])
        assert at <= E * KC * HID

        at3 = 0
        audio, at3 = carve(region3, at3, T, D)
        v_c, at3 = carve(region3, at3, 2, D + 1)
        k1, at3 = carve(region3, at3, 2, D)
        kvs, at3 = carve(region3, at3, 2, KC, D + 1)
        q1T, at3 = carve(region3, at3, 2, KC, P)
        den, at3 = carve(region3, at3, 2, KC, P)
        res, at3 = carve(region3, at3, 2, D)
        xn3, at3 = carve(region3, at3, 2, D)
        assert at3 <= SCRATCH
        kexp, at2 = carve(region2, E * IC * D, 2, D)
        qexp, at2 = carve(region2, at2, KC, P)
        xT3, at2 = carve(region2, at2, KC, P)
        assert at2 <= max(E * IC * D, 4 * HEADS * GRID)
        at3 = 0
        w1s = region1[:, :].rearrange("p (e k m) -> p e k m", e=E, k=KC)
        w2s = region2[:, 0:E * IC * D].rearrange("p (e m d) -> p e m d", e=E, m=IC)
        shifted, at3 = carve(region3, at3, T, E)
        onehot, at3 = carve(region3, at3, E, T)
        before, at3 = carve(region3, at3, E, T)
        places, at3 = carve(region3, at3, E, T)
        ranked, at3 = carve(region3, at3, T, E)
        fits, at3 = carve(region3, at3, E, T)
        slot_cmp, at3 = carve(region3, at3, SLOTS, E)
        top_logit, at3 = carve(region3, at3, T)
        exp_sum, at3 = carve(region3, at3, T)
        first_best, at3 = carve(region3, at3, T)
        place_f, at3 = carve(region3, at3, T)
        onehot_sum, at3 = carve(region3, at3, E)
        counts, at3 = carve(region3, at3, E)
        slots_of, at3 = carve(region3, at3, E)
        slot_end, at3 = carve(region3, at3, E)
        row_base, at3 = carve(region3, at3, E)
        slot_e, at3 = carve(region3, at3, SLOTS)
        b1s, at3 = carve(region3, at3, E, IC)
        b2s, at3 = carve(region3, at3, E, D)
        rows_in, _ = carve(region2, E * IC * D, 2, D)
        w1_even, at3 = carve(region3, at3, KC, HID)
        w1_odd, _ = carve(region4, 0, KC, HID)
        w1_slot = [w1_even, w1_odd]
        hTd, at3 = carve(region3, at3, 2, HID)
        rows_out, at3 = carve(region3, at3, 2, D)
        rows_late, at3 = carve(region3, at3, 2, D)
        below, at3 = carve(region3, at3, P)
        counted, at3 = carve(region3, at3, P)
        pos, at3 = carve(region3, at3, T)
        reached, at3 = carve(region3, at3, T)
        absent, at3 = carve(region3, at3, SLOTS)
        assert at3 <= SCRATCH
        pos_hot = w1_even.rearrange("p k m -> p (k m)").rearrange("p (t j) -> p t j", t=T)
        seats, at5 = carve(hTd.rearrange("p q m -> p (q m)"), 0, T, 2, SLOTS)
        passed, at5 = carve(hTd.rearrange("p q m -> p (q m)"), at5, T, SLOTS + 1)
        slot_hot, at5 = carve(hTd.rearrange("p q m -> p (q m)"), at5, T, SLOTS)
        wgates = sb("wgates", [P, KC, E])
        logits = sb("logits", [P, T, E])
        slot_expert = sb("slot_expert", [1, SLOTS], I32)
        index_in = sb("index_in", [P, 2], I32)
        index_late = sb("index_late", [P, 2], I32)
        index_out = sb("index_out", [P, 2], I32)
        gather_of = sb("gather_of", [P, SLOTS], I32)
        scatter_of = sb("scatter_of", [P, SLOTS], I32)
        weight_of = sb("weight_of", [P, SLOTS])
        same_expert = sb("same_expert", [P, E * T])
        down = sb("down", [P, E])
        slot_begin = sb("slot_begin", [P, SLOTS + 1])
        slot_no = sb("slot_no", [P, SLOTS])
        token_no = sb("token_no", [P, T])
        ints = sb("ints", [P, E + SLOTS + 1 + SLOTS + T + P], I32)

        stats2 = sb("stats2", [P, 2, 6])
        mv2 = sb("mv2", [P, 2, 2])
        ve2 = sb("ve2", [P, 2])
        rstd2 = sb("rstd2", [P, 2])
        shift2 = sb("shift2", [P, 2])
        stats3 = sb("stats3", [P, 2, 6])
        mv3 = sb("mv3", [P, 2, 2])
        ve3 = sb("ve3", [P, 2])
        rstd3 = sb("rstd3", [P, 2])
        shift3 = sb("shift3", [P, 2])

        col = 0

        def row(n):
            nonlocal col
            col += n
            return rowb[:, col - n:col]

        r_b0, r_bk, r_bv, r_bo, r_gamma, r_beta = (row(D) for _ in range(6))
        r_bgate, r_gates = row(E), row(4)
        assert col == NR

        waits_taken = sem("waits_taken")

        def held(eng, s, value):
            if isinstance(value, int) and value <= 0:
                return
            eng.wait_ge(s, value)
            eng.sem_inc(waits_taken, 1)

        ld_x = [sem(f"ld_x{q}") for q in range(2)]
        ld_ca = [sem(f"ld_ca{q}") for q in range(2)]
        ld_cc = [sem(f"ld_cc{q}") for q in range(2)]
        ld_a = sem("ld_a")
        ld_w0 = sem("ld_w0")
        ld_keys = sem("ld_keys")
        ld_b = sem("ld_b")
        ld_cw = sem("ld_cw")
        keyb_zero = sem("keyb_zero")
        consts = sem("consts")
        ident_zero = sem("ident_zero")
        gates_done = sem("gates_done")
        gated = sem("gated")
        simw_mm = sem("simw_mm")
        simw_done = sem("simw_done")

        def sems(prefix, names):
            return {n: sem(f"{prefix}_{n}") for n in names.split()}

        a = sems("a", "ve rstd xn xT xTs tq tqs vw vws sc mx ex ri pt pts o u r x")
        b = sems("b", "ve rstd xn xT xTs sim simS mx cand t8 nm d8 e8 z rz grid dots "
                      "pick ex zz act sum1 sum2 tail last st sts up act2 y x")
        c = sems("c", "ones ve rstd xn ab xT xTs kv vb kex k1 kvm kvms qT qex q1 den deni "
                      "num ao oo r ve2 rstd2 shift2 n ga be x")
        d = sems("d", "below ve rstd shift xn xT xTs lg lgs sh ex oh same cnt rank hot seated tables sei kept iota ld_b ld_w")
        routing = sem("routing")
        f = sems("f", "ix il ve rstd xn xT xTs h w1 hTa y yb yo tok")
        ln2_bn, ln2_ag = sem("ln2_bn"), sem("ln2_ag")
        ln3_bn, ln3_ag = sem("ln3_bn"), sem("ln3_ag")
        ln_bn, ln_ag = sem("ln_bn"), sem("ln_ag")
        ld_row = [sem(f"ld_row{q}") for q in range(2)]
        ld_late = [sem(f"ld_late{q}") for q in range(2)]
        sent = [sem(f"sent{q}") for q in range(2)]

        def ln_stats(dve, src, q, n, v):
            dve.bn_stats(stats[:, q, :], src).then_inc(ln_bn, 1)
            held(dve, ln_bn, n + 1)
            dve.bn_aggr(mv[:, q, :], stats[:, q, :]).then_inc(ln_ag, 1)
            dve.wait_ge(ln_ag, n + 1)
            dve.tensor_scalar(ve[:, q:q + 1], mv[:, q, 1:2], EPS_LN, None, ALU.add).then_inc(v, 1)

        def ln_apply(dve, dst, src, q, s, rs, done):
            dve.wait_ge(rs, s + 1)
            dve.tensor_scalar(dst, src, mv[:, q, 0:1], rstd[:, q:q + 1], ALU.subtract, ALU.mult)\
               .then_inc(done, 1)

        def ln_rstd(pool, q, s, v, rs):
            pool.wait_ge(v, s + 1)
            pool.tensor_tensor(rstd[:, q:q + 1], ve[:, q:q + 1], neg_half[:, :], ALU.pow).then_inc(rs, 1)

        def tile_of(t):
            return bass.ds(t, 1)

        def loads(t, q):
            return 8 * (t - q) + 16

        def x_at(t):
            return xs[:, tile_of(t)].rearrange("p a d -> p (a d)")

        block = ctx.enter_context(nc.Block())

        @block.sync
        def _(sp):
            def load_a(t, q, live):
                wait(sp, ln_bn, t - 1)
                sp.dma_start(x_at(t), x[tile_of(t)].rearrange("a p d -> (a p) d")).then_inc(ld_x[q], 16)
                wait(sp, a["vw"], t - 1)
                sp.dma_start(ctxb[:, q], ctxT[tile_of(t)].rearrange("a p k n -> (a p) k n")).then_inc(ld_ca[q], 16)
                if isinstance(t, int) and t == 0:
                    sp.dma_start(w0s, w0).then_inc(ld_w0, 16)
                    sp.dma_start(colb[:], cols).then_inc(ld_w0, 16)
                if isinstance(t, int) and t == 1:
                    sp.dma_start(rowb[:], rows.partition_broadcast(P).rearrange("p a n -> p (a n)")).then_inc(ld_a, 16)
                    sp.dma_start(wgates[:], wgate).then_inc(ld_a, 16)
            pipeline(sp, T, 2, lambda t, q, live: load_a(t, q, live) if 0 in live else None)

            def load_c(t, q, live):
                if 0 in live:
                    if isinstance(t, int):
                        sp.wait_ge(a["vw"], T)
                    wait(sp, c["kv"], t - 1)
                    sp.dma_start(ctxb[:, q], ctxT[tile_of(t)].rearrange("a p k n -> (a p) k n")).then_inc(ld_cc[q], 16)
                if 1 in live:
                    if isinstance(t, int):
                        sp.wait_ge(b["x"], T)
                    for dst, src, n in ((w1s, w1, E * KC // T), (w2s, w2, E * IC // T)):
                        sp.dma_start(dst.rearrange("p e k m -> p (e k) m")[:, bass.ds((t - 1) * n, n)],
                                     src.rearrange("p e k m -> p (e k) m")[:, bass.ds((t - 1) * n, n)])\
                          .then_inc(d["ld_w"], 16)
                if 7 in live:
                    sp.wait_ge(c["x"], t - 6)
                    sp.dma_start(tokens[bass.ds((t - 7) * P, P), :], x_at(t - 7)).then_inc(d["kept"], 16)
            assert E * KC % T == 0
            pipeline(sp, T, 8, load_c)

        @block.gpsimd
        def _(pool):
            pool.memset(keyb, 0.0).then_inc(keyb_zero, 1)
            pool.memset(ident[:], 0.0).then_inc(ident_zero, 1)
            pool.memset(ones[:], 1.0).then_inc(consts, 1)
            pool.memset(neg_half[:], -0.5).then_inc(consts, 1)
            pool.memset(minus_one[:], -1.0).then_inc(consts, 1)
            pool.wait_ge(ident_zero, 1)
            pool.affine_select(out=ident[:], in_=ident[:], compare_op=ALU.not_equal, fill=1.0, base=0,
                               pattern=[[-1, P]], channel_multiplier=1).then_inc(consts, 1)
            n = 0
            for count, first, step, channel in ((E, E, -1, 0), (SLOTS + 1, 0, P, 0), (SLOTS, 0, 1, 0), (T, 1, P, 1),
                                                (P, 0, 1, 0)):
                pool.iota(ints[:, n:n + count], pattern=[[step, count]], base=first,
                          channel_multiplier=channel).then_inc(d["iota"], 1)
                n += count
            pool.wait_ge(consts, 4)

            def step_a(t, q, live):
                if 0 in live:
                    ln_rstd(pool, q, t, a["ve"], a["rstd"])

            def grids(s, r):
                pool.wait_ge(b["simS"], s + 1)
                wait(pool, b["zz"], HEADS * (s - 1))
                for h in range(HEADS):
                    pool.tensor_tensor(
                        grid[:, r, h, 0:HID].rearrange("p (a b) -> p a b", b=NK),
                        simS[:, r, h * NK:h * NK + NX].unsqueeze(2).to_broadcast([P, NX, NK]),
                        simS[:, r, BANK // 2 + h * NK:BANK // 2 + (h + 1) * NK].unsqueeze(1).to_broadcast([P, NX, NK]),
                        ALU.add).then_inc(b["grid"], 1)

            def sum_pairs(s, q, pairs):
                for h in pairs:
                    pool.wait_ge(b["act"], HEADS * s + h + 2)
                    pool.tensor_tensor(picked[:, q, h], picked[:, q, h], picked[:, q, h + 1], ALU.add)\
                        .then_inc(b["sum1"], 1)

            def sum_rest(s, q):
                pool.wait_ge(b["sum1"], 2 * s + 2)
                pool.tensor_tensor(picked[:, q, 0], picked[:, q, 0], picked[:, q, 2], ALU.add)\
                    .then_inc(b["sum2"], 1)

            def step_b(t, q, live):
                if 3 in live:
                    sum_pairs(t - 3, 1 - q, (0,))
                if 0 in live:
                    ln_rstd(pool, q, t, b["ve"], b["rstd"])
                if 3 in live:
                    sum_pairs(t - 3, 1 - q, (2,))
                    sum_rest(t - 3, 1 - q)
                if 1 in live:
                    grids(t - 1, 1 - q)

            def scale_and_shift(scale, shift, ve, mean, scaled, shifted, s):
                pool.tensor_tensor(scale, ve, neg_half[:, :], ALU.pow).then_inc(scaled, 1)
                pool.tensor_tensor(shift, mean, minus_one[:, :], ALU.mult).then_inc(shifted, 1)
                pool.wait_ge(scaled, s + 1)
                pool.wait_ge(shifted, 2 * s + 1)
                pool.tensor_tensor(shift, shift, scale, ALU.mult).then_inc(shifted, 1)

            def step_c(t, q, live):
                if 0 in live:
                    ln_rstd(pool, q, t, c["ve"], c["rstd"])
                if 6 in live:
                    pool.wait_ge(d["ve"], t - 5)
                    scale_and_shift(rstd3[:, q:q + 1], shift3[:, q:q + 1], ve3[:, q:q + 1], mv3[:, q, 0:1],
                                    d["rstd"], d["shift"], t - 6)
                if 5 in live:
                    s, r = t - 5, 1 - q
                    if isinstance(t, int):
                        pool.wait_ge(gated, 2)
                    pool.wait_ge(c["n"], s + 1)
                    pool.tensor_tensor(res[:, r], res[:, r], r_gamma, ALU.mult).then_inc(c["ga"], 1)
                    pool.wait_ge(c["ga"], s + 1)
                    pool.tensor_tensor(res[:, r], res[:, r], r_beta, ALU.add).then_inc(c["be"], 1)
                    pool.wait_ge(c["be"], s + 1)
                    pool.tensor_tensor(x_at(s), x_at(s), res[:, r], ALU.add).then_inc(c["x"], 1)
                if 0 in live:
                    pool.wait_ge(c["xn"], t + 1)
                    pool.tensor_tensor(audio[:, tile_of(t)].rearrange("p a d -> p (a d)"), xn[:, q], r_bo, ALU.add)\
                        .then_inc(c["ab"], 1)
                if 4 in live:
                    pool.wait_ge(c["ve2"], t - 3)
                    scale_and_shift(rstd2[:, q:q + 1], shift2[:, q:q + 1], ve2[:, q:q + 1], mv2[:, q, 0:1],
                                    c["rstd2"], c["shift2"], t - 4)
            pipeline(pool, T, 5, step_a, then=(5, step_b, LAG_B, (8, step_c, LAG_C, None)))

            pool.wait_ge(d["lgs"], T)
            pool.affine_select(out=below, in_=ones[:], compare_op=ALU.is_gt, fill=0.0, base=0,
                               pattern=[[1, P]], channel_multiplier=-1).then_inc(d["below"], 1)
            pool.wait_ge(d["kept"], 16 * T)

            def gather(rows, index, q, done):
                pool.indirect_dma_start(out=rows[:, q], out_offset=None, in_=tokens,
                                        in_offset=bass.IndirectOffsetOnAxis(ap=index[:, q:q + 1], axis=0))\
                    .then_inc(done[q], 16)

            def step_f(t, q, live):
                if 1 in live:
                    ln_rstd(pool, 1 - q, t - 1, f["ve"], f["rstd"])
                if 0 in live:
                    held(pool, f["ix"], t + 1)
                    held(pool, f["xn"], t - 1)
                    gather(rows_in, index_in, q, ld_row)
                if 4 in live:
                    held(pool, f["yo"], t - 3)
                    pool.indirect_dma_start(
                        out=out.rearrange("t p d -> (t p) d"),
                        out_offset=bass.IndirectOffsetOnAxis(ap=index_out[:, q:q + 1], axis=0),
                        in_=rows_out[:, q], in_offset=None, bounds_check=T * P - 1, oob_is_err=False)\
                        .then_inc(sent[q], 16)
                if 2 in live:
                    held(pool, f["il"], t - 1)
                    held(pool, f["yo"], t - 3)
                    gather(rows_late, index_late, q, ld_late)
            pipeline(pool, SLOTS, 5, step_f)
            pool.wait_ge(sent[0], 16 * ((SLOTS + 1) // 2))
            pool.wait_ge(sent[1], 16 * (SLOTS // 2))

        @block.vector
        def _(dve):
            def step_a(t, q, live):
                if isinstance(t, int) and t == 3:
                    dve.wait_ge(ld_a, 32)
                    dve.wait_ge(gates_done, 1)
                    for r in (r_gamma, r_beta):
                        dve.tensor_scalar(r, r, gate[:, 1:2], None, ALU.mult).then_inc(gated, 1)
                    dve.wait_ge(d["iota"], 5)
                    dve.memset(same_expert[:, :], 1.0).then_inc(d["same"], 1)
                    n = 0
                    for dst in (down, slot_begin, slot_no, token_no):
                        dve.tensor_copy(dst[:, :], ints[:, n:n + dst.shape[1]])
                        n += dst.shape[1]
                    dve.wait_ge(d["same"], 1)
                    dve.memset(same_expert[:, :].rearrange("p (e t) -> p e t", e=E)[:, :, 0], 0.0)
                if 3 in live:
                    s, r = t - 3, 1 - q
                    dve.wait_ge(a["ex"], s + 1)
                    dve.reciprocal(rsum[:, r:r + 1], esum[:, r:r + 1]).then_inc(a["ri"], 1)
                if 0 in live:
                    dve.wait_ge(ld_x[q], loads(t, q))
                    ln_stats(dve, x_at(t), q, t, a["ve"])
                if 4 in live:
                    s = t - 4
                    dve.wait_ge(a["o"], s + 1)
                    held(dve, a["ri"], s + 1)
                    dve.scalar_tensor_tensor(out=u_buf[:, q], in0=outA[q][:, 0:D], scalar=rsum[:, q:q + 1],
                                             in1=r_b0, op0=ALU.mult, op1=ALU.add).then_inc(a["u"], 1)
                if 0 in live:
                    ln_apply(dve, xn[:, q], x_at(t), q, t, a["rstd"], a["xn"])
                if 4 in live:
                    dve.wait_ge(a["u"], s + 1)
                    dve.tensor_scalar(r_buf[:, q], u_buf[:, q], 0.0, gate[:, 0:1], ALU.max, ALU.mult)\
                       .then_inc(a["r"], 1)
                if 2 in live:
                    dve.wait_ge(a["sc"], t - 1)
                    dve.tensor_reduce(nmax[:, q:q + 1], scoresA[q][:, 0:P], AX.X, ALU.max, negate=True)\
                        .then_inc(a["mx"], 1)
                if 4 in live:
                    dve.wait_ge(a["r"], s + 1)
                    dve.tensor_tensor(x_at(s), x_at(s), r_buf[:, q], ALU.add).then_inc(a["x"], 1)
                if 1 in live:
                    dve.wait_ge(a["xT"], t)
                    dve.tensor_copy(xT[:, 1 - q].rearrange("p k n -> p (k n)"), banks[0][:, 0:D]).then_inc(a["xTs"], 1)
            def pick(s, r, h):
                if h == 0:
                    dve.wait_ge(b["dots"], s + 1)
                    wait(dve, b["st"], 2 * (s - 1))
                dve.wait_ge(b["grid"], HEADS * s + h + 1)
                least = top[:, r, h, TOP - 1:TOP]
                dve.scalar_tensor_tensor(out=picked[:, r, h, 0:HID], in0=grid[:, r, h, 0:HID], scalar=least,
                                         in1=table_dots[:, :], op0=ALU.is_ge, op1=ALU.mult).then_inc(b["pick"], 1)
                dve.scalar_tensor_tensor(out=picked[:, r, h, HID:GRID], in0=grid[:, r, h, HID:GRID], scalar=least,
                                         in1=table_dots[:, HID - 1:HID].to_broadcast([P, PAIRS]),
                                         op0=ALU.is_ge, op1=ALU.mult).then_inc(b["pick"], 1)

            def weigh(s, r, h):
                dve.wait_ge(b["ex"], HEADS * s + h + 1)
                dve.tensor_tensor(picked[:, r, h], picked[:, r, h], grid[:, r, h], ALU.mult).then_inc(b["zz"], 1)

            def step_b(t, q, live):
                f, p, s, r = t - 1, t - 2, t - 3, 1 - q
                L, F, B1, B2, FIN = (k in live for k in range(5))
                if FIN:
                    dve.wait_ge(b["y"], t - 3)
                    dve.scalar_tensor_tensor(out=x_at(t - 4), in0=banks[6][:, 0:D], scalar=gate[:, 2:3],
                                             in1=x_at(t - 4), op0=ALU.mult, op1=ALU.add).then_inc(b["x"], 1)
                if L:
                    dve.wait_ge(a["x"], t + 1)
                    ln_stats(dve, x_at(t), q, t + T, b["ve"])
                if B1:
                    pick(p, q, 0)
                    dve.wait_ge(b["e8"], p + 1)
                    dve.tensor_reduce(zsum[:, q], e8[:, q].rearrange("p (h k) -> p h k", k=TOP), AX.X, ALU.add)\
                       .then_inc(b["z"], 1)
                    pick(p, q, 1)
                    dve.wait_ge(b["z"], p + 1)
                    dve.reciprocal(rz[:, q], zsum[:, q]).then_inc(b["rz"], 1)
                    pick(p, q, 2)
                    pick(p, q, 3)
                if L:
                    if isinstance(t, int) and t < 2:
                        dve.wait_ge(a["xT"], T)
                    wait(dve, b["xT"], t - 1)
                    ln_apply(dve, xn[:, q], x_at(t), q, t, b["rstd"], b["xn"])
                if B1:
                    weigh(p, q, 0)
                if B2:
                    dve.wait_ge(b["sum2"], s + 1)
                    dve.tensor_reduce(tail[:, r:r + 1], picked[:, r, 0, HID - 1:GRID], AX.X, ALU.add)\
                       .then_inc(b["tail"], 1)
                if B1:
                    weigh(p, q, 1)
                if B2:
                    dve.wait_ge(b["tail"], s + 1)
                    dve.tensor_copy(picked[:, r, 0, HID - 1:HID], tail[:, r:r + 1]).then_inc(b["last"], 1)
                if F:
                    held(dve, b["simS"], f + 1)
                    for h in range(HEADS):
                        first, second = h * NK, BANK // 2 + h * NK
                        dve.max(top_x[:, r, h], simS[:, r, first:first + NK])
                        dve.max(top_y[:, r, h], simS[:, r, second:second + NK])
                        last = dve.max(top_c[:, r, h], simS[:, r, first + NX:first + NK])
                    last.then_inc(b["mx"], 1)
                if B1:
                    weigh(p, q, 2)
                if F:
                    dve.wait_ge(b["mx"], f + 1)
                    wait(dve, b["ex"], HEADS * (f - 1))
                    y = top_y[:, r].unsqueeze(2).to_broadcast([P, HEADS, TOP, TOP])
                    dve.tensor_tensor(cand[:, r].rearrange("p h (i j) -> p h i j", j=TOP),
                                      top_x[:, r].unsqueeze(3).to_broadcast([P, HEADS, TOP, TOP]), y, ALU.add)\
                       .then_inc(b["cand"], 1)
                    dve.tensor_tensor(grid[:, r, :, HID:GRID].rearrange("p h (i j) -> p h i j", j=TOP),
                                      top_c[:, r].unsqueeze(3).to_broadcast([P, HEADS, TOP, TOP]), y, ALU.add)\
                       .then_inc(b["cand"], 1)
                    held(dve, b["cand"], 2 * f + 2)
                    for h in range(HEADS):
                        last = dve.max(top[:, r, h], cand[:, r, h])
                    last.then_inc(b["t8"], 1)
                if B1:
                    weigh(p, q, 3)
                if F:
                    dve.wait_ge(b["t8"], f + 1)
                    dve.tensor_scalar(nm[:, r], top[:, r, :, 0], -1.0, None, ALU.mult).then_inc(b["nm"], 1)
                    wait(dve, b["e8"], f - 1)
                    dve.tensor_tensor(d8[:, r].rearrange("p (h k) -> p h k", k=TOP), top[:, r],
                                      top[:, r, :, 0:1].to_broadcast([P, HEADS, TOP]), ALU.subtract).then_inc(b["d8"], 1)

            def step_c(t, q, live):
                if 2 in live:
                    s = t - 2
                    dve.wait_ge(c["kex"], s + 1)
                    dve.scalar_tensor_tensor(out=k1[:, q], in0=kexp[:, q], scalar=1.0, in1=k1[:, q],
                                             op0=ALU.min, op1=ALU.add).then_inc(c["k1"], 1)
                if 3 in live:
                    s, r = t - 3, 1 - q
                    dve.wait_ge(c["qex"], s + 1)
                    dve.scalar_tensor_tensor(out=q1T[:, r], in0=qexp, scalar=1.0, in1=q1T[:, r],
                                             op0=ALU.min, op1=ALU.add).then_inc(c["q1"], 1)
                    dve.wait_ge(c["q1"], s + 1)
                    dve.wait_ge(c["kvms"], s + 1)
                    wait(dve, c["oo"], s - 1)
                    for k in range(KC):
                        dve.tensor_scalar(den[:, r, k], q1T[:, r, k], kvs[:, r, k, D:D + 1], EPS_DENOM,
                                          ALU.mult, ALU.add).then_inc(c["den"], 1)
                if 6 in live:
                    dve.wait_ge(c["x"], t - 5)
                    dve.bn_stats(stats3[:, q, :], x_at(t - 6)).then_inc(ln3_bn, 1)
                if isinstance(t, int) and t == 0:
                    dve.memset(v_c[:, :, D:D + 1], 1.0).then_inc(c["ones"], 1)
                if 0 in live:
                    dve.wait_ge(b["x"], t + 1)
                    ln_stats(dve, x_at(t), q, t + 2 * T, c["ve"])
                if 6 in live:
                    held(dve, ln3_bn, t - 5)
                    dve.bn_aggr(mv3[:, q, :], stats3[:, q, :]).then_inc(ln3_ag, 1)
                    dve.wait_ge(ln3_ag, t - 5)
                    dve.tensor_scalar(ve3[:, q:q + 1], mv3[:, q, 1:2], EPS_LN, None, ALU.add).then_inc(d["ve"], 1)
                if 3 in live:
                    dve.wait_ge(c["den"], 2 * s + 2)
                    dve.reciprocal(den[:, r], den[:, r]).then_inc(c["deni"], 1)
                if 4 in live:
                    s = t - 4
                    dve.wait_ge(c["oo"], s + 1)
                    dve.wait_ge(c["ab"], s + 1)
                    wait(dve, c["x"], s - 1)
                    dve.tensor_tensor(res[:, q], banks[7][:, 0:D], audio[:, tile_of(s)].rearrange("p a d -> p (a d)"),
                                      ALU.add).then_inc(c["r"], 1)
                if 0 in live:
                    if isinstance(t, int) and t < 2:
                        dve.wait_ge(b["xT"], T)
                    wait(dve, c["xT"], t - 1)
                    wait(dve, c["ab"], t - 1)
                    ln_apply(dve, xn[:, q], x_at(t), q, t, c["rstd"], c["xn"])
                if 4 in live:
                    dve.wait_ge(c["r"], s + 1)
                    dve.bn_stats(stats2[:, q, :], res[:, q]).then_inc(ln2_bn, 1)
                if 1 in live:
                    s, r = t - 1, 1 - q
                    dve.wait_ge(c["kv"], s + 1)
                    wait(dve, c["kvm"], s - 1)
                    dve.tensor_tensor(v_c[:, r, 0:D], banks[5][:, 0:D], r_bv, ALU.add).then_inc(c["vb"], 1)
                if 4 in live:
                    s = t - 4
                    held(dve, ln2_bn, s + 1)
                    dve.bn_aggr(mv2[:, q, :], stats2[:, q, :]).then_inc(ln2_ag, 1)
                    dve.wait_ge(ln2_ag, s + 1)
                    dve.tensor_scalar(ve2[:, q:q + 1], mv2[:, q, 1:2], EPS_LN, None, ALU.add).then_inc(c["ve2"], 1)
                if 3 in live:
                    s, r = t - 3, 1 - q
                    dve.wait_ge(c["deni"], s + 1)
                    dve.wait_ge(c["num"], s + 1)
                    dve.tensor_tensor(den[:, r].rearrange("p k n -> p (k n)"), banks[6][:, 0:D],
                                      den[:, r].rearrange("p k n -> p (k n)"), ALU.mult).then_inc(c["ao"], 1)
                if 7 in live:
                    s = t - 7
                    dve.wait_ge(d["lg"], s + 1)
                    dve.tensor_tensor(logits[:, tile_of(s), :].rearrange("p a e -> p (a e)"), banks[7][:, D:D + E],
                                      r_bgate, ALU.add).then_inc(d["lgs"], 1)
            pipeline(dve, T, 5, step_a, then=(5, step_b, LAG_B, (8, step_c, LAG_C, None)))

            links = [0]

            def link(ins):
                links[0] += 1
                ins.then_inc(routing, 1)
                dve.wait_ge(routing, links[0])

            n = ints.shape[1] - P
            dve.tensor_copy(counted, ints[:, n:n + P])
            dve.wait_ge(d["lgs"], T)
            link(dve.tensor_reduce(top_logit, logits[:, :, :], AX.X, ALU.max))
            best = top_logit.unsqueeze(2).to_broadcast([P, T, E])
            dve.tensor_tensor(shifted, logits[:, :, :], best, ALU.subtract).then_inc(d["sh"], 1)
            link(dve.tensor_tensor(ranked, logits[:, :, :], best, ALU.is_ge))
            link(dve.tensor_tensor(ranked, ranked, down[:, :].unsqueeze(1).to_broadcast([P, T, E]), ALU.mult))
            link(dve.tensor_reduce(first_best, ranked, AX.X, ALU.max))
            link(dve.tensor_tensor(onehot.rearrange("p e t -> p t e"), ranked,
                                   first_best.unsqueeze(2).to_broadcast([P, T, E]), ALU.is_equal))
            flat = lambda v: v.rearrange("p e t -> p (e t)")
            link(dve.tensor_tensor_scan(flat(before), same_expert[:, :], flat(onehot), 0.0, ALU.mult, ALU.add))
            link(dve.tensor_copy(onehot_sum, before[:, :, T - 1]))
            dve.tensor_tensor(before, before, onehot, ALU.subtract).then_inc(d["oh"], 1)
            dve.wait_ge(d["ex"], 1)
            link(dve.tensor_reduce(exp_sum, shifted, AX.X, ALU.add))
            link(dve.reciprocal(exp_sum, exp_sum))
            link(dve.tensor_scalar(exp_sum, exp_sum, gate[:, 3:4], None, ALU.mult))
            dve.wait_ge(d["cnt"], 1)
            link(dve.tensor_copy(counts, banks[5][:, 0:E]))
            link(dve.tensor_tensor(fits, counts.unsqueeze(2).to_broadcast([P, E, T]),
                                   slot_begin[:, 0:T].unsqueeze(1).to_broadcast([P, E, T]), ALU.is_gt))
            link(dve.tensor_reduce(slots_of, fits, AX.X, ALU.add))
            link(dve.tensor_tensor_scan(slot_end, ones[:, 0:E], slots_of, 0.0, ALU.mult, ALU.add))
            link(dve.tensor_tensor(row_base, slot_end, slots_of, ALU.subtract))
            link(dve.tensor_scalar(row_base, row_base, float(P), None, ALU.mult))
            dve.wait_ge(d["rank"], 1)
            link(dve.tensor_tensor(places, banks[4][:, 0:T * E].rearrange("p (e t) -> p e t", e=E),
                                   row_base.unsqueeze(2).to_broadcast([P, E, T]), ALU.add))
            link(dve.tensor_tensor(places, places, onehot, ALU.mult))
            link(dve.tensor_reduce(place_f, places.rearrange("p e t -> p t e"), AX.X, ALU.add))
            link(dve.tensor_tensor(passed, place_f.unsqueeze(2).to_broadcast([P, T, SLOTS + 1]),
                                   slot_begin[:, :].unsqueeze(1).to_broadcast([P, T, SLOTS + 1]), ALU.is_ge))
            dve.tensor_tensor(slot_hot, passed[:, :, 0:SLOTS], passed[:, :, 1:SLOTS + 1], ALU.subtract)
            link(dve.tensor_reduce(reached, passed, AX.X, ALU.add))
            link(dve.scalar_tensor_tensor(out=pos, in0=reached, scalar=-float(P), in1=place_f,
                                          op0=ALU.mult, op1=ALU.add))
            dve.tensor_tensor(seats[:, :, 0], slot_hot,
                              token_no[:, :].unsqueeze(2).to_broadcast([P, T, SLOTS]), ALU.mult)
            dve.tensor_tensor(seats[:, :, 1], slot_hot,
                              exp_sum.unsqueeze(2).to_broadcast([P, T, SLOTS]), ALU.mult)
            link(dve.tensor_scalar(pos, pos, float(P), None, ALU.add))
            for t in range(T):
                dve.tensor_scalar(pos_hot[:, t], counted, pos[:, t:t + 1], None, ALU.is_equal).then_inc(d["hot"], 1)
            link(dve.tensor_tensor(slot_cmp, slot_no[:, :].unsqueeze(2).to_broadcast([P, SLOTS, E]),
                                   slot_end.unsqueeze(1).to_broadcast([P, SLOTS, E]), ALU.is_ge))
            link(dve.tensor_reduce(slot_e, slot_cmp, AX.X, ALU.add))
            dve.tensor_scalar(slot_expert[:, :], slot_e[0:1], float(E - 1), None, ALU.min).then_inc(d["sei"], 1)
            dve.wait_ge(d["seated"], 1)
            no = banks[6][:, 0:SLOTS]
            dve.tensor_scalar(gather_of[:, :], no, 1.0, 1.0, ALU.max, ALU.subtract).then_inc(d["tables"], 1)
            link(dve.tensor_scalar(absent, no, 0.0, FAR, ALU.is_equal, ALU.mult))
            dve.scalar_tensor_tensor(out=scatter_of[:, :], in0=no, scalar=-1.0, in1=absent, op0=ALU.add, op1=ALU.add)\
               .then_inc(d["tables"], 1)
            dve.tensor_copy(weight_of[:, :], banks[6][:, SLOTS:2 * SLOTS]).then_inc(d["tables"], 1)


            def step_f(t, q, live):
                r, u, s = 1 - q, t - 1, t - 4
                if 1 in live:
                    dve.wait_ge(ld_row[r], loads(u, r))
                    ln_stats(dve, rows_in[:, r], r, u + 3 * T, f["ve"])
                if 4 in live:
                    e = dve.value_load(slot_expert[0:1, bass.ds(s, 1)], min_val=0, max_val=E - 1)
                    wait(dve, sent[q], loads(s, q) - 16)
                    dve.wait_ge(f["y"], s + 1)
                    dve.tensor_tensor(rows_out[:, q], banks[6][:, 0:D], b2s[:, bass.ds(e, 1)].rearrange("p a d -> p (a d)"),
                                      ALU.add).then_inc(f["yb"], 1)
                if 1 in live:
                    ln_apply(dve, xn[:, r], rows_in[:, r], r, u, f["rstd"], f["xn"])
                if 0 in live:
                    dve.tensor_copy(index_in[:, q:q + 1], gather_of[:, bass.ds(t, 1)]).then_inc(f["ix"], 1)
                if 4 in live:
                    held(dve, ld_late[q], loads(s, q))
                    dve.tensor_copy(index_out[:, q:q + 1], scatter_of[:, bass.ds(s, 1)]).then_inc(f["tok"], 1)
                    dve.wait_ge(f["yb"], s + 1)
                    dve.scalar_tensor_tensor(out=rows_out[:, q], in0=rows_out[:, q], scalar=weight_of[:, bass.ds(s, 1)],
                                             in1=rows_late[:, q], op0=ALU.mult, op1=ALU.add).then_inc(f["yo"], 1)
                if 1 in live:
                    held(dve, ld_late[r], loads(u, r) - 16)
                    dve.tensor_copy(index_late[:, r:r + 1], gather_of[:, bass.ds(u, 1)]).then_inc(f["il"], 1)
                    e = dve.value_load(slot_expert[0:1, bass.ds(u, 1)], min_val=0, max_val=E - 1)
                    wait(dve, f["h"], 2 * (u - 1))
                    dve.tensor_copy(w1_slot[r], w1s[:, bass.ds(e, 1)].rearrange("p a k m -> p (a k) m"))\
                       .then_inc(f["w1"], 1)
                    dve.wait_ge(f["xT"], u + 1)
                    dve.tensor_copy(xT[:, r].rearrange("p k n -> p (k n)"), banks[0][:, 0:D]).then_inc(f["xTs"], 1)
            dve.wait_ge(d["tables"], 3)
            dve.wait_ge(d["sei"], 1)
            dve.wait_ge(d["ld_b"], 32)
            dve.wait_ge(d["ld_w"], 2 * 16 * T)
            pipeline(dve, SLOTS, 5, step_f)

        @block.scalar
        def _(act):
            act.dma_start(wqs, wq).then_inc(ld_keys, 16)
            act.wait_ge(keyb_zero, 1)
            act.dma_start(keyb[0:NK, :, 0:NK], keys[0:NK]).then_inc(ld_keys, 16)
            act.dma_start(keyb[NK:P, :, NK:P], keys[NK:P]).then_inc(ld_keys, 16)
            act.wait_ge(ld_w0, 32)

            def step_a(t, q, live):
                if isinstance(t, int) and t == 2:
                    act.wait_ge(ld_a, 32)
                    act.activation(gate[:], r_gates, ACT.Tanh).then_inc(gates_done, 1)
                if isinstance(t, int) and t == 3:
                    act.wait_ge(simw_mm, 1)
                    act.activation(simw[:, 0], banks[6][:], ACT.Copy).then_inc(simw_done, 1)
                    act.activation(simw[:, 1], banks[7][:], ACT.Copy).then_inc(simw_done, 1)
                if isinstance(t, int) and 2 <= t < 6:
                    dst, src = ((dembs, demb), (wups, wup), (wdns, wdn), (uembs, uemb))[t - 2]
                    act.dma_start(dst, src).then_inc(ld_b, 16)
                if 2 in live:
                    s = t - 2
                    act.wait_ge(a["vw"], s + 1)
                    wait(act, a["o"], s - 1)
                    act.activation(vws[:, q], banks[2][:, 0:D], ACT.Copy).then_inc(a["vws"], 1)
                if 3 in live:
                    s, r = t - 3, 1 - q
                    act.wait_ge(a["pt"], s + 1)
                    wait(act, a["o"], s - 1)
                    act.activation(probT[:, r], banks[5][:, 0:P], ACT.Copy).then_inc(a["pts"], 1)
                if 2 in live:
                    s = t - 2
                    act.wait_ge(a["mx"], s + 1)
                    wait(act, a["pt"], s - 1)
                    wait(act, a["ri"], s - 1)
                    act.activation(prob[:, q], scoresA[q][:, 0:P], ACT.Exp, bias=nmax[:, q:q + 1],
                                   accum_out=esum[:, q:q + 1]).then_inc(a["ex"], 1)
                if 1 in live:
                    s, r = t - 1, 1 - q
                    act.wait_ge(a["tq"], s + 1)
                    wait(act, a["sc"], s - 1)
                    for k in range(KC):
                        last = act.activation(tqs[:, r, k], banks[1][:, k * P:(k + 1) * P], ACT.Identity,
                                              bias=colb[:, k:k + 1])
                    last.then_inc(a["tqs"], 1)

            def silu(p, q, h):
                act.wait_ge(b["zz"], HEADS * p + h + 1)
                act.activation(picked[:, q, h], picked[:, q, h], ACT.Silu, scale=rz[:, q, h:h + 1])\
                   .then_inc(b["act"], 1)

            def step_b(t, q, live):
                f, p, s, r = t - 1, t - 2, t - 3, 1 - q
                F, B1, B2 = (k in live for k in (1, 2, 3))
                if isinstance(t, int) and t == 0:
                    for dst, src in ((wkvs, wkv), (wqcs, wqc), (wocs, woc)):
                        act.dma_start(dst, src).then_inc(ld_cw, 16)
                if F:
                    if isinstance(t, int) and t <= 2:
                        act.wait_ge(a["sc"], T)
                    act.wait_ge(b["xT"], f + 1)
                    wait(act, b["up"], 2 * (f - 1))
                    act.activation(xT[:, r].rearrange("p k n -> p (k n)"), banks[0][:, 0:D], ACT.Copy)\
                       .then_inc(b["xTs"], 1)
                if B1:
                    act.wait_ge(b["d8"], p + 1)
                    act.activation(e8[:, q], d8[:, q], ACT.Exp).then_inc(b["e8"], 1)
                    act.wait_ge(b["pick"], 2 * HEADS * p + 2)
                    act.activation(grid[:, q, 0], grid[:, q, 0], ACT.Exp, bias=nm[:, q, 0:1]).then_inc(b["ex"], 1)
                    act.wait_ge(b["pick"], 2 * (HEADS * p + 1) + 2)
                    act.activation(grid[:, q, 1], grid[:, q, 1], ACT.Exp, bias=nm[:, q, 1:2]).then_inc(b["ex"], 1)
                if F:
                    act.wait_ge(b["sim"], f + 1)
                    wait(act, b["grid"], HEADS * (f - 1))
                    wait(act, b["mx"], f - 1)
                    act.activation(simS[:, r], banks[1][:], ACT.Copy).then_inc(b["simS"], 1)
                if B1:
                    for h in range(2, HEADS):
                        act.wait_ge(b["pick"], 2 * (HEADS * p + h) + 2)
                        act.activation(grid[:, q, h], grid[:, q, h], ACT.Exp, bias=nm[:, q, h:h + 1])\
                           .then_inc(b["ex"], 1)
                    for g in range(2):
                        act.wait_ge(b["up"], 2 * p + g + 1)
                        if g == 0:
                            wait(act, b["y"], p - 1)
                        act.activation(hT[:, q, g * BANK:(g + 1) * BANK], banks[4 + g][:], ACT.Silu)\
                           .then_inc(b["act2"], 1)
                    act.wait_ge(b["rz"], p + 1)
                    silu(p, q, 0)
                if B2:
                    for g in range(2):
                        act.wait_ge(b["st"], 2 * s + g + 1)
                        if g == 0:
                            wait(act, b["y"], s)
                        act.activation(pickT[:, g * BANK:(g + 1) * BANK], banks[7][:] if g else banks[0][:, :],
                                       ACT.Copy).then_inc(b["sts"], 1)
                if B1:
                    for h in range(1, HEADS):
                        silu(p, q, h)

            def step_c(t, q, live):
                if 5 in live:
                    s, r = t - 5, 1 - q
                    act.wait_ge(c["shift2"], 2 * s + 2)
                    act.activation(res[:, r], res[:, r], ACT.Identity, bias=shift2[:, r:r + 1],
                                   scale=rstd2[:, r:r + 1]).then_inc(c["n"], 1)
                if 1 in live:
                    s, r = t - 1, 1 - q
                    if isinstance(t, int) and t <= 2:
                        act.wait_ge(b["up"], 2 * T)
                    act.wait_ge(c["xT"], s + 1)
                    wait(act, c["qT"], s - 1)
                    act.activation(xT[:, r].rearrange("p k n -> p (k n)"), banks[0][:, 0:D], ACT.Copy)\
                       .then_inc(c["xTs"], 1)
                if 7 in live:
                    s = t - 7
                    act.wait_ge(d["xT"], s + 1)
                    wait(act, d["lg"], s)
                    act.activation(xT3.rearrange("p k n -> p (k n)"), banks[0][:, D:2 * D], ACT.Copy)\
                       .then_inc(d["xTs"], 1)
                if 2 in live:
                    s = t - 2
                    act.wait_ge(c["qT"], s + 1)
                    wait(act, c["q1"], s)
                    wait(act, c["den"], 2 * (s - 1))
                    wait(act, c["num"], s - 1)
                    for k in range(KC):
                        act.activation(qexp[:, k], banks[4][:, k * P:(k + 1) * P], ACT.Exp,
                                       bias=colb[:, KC + k:KC + k + 1])
                        last = act.activation(q1T[:, q, k], banks[4][:, k * P:(k + 1) * P], ACT.Relu,
                                              bias=colb[:, KC + k:KC + k + 1])
                    last.then_inc(c["qex"], 1)
                if 1 in live:
                    s, r = t - 1, 1 - q
                    if isinstance(t, int) and t <= 2:
                        act.wait_ge(b["sum1"], 2 * T)
                    act.wait_ge(c["kv"], s + 1)
                    wait(act, c["kvm"], s - 1)
                    act.activation(kexp[:, r], banks[1][:, 0:D], ACT.Exp)
                    act.activation(k1[:, r], banks[1][:, 0:D], ACT.Relu).then_inc(c["kex"], 1)
                if 2 in live:
                    s = t - 2
                    act.wait_ge(c["kvm"], s + 1)
                    wait(act, c["num"], s - 1)
                    wait(act, c["den"], 2 * (s - 1))
                    for k in range(KC):
                        last = act.activation(kvs[:, q, k], banks[2 + k][:, 0:D + 1], ACT.Copy)
                    last.then_inc(c["kvms"], 1)
                if 6 in live:
                    s = t - 6
                    held(act, d["shift"], 2 * s + 2)
                    held(act, d["xT"], s - 1)
                    act.activation(xn3[:, q], x_at(s), ACT.Identity, bias=shift3[:, q:q + 1],
                                   scale=rstd3[:, q:q + 1]).then_inc(d["xn"], 1)
            pipeline(act, T, 5, step_a, then=(5, step_b, LAG_B, (8, step_c, LAG_C, None)))

            act.wait_ge(d["lgs"], T)
            act.dma_start(b1s, b1).then_inc(d["ld_b"], 16)
            act.dma_start(b2s.rearrange("p e d -> p (e d)"), b2.partition_broadcast(P).rearrange("p a n -> p (a n)"))\
               .then_inc(d["ld_b"], 16)
            act.wait_ge(d["sh"], 1)
            act.activation(shifted, shifted, ACT.Exp).then_inc(d["ex"], 1)
            act.wait_ge(d["sei"], 1)
            act.wait_ge(d["ld_b"], 32)

            def step_f(t, q, live):
                if 1 in live:
                    s, r = t - 1, 1 - q
                    e = act.value_load(slot_expert[0:1, bass.ds(s, 1)], min_val=0, max_val=E - 1)
                    for g in range(2):
                        held(act, f["h"], 2 * s + g + 1)
                        if g == 0:
                            held(act, f["y"], s - 1)
                        for m in range(4 * g, 4 * g + 4):
                            last = act.activation(hTd[:, r, m * P:(m + 1) * P],
                                                  banks[2 + 2 * r + g][:, (m % 4) * P:(m % 4 + 1) * P],
                                                  ACT.Relu, bias=b1s[:, bass.ds(e, 1), m])
                        last.then_inc(f["hTa"], 1)
            pipeline(act, SLOTS, 3, step_f)

        @block.tensor
        def _(pe):
            pe.wait_ge(consts, 4)
            pe.wait_ge(ld_w0, 32)

            def transpose2(dst, src, done):
                for k in range(KC):
                    last = pe.transpose(dst[:, k * P:(k + 1) * P], src[:, k * P:(k + 1) * P], ident[:, :])
                last.then_inc(done, 1)

            def step_a(t, q, live):
                if isinstance(t, int) and t == 3:
                    pe.wait_ge(ld_keys, 48)
                    for k in range(KC):
                        for n in range(4):
                            last = pe.matmul(banks[6 + k][:, n * P:(n + 1) * P], wqs[:, n, k * P:(k + 1) * P],
                                             keyb[:, n], start=True, stop=True)
                    last.then_inc(simw_mm, 1)
                if 2 in live:
                    s = t - 2
                    wait(pe, a["vws"], s)
                    for k in range(KC):
                        last = pe.matmul(banks[2][:, 0:D], ctxb[:, q, k], w0s[:, k], start=(k == 0), stop=(k == KC - 1))
                    last.then_inc(a["vw"], 1)
                if 4 in live:
                    s = t - 4
                    pe.wait_ge(a["pts"], s + 1)
                    pe.wait_ge(a["vws"], s + 1)
                    if isinstance(t, int) and s < 2:
                        pe.wait_ge(simw_done, 2)
                    wait(pe, a["u"], s - 1)
                    pe.matmul(outA[q][:, 0:D], probT[:, q], vws[:, q], start=True, stop=True).then_inc(a["o"], 1)
                if 3 in live:
                    s, r = t - 3, 1 - q
                    pe.wait_ge(a["ex"], s + 1)
                    wait(pe, a["pts"], s)
                    pe.transpose(banks[5][:, 0:P], prob[:, r], ident[:, :]).then_inc(a["pt"], 1)
                if 2 in live:
                    s = t - 2
                    pe.wait_ge(a["xTs"], s + 1)
                    pe.wait_ge(a["tqs"], s + 1)
                    wait(pe, a["ex"], s - 1)
                    for k in range(KC):
                        last = pe.matmul(scoresA[q][:, 0:P], xT[:, q, k], tqs[:, q, k],
                                         start=(k == 0), stop=(k == KC - 1))
                    last.then_inc(a["sc"], 1)
                if 1 in live:
                    s, r = t - 1, 1 - q
                    pe.wait_ge(a["xn"], s + 1)
                    wait(pe, a["xTs"], s)
                    transpose2(banks[0], xn[:, r], a["xT"])
                if 1 in live:
                    s, r = t - 1, 1 - q
                    pe.wait_ge(ld_ca[r], loads(s, r))
                    wait(pe, a["tqs"], s)
                    for o in range(KC):
                        for k in range(KC):
                            last = pe.matmul(banks[1][:, o * P:(o + 1) * P], w0s[:, k, o * P:(o + 1) * P], ctxb[:, r, k],
                                             start=(k == 0), stop=(k == KC - 1))
                    last.then_inc(a["tq"], 1)

            def dense(s, r, g):
                pe.wait_ge(b["act2"], 2 * s + g + 1)
                for m in range(4 * g, 4 * g + 4):
                    pe.matmul(banks[6][:, 0:D], hT[:, r, m * P:(m + 1) * P], wdns[:, m], start=(m == 0), stop=False)

            def step_b(t, q, live):
                f, p, s, r = t - 1, t - 2, t - 3, 1 - q
                F, B1, B2 = (k in live for k in (1, 2, 3))
                if isinstance(t, int) and t == 1:
                    pe.wait_ge(ld_b, 64)
                    for bank in ("xTs", "tqs", "vws", "ex"):
                        pe.wait_ge(a[bank], T)
                if isinstance(t, int) and t == 2:
                    pe.wait_ge(a["pts"], T)
                if isinstance(t, int) and t == 3:
                    pe.wait_ge(a["u"], T)
                if F:
                    pe.wait_ge(b["xn"], f + 1)
                    wait(pe, b["sts"], 2 * (t - 4) + 1)
                    transpose2(banks[0], xn[:, r], b["xT"])
                if B1:
                    for g in range(2):
                        wait(pe, b["act2"], 2 * (p - 1) + g + 1)
                        for m in range(4):
                            for k in range(KC):
                                last = pe.matmul(banks[4 + g][:, m * P:(m + 1) * P],
                                                 wups[:, k, (4 * g + m) * P:(4 * g + m + 1) * P],
                                                 xT[:, q, k], start=(k == 0), stop=(k == KC - 1))
                        last.then_inc(b["up"], 1)
                if F:
                    pe.wait_ge(b["xTs"], f + 1)
                    wait(pe, b["simS"], f)
                    for k in range(KC):
                        last = pe.matmul(banks[1][:], xT[:, r, k], simw[:, k], start=(k == 0), stop=(k == KC - 1))
                    last.then_inc(b["sim"], 1)
                if B2:
                    wait(pe, b["x"], s)
                    dense(s, r, 0)
                if F:
                    wait(pe, b["pick"], 2 * HEADS * f)
                    for g in range(2):
                        for k in range(KC):
                            last = pe.matmul(banks[2 + g], xT[:, r, k], dembs[:, k, g * BANK:(g + 1) * BANK],
                                             start=(k == 0), stop=(k == KC - 1))
                    last.then_inc(b["dots"], 1)
                if B2:
                    pe.wait_ge(b["last"], s + 1)
                    for g in range(2):
                        if g == 1:
                            wait(pe, b["sts"], 2 * s)
                        for m in range(4):
                            last = pe.transpose((banks[7] if g else banks[0])[:, m * P:(m + 1) * P],
                                                picked[:, r, 0, (4 * g + m) * P:(4 * g + m + 1) * P], ident[:, :])
                        last.then_inc(b["st"], 1)
                    dense(s, r, 1)
                    for m in range(IC):
                        if m % 4 == 0:
                            pe.wait_ge(b["sts"], 2 * s + m // 4 + 1)
                        last = pe.matmul(banks[6][:, 0:D], pickT[:, m * P:(m + 1) * P], uembs[:, m],
                                         start=False, stop=(m == IC - 1))
                    last.then_inc(b["y"], 1)

            def step_c(t, q, live):
                if isinstance(t, int) and t == 1:
                    pe.wait_ge(ld_cw, 48)
                    pe.wait_ge(c["ones"], 1)
                    pe.wait_ge(b["sts"], 2 * T)
                    pe.wait_ge(b["simS"], T)
                    pe.wait_ge(b["pick"], 2 * HEADS * T)
                    pe.wait_ge(b["act2"], 2 * T)
                if isinstance(t, int) and t == 3:
                    pe.wait_ge(b["x"], T)
                wait(pe, c["xTs"], at_most(t - 1, T))
                if 7 in live:
                    s, r = t - 7, 1 - q
                    wait(pe, d["xTs"], s)
                    pe.wait_ge(d["xn"], s + 1)
                    transpose2(banks[0][:, D:2 * D], xn3[:, r], d["xT"])
                if 1 in live:
                    s, r = t - 1, 1 - q
                    wait(pe, d["xTs"], t - 7)
                    pe.wait_ge(c["xn"], s + 1)
                    transpose2(banks[0], xn[:, r], c["xT"])
                if 2 in live:
                    s = t - 2
                    pe.wait_ge(c["xTs"], s + 1)
                    wait(pe, c["qex"], s)
                    for o in range(KC):
                        for k in range(KC):
                            last = pe.matmul(banks[4][:, o * P:(o + 1) * P], wqcs[:, k, o * P:(o + 1) * P], xT[:, q, k],
                                             start=(k == 0), stop=(k == KC - 1))
                    last.then_inc(c["qT"], 1)
                if 4 in live:
                    s = t - 4
                    pe.wait_ge(c["ao"], s + 1)
                    wait(pe, c["r"], s)
                    wait(pe, d["lgs"], t - 7)
                    for k in range(KC):
                        last = pe.matmul(banks[7][:, 0:D], den[:, q, k], wocs[:, k], start=(k == 0), stop=(k == KC - 1))
                    last.then_inc(c["oo"], 1)
                if 1 in live:
                    s, r = t - 1, 1 - q
                    pe.wait_ge(ld_cc[r], loads(s, r))
                    wait(pe, c["kex"], s)
                    wait(pe, c["vb"], s)
                    pe.matmul(banks[1][:, 0:D], ones[0:1, :], r_bk[0:1], start=True, stop=False)
                    for k in range(KC):
                        pe.matmul(banks[1][:, 0:D], ctxb[:, r, k], wkvs[:, k, 0:D], start=False, stop=(k == KC - 1))
                    for k in range(KC):
                        last = pe.matmul(banks[5][:, 0:D], ctxb[:, r, k], wkvs[:, k, D:2 * D],
                                         start=(k == 0), stop=(k == KC - 1))
                    last.then_inc(c["kv"], 1)
                if 2 in live:
                    s = t - 2
                    pe.wait_ge(c["k1"], s + 1)
                    pe.wait_ge(c["vb"], s + 1)
                    wait(pe, c["kvms"], s)
                    for k in range(KC):
                        last = pe.matmul(banks[2 + k][:, 0:D + 1], k1[:, q, k * P:(k + 1) * P], v_c[:, q],
                                         start=True, stop=True)
                    last.then_inc(c["kvm"], 1)
                if 3 in live:
                    s, r = t - 3, 1 - q
                    pe.wait_ge(c["kvms"], s + 1)
                    pe.wait_ge(c["q1"], s + 1)
                    wait(pe, c["ao"], s)
                    for o in range(KC):
                        for k in range(KC):
                            last = pe.matmul(banks[6][:, o * P:(o + 1) * P], kvs[:, r, k, o * P:(o + 1) * P], q1T[:, r, k],
                                             start=(k == 0), stop=(k == KC - 1))
                    last.then_inc(c["num"], 1)
                if 7 in live:
                    s = t - 7
                    pe.wait_ge(d["xTs"], s + 1)
                    wait(pe, d["lgs"], s)
                    wait(pe, c["r"], at_most(t - 3, T))
                    for k in range(KC):
                        last = pe.matmul(banks[7][:, D:D + E], xT3[:, k], wgates[:, k], start=(k == 0), stop=(k == KC - 1))
                    last.then_inc(d["lg"], 1)
            pipeline(pe, T, 5, step_a, then=(5, step_b, LAG_B, (8, step_c, LAG_C, None)))

            pe.wait_ge(d["oh"], 1)
            pe.matmul(banks[5][:, 0:E], ones[:, :], onehot_sum, start=True, stop=True).then_inc(d["cnt"], 1)
            pe.wait_ge(d["below"], 1)
            pe.matmul(banks[4][:, 0:T * E], below, onehot.rearrange("p e t -> p (e t)"), start=True, stop=False)
            pe.matmul(banks[4][:, 0:T * E], ones[:, :], before.rearrange("p e t -> p (e t)"), start=False, stop=True)\
              .then_inc(d["rank"], 1)

            for t in range(T):
                pe.wait_ge(d["hot"], t + 1)
                last = pe.matmul(banks[6][:, 0:2 * SLOTS], pos_hot[:, t], seats[:, t].rearrange("p a s -> p (a s)"),
                                 start=(t == 0), stop=(t == T - 1))
            last.then_inc(d["seated"], 1)

            pe.wait_ge(d["sei"], 1)
            pe.wait_ge(d["tables"], 3)
            pe.wait_ge(d["ld_w"], 2 * 16 * T)
            pe.wait_ge(d["ld_b"], 32)

            def step_f(t, q, live):
                S0, S1, S2 = (k in live for k in range(3))
                if S2:
                    e = pe.value_load(slot_expert[0:1, bass.ds(t - 2, 1)], min_val=0, max_val=E - 1)
                if S1:
                    s, r = t - 1, 1 - q
                    pe.wait_ge(f["xTs"], s + 1)
                    pe.wait_ge(f["w1"], s + 1)
                    wait(pe, f["hTa"], 2 * (s - 1))
                    for g in range(2):
                        for m in range(4):
                            for k in range(KC):
                                last = pe.matmul(banks[2 + 2 * r + g][:, m * P:(m + 1) * P],
                                                 w1_slot[r][:, k, (4 * g + m) * P:(4 * g + m + 1) * P], xT[:, r, k],
                                                 start=(k == 0), stop=(k == KC - 1))
                        last.then_inc(f["h"], 1)
                if S0:
                    pe.wait_ge(f["xn"], t + 1)
                    wait(pe, f["xTs"], t)
                    transpose2(banks[0], xn[:, q], f["xT"])
                if S2:
                    s = t - 2
                    wait(pe, f["yb"], s)
                    for m in range(IC):
                        if m % 4 == 0:
                            pe.wait_ge(f["hTa"], 2 * s + m // 4 + 1)
                        last = pe.matmul(banks[6][:, 0:D], hTd[:, q, m * P:(m + 1) * P],
                                         w2s[:, bass.ds(e, 1), m].rearrange("p a n -> p (a n)"),
                                         start=(m == 0), stop=(m == IC - 1))
                    last.then_inc(f["y"], 1)
            pipeline(pe, SLOTS, 3, step_f)



def kernel(**inputs):
    import numpy as np
    import concourse.bacc as bacc
    from concourse.bass_utils import run_bass_kernel_spmd as run

    v = {k: np.asarray(a) for k, a in inputs.items()}

    def chunks(w):
        return w.reshape(-1, P, w.shape[-1]).transpose(1, 0, 2)

    x, context = v["x"], v["ctx_1024"]
    T, _, D = x.shape
    w1, w2 = v["L1_ffn_W1"], v["L1_ffn_W2"]
    E = w1.shape[0]
    keys = v["L0_ffn_keys"]
    arrays = {
        "x": x,
        "ctxT": context.transpose(0, 2, 1).reshape(T, -1, P, P).transpose(0, 2, 1, 3),
        "rows": np.concatenate([v[n].reshape(-1) for n in (
            "L0_xattn_b", "L1_xattn_bk", "L1_xattn_bv", "L1_xattn_bo", "L1_xattn_gamma",
            "L1_xattn_beta", "L1_ffn_b_gate", "g_xattn", "g_ffn")])[None],
        "cols": np.concatenate([v["L0_xattn_b"], v["L1_xattn_bq"]]).reshape(-1, P).T,
        "w0": chunks(v["L0_xattn_W"].T),
        "wup": chunks(v["L0_ffn_W_up"].T),
        "wdn": chunks(v["L0_ffn_W_down"].T),
        "wq": chunks(v["L0_ffn_W_q"]),
        "keys": chunks(keys.transpose(2, 0, 3, 1).reshape(-1, keys.shape[1])),
        "demb": chunks(v["L0_ffn_down_embed"].T),
        "uemb": chunks(v["L0_ffn_up_embed"]),
        "wkv": chunks(np.concatenate([v["L1_xattn_Wk"].T, v["L1_xattn_Wv"].T], axis=1)),
        "wqc": chunks(v["L1_xattn_Wq"].T),
        "woc": chunks(v["L1_xattn_Wo"].T),
        "wgate": chunks(v["L1_ffn_w_gate"]),
        "w1": w1.reshape(E, -1, P, w1.shape[2]).transpose(2, 0, 1, 3),
        "w2": w2.reshape(E, -1, P, D).transpose(2, 0, 1, 3),
        "b1": v["L1_ffn_b1"].reshape(E, -1, P).transpose(2, 0, 1),
        "b2": v["L1_ffn_b2"].reshape(1, -1),
    }
    arrays = {f"in_{n}": np.ascontiguousarray(a) for n, a in arrays.items()}
    nc = bacc.Bacc("TRN2", target_bir_lowering=False, num_devices=1)
    args = [nc.dram_tensor(n, a.shape, mybir.dt.from_np(a.dtype), kind="ExternalInput").ap()
            for n, a in arrays.items()]
    out = nc.dram_tensor("out", x.shape, F32, kind="ExternalOutput").ap()
    build(nc, *args, out)
    r = run(nc, [arrays], core_ids=[0])
    return r.results[0]["out"]
```
